# Optimizing a Trainium2 kernel written in Bass

```python
import numpy as np
import jax
import jax.numpy as jnp

def _softmax(x, axis=-1):
    return jax.nn.softmax(x, axis=axis)

def _gelu(x):
    return jax.nn.gelu(x, approximate=True)

def _silu(x):
    return jax.nn.silu(x)

def _sigmoid(x):
    return jax.nn.sigmoid(x)

def _layernorm(x, axis=-1, eps=1e-05):
    m = jnp.mean(x, axis=axis, keepdims=True)
    v = jnp.var(x, axis=axis, keepdims=True)
    return (x - m) / jnp.sqrt(v + eps)

def _scatter_add(tgt, idx, src, axis=0):
    return tgt.at[idx].add(src)

def _segment_sum(src, seg, n):
    return jax.ops.segment_sum(src, seg, n)
kernel_name = 'mk_perceiver_d1_seqx_r4_7af2ab'

def setup_inputs(seed: int=0):
    np.random.seed(seed)
    _w = jnp.asarray

    def _rec_inputs():
        import jax
        import jax.numpy as jnp
        _rk = jax.random.key(seed)
        x = -0.0003929 + 0.9999 * jax.random.normal(jax.random.fold_in(_rk, 1), (2, 256, 512), jnp.float32)
        _lenS = 256 - jax.random.randint(jax.random.fold_in(_rk, 7), (2,), 0, max(1, 256 // 4) + 1, jnp.int32)
        _lenS2 = 4096 - jax.random.randint(jax.random.fold_in(_rk, 8), (2,), 0, max(1, 4096 // 4) + 1, jnp.int32)
        _ctx_1024P = jax.random.normal(jax.random.fold_in(_rk, 11), (2, 16, 256), jnp.float32)
        _ctx_1024c = jax.random.dirichlet(jax.random.fold_in(_rk, 511), 0.3 * jnp.ones((16,), jnp.float32), (2, 4096))
        _ctx_1024t = jnp.einsum('bsk,bkd->bsd', _ctx_1024c, _ctx_1024P)
        _ctx_1024t = _ctx_1024t * jax.lax.rsqrt(jnp.mean(jnp.square(_ctx_1024t)) + 1e-12) * 0.953939
        ctx_1024 = -0.000494167 + 1.00018 * (_ctx_1024t + 0.3 * jax.random.normal(jax.random.fold_in(_rk, 611), (2, 4096, 256), jnp.float32))
        _validS = jnp.arange(256)[None, :] < _lenS[:, None]
        _validS2 = jnp.arange(4096)[None, :] < _lenS2[:, None]
        _causal = jnp.tril(jnp.ones((256, 256), dtype=bool))
        mask_BxS2_bf1 = jnp.ones((2, 4096), dtype=bool)
        return (x, ctx_1024, mask_BxS2_bf1)
    x, ctx_1024, mask_BxS2_bf1 = _rec_inputs()

    def _L0_xattn_setup():
        import jax, jax.numpy as jnp
        import numpy as np
        N_HEADS = 16
        N_KV_HEADS = 8
        HEAD_DIM = 128
        D_TEXT = 512
        D_VISION = 256
        GROUPS = N_HEADS // N_KV_HEADS
        key = jax.random.key(seed)
        ks = jax.random.split(key, 6)
        B, T_text, T_vis = (4, 512, 144)
        text_hidden = jax.random.normal(ks[0], (B, T_text, D_TEXT), dtype=jnp.float32)
        vision_tokens = jax.random.normal(ks[1], (B, T_vis, D_VISION), dtype=jnp.float32)
        vision_mask = jnp.ones((B, T_vis), dtype=bool)
        s = 0.02
        Wq = jax.random.normal(ks[2], (D_TEXT, N_HEADS * HEAD_DIM), dtype=jnp.float32) * s
        Wk = jax.random.normal(ks[3], (D_VISION, N_KV_HEADS * HEAD_DIM), dtype=jnp.float32) * s
        Wv = jax.random.normal(ks[4], (D_VISION, N_KV_HEADS * HEAD_DIM), dtype=jnp.float32) * s
        Wo = jax.random.normal(ks[5], (N_HEADS * HEAD_DIM, D_TEXT), dtype=jnp.float32) * s
        return {'text_hidden': text_hidden, 'vision_tokens': vision_tokens, 'vision_mask': vision_mask, 'Wq': Wq, 'Wk': Wk, 'Wv': Wv, 'Wo': Wo}
    _L0_xattn_all = _L0_xattn_setup()
    _L0_xattn_in = {k: v for k, v in _L0_xattn_all.items() if k in ('Wq', 'Wk', 'Wv', 'Wo')}
    del _L0_xattn_all

    def _L0_attn_setup():
        import jax, jax.numpy as jnp
        import numpy as np
        D_MODEL = 512
        NUM_HEADS = 16
        HEAD_DIM = D_MODEL // NUM_HEADS
        SCALE = HEAD_DIM ** (-0.5)
        ALPHA = 1.0
        key = jax.random.key(seed)
        ks = jax.random.split(key, 9)
        B, T = (2, 512)
        s = 0.02
        w = lambda k: jax.random.normal(k, (D_MODEL, D_MODEL), jnp.float32) * s
        b = lambda k: jax.random.normal(k, (D_MODEL,), jnp.float32) * s
        return {'x': jax.random.normal(ks[0], (B, T, D_MODEL), jnp.float32), 'q_w': w(ks[1]), 'q_b': b(ks[2]), 'k_w': w(ks[3]), 'k_b': b(ks[4]), 'v_w': w(ks[5]), 'v_b': b(ks[6]), 'o_w': w(ks[7]), 'o_b': b(ks[8])}
    _L0_attn_all = _L0_attn_setup()
    _L0_attn_in = {k: v for k, v in _L0_attn_all.items() if k in ('q_w', 'q_b', 'k_w', 'k_b', 'v_w', 'v_b', 'o_w', 'o_b')}
    del _L0_attn_all

    def _L0_ffn_setup():
        import jax, jax.numpy as jnp
        import numpy as np
        from jax import lax
        DIM = 512
        E = 8
        K = 2
        RANK = 32
        CAP_FACTOR = 1.25

        def gelu(x):
            return jax.nn.gelu(x, approximate=False)

        def _moe_forward(x, gate_w, w1, b1, w2, b2, wd, wu, sw1, sb1, sw2, sb2, swd, swu):
            B, S, D = x.shape
            T = B * S
            cap = max(1, int(T * CAP_FACTOR / E))
            xt = x.reshape(T, D)
            logits = xt @ gate_w
            probs_full = jax.nn.softmax(logits, axis=-1)
            top_p, top_i = lax.top_k(probs_full, K)
            out = jnp.zeros_like(xt)
            for k in range(K):
                e = top_i[:, k]
                w = top_p[:, k]
                onehot = jax.nn.one_hot(e, E, dtype=jnp.int32)
                pos_all = jnp.cumsum(onehot, axis=0) - 1
                pos = jnp.take_along_axis(pos_all, e[:, None], axis=1)[:, 0]
                keep = pos < cap
                pos_c = jnp.where(keep, pos, cap)
                buf = jnp.zeros((E, cap, D), x.dtype).at[e, pos_c].set(xt * keep[:, None].astype(x.dtype), mode='drop')
                h = gelu(jnp.einsum('ecd,edf->ecf', buf, w1) + b1[:, None, :])
                y = jnp.einsum('ecf,efd->ecd', h, w2) + b2[:, None, :]
                a = jnp.einsum('ecr,erd->ecd', gelu(jnp.einsum('ecd,edr->ecr', buf, wd)), wu)
                y = y + a
                tok = y[e, jnp.minimum(pos_c, cap - 1)]
                out = out + tok * keep[:, None].astype(x.dtype) * w[:, None]
            sh = gelu(xt @ sw1 + sb1) @ sw2 + sb2
            sh = sh + gelu(xt @ swd) @ swu
            out = out + 0.2 * sh
            return out.reshape(B, S, D)
        key = jax.random.key(seed)
        ks = jax.random.split(key, 16)
        s = 0.02
        d, h = (DIM, 4 * DIM)
        inp = {'x': jax.random.normal(ks[0], (4, 512, d), dtype=jnp.float32), 'gate_w': jax.random.normal(ks[1], (d, E), dtype=jnp.float32) * s, 'w1': jax.random.normal(ks[2], (E, d, h), dtype=jnp.float32) * s, 'b1': jnp.zeros((E, h), dtype=jnp.float32), 'w2': jax.random.normal(ks[3], (E, h, d), dtype=jnp.float32) * s, 'b2': jnp.zeros((E, d), dtype=jnp.float32), 'wd': jax.random.normal(ks[4], (E, d, RANK), dtype=jnp.float32) * s, 'wu': jax.random.normal(ks[5], (E, RANK, d), dtype=jnp.float32) * s, 'sw1': jax.random.normal(ks[6], (d, h), dtype=jnp.float32) * s, 'sb1': jnp.zeros((h,), dtype=jnp.float32), 'sw2': jax.random.normal(ks[7], (h, d), dtype=jnp.float32) * s, 'sb2': jnp.zeros((d,), dtype=jnp.float32), 'swd': jax.random.normal(ks[8], (d, RANK), dtype=jnp.float32) * s, 'swu': jax.random.normal(ks[9], (RANK, d), dtype=jnp.float32) * s}
        return inp
    _L0_ffn_all = _L0_ffn_setup()
    _L0_ffn_in = {k: v for k, v in _L0_ffn_all.items() if k in ('gate_w', 'w1', 'b1', 'w2', 'b2', 'wd', 'wu', 'sw1', 'sb1', 'sw2', 'sb2', 'swd', 'swu')}
    del _L0_ffn_all
    return {'x': x, 'ctx_1024': ctx_1024, 'mask_BxS2_bf1': mask_BxS2_bf1, 'L0_xattn_Wq': _L0_xattn_in['Wq'], 'L0_xattn_Wk': _L0_xattn_in['Wk'], 'L0_xattn_Wv': _L0_xattn_in['Wv'], 'L0_xattn_Wo': _L0_xattn_in['Wo'], 'L0_attn_q_w': _L0_attn_in['q_w'], 'L0_attn_q_b': _L0_attn_in['q_b'], 'L0_attn_k_w': _L0_attn_in['k_w'], 'L0_attn_k_b': _L0_attn_in['k_b'], 'L0_attn_v_w': _L0_attn_in['v_w'], 'L0_attn_v_b': _L0_attn_in['v_b'], 'L0_attn_o_w': _L0_attn_in['o_w'], 'L0_attn_o_b': _L0_attn_in['o_b'], 'L0_ffn_gate_w': _L0_ffn_in['gate_w'], 'L0_ffn_w1': _L0_ffn_in['w1'], 'L0_ffn_b1': _L0_ffn_in['b1'], 'L0_ffn_w2': _L0_ffn_in['w2'], 'L0_ffn_b2': _L0_ffn_in['b2'], 'L0_ffn_wd': _L0_ffn_in['wd'], 'L0_ffn_wu': _L0_ffn_in['wu'], 'L0_ffn_sw1': _L0_ffn_in['sw1'], 'L0_ffn_sb1': _L0_ffn_in['sb1'], 'L0_ffn_sw2': _L0_ffn_in['sw2'], 'L0_ffn_sb2': _L0_ffn_in['sb2'], 'L0_ffn_swd': _L0_ffn_in['swd'], 'L0_ffn_swu': _L0_ffn_in['swu']}

def reference(x, ctx_1024, mask_BxS2_bf1, L0_xattn_Wq, L0_xattn_Wk, L0_xattn_Wv, L0_xattn_Wo, L0_attn_q_w, L0_attn_q_b, L0_attn_k_w, L0_attn_k_b, L0_attn_v_w, L0_attn_v_b, L0_attn_o_w, L0_attn_o_b, L0_ffn_gate_w, L0_ffn_w1, L0_ffn_b1, L0_ffn_w2, L0_ffn_b2, L0_ffn_wd, L0_ffn_wu, L0_ffn_sw1, L0_ffn_sb1, L0_ffn_sw2, L0_ffn_sb2, L0_ffn_swd, L0_ffn_swu):
    import jax
    import jax.numpy as jnp

    def _L0_xattn_ref(text_hidden, vision_tokens, vision_mask, Wq, Wk, Wv, Wo):
        import jax, jax.numpy as jnp
        import numpy as np
        N_HEADS = 16
        N_KV_HEADS = 8
        HEAD_DIM = 128
        D_TEXT = 512
        D_VISION = 256
        GROUPS = N_HEADS // N_KV_HEADS
        B, T_text, _ = text_hidden.shape
        T_vis = vision_tokens.shape[1]
        scale = jnp.float32(np.sqrt(HEAD_DIM))
        q = (text_hidden @ Wq).reshape(B, T_text, N_HEADS, HEAD_DIM).transpose(0, 2, 1, 3)
        k = (vision_tokens @ Wk).reshape(B, T_vis, N_KV_HEADS, HEAD_DIM).transpose(0, 2, 1, 3)
        v = (vision_tokens @ Wv).reshape(B, T_vis, N_KV_HEADS, HEAD_DIM).transpose(0, 2, 1, 3)
        k = jnp.repeat(k, GROUPS, axis=1)
        v = jnp.repeat(v, GROUPS, axis=1)
        scores = jnp.einsum('bhtd,bhsd->bhts', q, k) / scale
        mask = vision_mask[:, None, None, :]
        scores = jnp.where(mask, scores, -jnp.inf)
        attn = jax.nn.softmax(scores, axis=-1)
        attn = jnp.nan_to_num(attn, nan=0.0)
        out = jnp.einsum('bhts,bhsd->bhtd', attn, v)
        out = out.transpose(0, 2, 1, 3).reshape(B, T_text, N_HEADS * HEAD_DIM)
        return out @ Wo

    def _L0_attn_ref(x, q_w, q_b, k_w, k_b, v_w, v_b, o_w, o_b):
        import jax, jax.numpy as jnp
        import numpy as np
        D_MODEL = 512
        NUM_HEADS = 16
        HEAD_DIM = D_MODEL // NUM_HEADS
        SCALE = HEAD_DIM ** (-0.5)
        ALPHA = 1.0
        B, T, D = x.shape
        H, HD = (NUM_HEADS, HEAD_DIM)

        def proj_split(w, bias):
            y = x @ w.T + bias
            return y.reshape(B, T, H, HD).transpose(0, 2, 1, 3).reshape(B * H, T, HD)
        Q = proj_split(q_w, q_b)
        K = proj_split(k_w, k_b)
        V = proj_split(v_w, v_b)
        S = jnp.einsum('hid,hjd->hij', K, Q) * SCALE
        idx = jnp.arange(T)
        delta = idx[:, None] - idx[None, :]
        decay = jnp.where(delta < 0, 0.0, -delta.astype(jnp.float32) ** ALPHA)
        S = jnp.where(delta < 0, -jnp.inf, S) + decay
        C = jax.nn.softmax(S, axis=-1)
        attn = jnp.einsum('hij,hjd->hid', C, V)
        attn = attn.reshape(B, H, T, HD).transpose(0, 2, 1, 3).reshape(B, T, D)
        return attn @ o_w.T + o_b

    def _L0_ffn_ref(x, gate_w, w1, b1, w2, b2, wd, wu, sw1, sb1, sw2, sb2, swd, swu):
        import jax, jax.numpy as jnp
        import numpy as np
        from jax import lax
        DIM = 512
        E = 8
        K = 2
        RANK = 32
        CAP_FACTOR = 1.25

        def gelu(x):
            return jax.nn.gelu(x, approximate=False)

        def _moe_forward(x, gate_w, w1, b1, w2, b2, wd, wu, sw1, sb1, sw2, sb2, swd, swu):
            B, S, D = x.shape
            T = B * S
            cap = max(1, int(T * CAP_FACTOR / E))
            xt = x.reshape(T, D)
            logits = xt @ gate_w
            probs_full = jax.nn.softmax(logits, axis=-1)
            top_p, top_i = lax.top_k(probs_full, K)
            out = jnp.zeros_like(xt)
            for k in range(K):
                e = top_i[:, k]
                w = top_p[:, k]
                onehot = jax.nn.one_hot(e, E, dtype=jnp.int32)
                pos_all = jnp.cumsum(onehot, axis=0) - 1
                pos = jnp.take_along_axis(pos_all, e[:, None], axis=1)[:, 0]
                keep = pos < cap
                pos_c = jnp.where(keep, pos, cap)
                buf = jnp.zeros((E, cap, D), x.dtype).at[e, pos_c].set(xt * keep[:, None].astype(x.dtype), mode='drop')
                h = gelu(jnp.einsum('ecd,edf->ecf', buf, w1) + b1[:, None, :])
                y = jnp.einsum('ecf,efd->ecd', h, w2) + b2[:, None, :]
                a = jnp.einsum('ecr,erd->ecd', gelu(jnp.einsum('ecd,edr->ecr', buf, wd)), wu)
                y = y + a
                tok = y[e, jnp.minimum(pos_c, cap - 1)]
                out = out + tok * keep[:, None].astype(x.dtype) * w[:, None]
            sh = gelu(xt @ sw1 + sb1) @ sw2 + sb2
            sh = sh + gelu(xt @ swd) @ swu
            out = out + 0.2 * sh
            return out.reshape(B, S, D)
        return _moe_forward(x, gate_w, w1, b1, w2, b2, wd, wu, sw1, sb1, sw2, sb2, swd, swu)
    x = x + _L0_xattn_ref(_layernorm(x, axis=-1), ctx_1024, mask_BxS2_bf1, L0_xattn_Wq, L0_xattn_Wk, L0_xattn_Wv, L0_xattn_Wo)
    x = x + _L0_attn_ref(_layernorm(x, axis=-1), L0_attn_q_w, L0_attn_q_b, L0_attn_k_w, L0_attn_k_b, L0_attn_v_w, L0_attn_v_b, L0_attn_o_w, L0_attn_o_b)
    x = x + _L0_ffn_ref(_layernorm(x, axis=-1), L0_ffn_gate_w, L0_ffn_w1, L0_ffn_b1, L0_ffn_w2, L0_ffn_b2, L0_ffn_wd, L0_ffn_wu, L0_ffn_sw1, L0_ffn_sb1, L0_ffn_sw2, L0_ffn_sb2, L0_ffn_swd, L0_ffn_swu)
    return x

_drawn_inputs = setup_inputs


def setup_inputs(seed=0):
    import zlib

    import numpy as np

    out = dict(_drawn_inputs(seed))
    spreads = {'L0_ffn_b1': (0.0, 0.537),
     'L0_ffn_b2': (0.0, 0.281),
     'L0_ffn_sb1': (0.0, 0.779),
     'L0_ffn_sb2': (0.0, 0.401)}
    factors = {'L0_xattn_Wq': 6.35,
     'L0_xattn_Wk': 5.678,
     'L0_attn_q_w': 2.776,
     'L0_attn_q_b': 8.0,
     'L0_attn_k_b': 8.0,
     'L0_attn_v_b': 4.841,
     'L0_attn_o_b': 2.757,
     'L0_ffn_wd': 7.262,
     'L0_ffn_wu': 6.922,
     'L0_ffn_swd': 8.0,
     'L0_ffn_swu': 8.0}
    for name, (base, spread) in spreads.items():
        noise = np.random.default_rng([zlib.crc32(name.encode()), seed]).standard_normal(out[name].shape)
        drawn = base * np.exp(spread * noise) if base else spread * noise
        out[name] = jnp.asarray(drawn.astype(out[name].dtype))
    for name, factor in factors.items():
        out[name] = (out[name] * factor).astype(out[name].dtype)
    return out
```

```python
import concourse.bass as bass
from concourse import mybir
from contextlib import ExitStack

F32 = mybir.dt.float32
F32R = mybir.dt.float32r
BF16 = mybir.dt.bfloat16
U8 = mybir.dt.uint8
U32 = mybir.dt.uint32
ACT = mybir.ActivationFunctionType
ALU = mybir.AluOpType
AX = mybir.AxisListType

P = 128
BANK = 512
B, TQ, D = 2, 256, 512
TT = B * TQ // P
RT = TQ // P
KC = D // P
S, DC = 4096, 256
CC = DC // P
SCH = S // P
SB = S // BANK
H, HKV, HD = 16, 8, 128
GRP = H // HKV
EPS = 1e-5
NEG = -3.0e38


class Tensors:

    def __init__(self, nc, ctx, tag):
        self.nc, self.ctx, self.tag = nc, ctx, tag

    def sb(self, name, shape, dt=F32):
        return self.ctx.enter_context(self.nc.sbuf_tensor(f"{self.tag}_{name}", shape, dt))

    def ps(self, name, shape=(P, BANK), dt=F32):
        return self.ctx.enter_context(self.nc.psum_tensor(f"{self.tag}_{name}", list(shape), dt))

    def sem(self, name):
        return self.ctx.enter_context(self.nc.semaphore(f"{self.tag}_{name}"))


class Chain:

    def __init__(self, eng, sem):
        self.eng, self.sem, self.n = eng, sem, 0

    def link(self, ins):
        self.n += 1
        ins.then_inc(self.sem, 1)
        self.eng.wait_ge(self.sem, self.n)


def ln_scratch(t):
    return dict(stats=t.sb("ln_stats", [P, TT, 6]), mv=t.sb("ln_mv", [P, TT, 2]), root=t.sb("ln_root", [P, TT]),
                div=t.sb("ln_div", [P, TT]), rstd=t.sb("ln_rstd", [P, TT]), veps=t.sb("ln_veps", [P, TT]))


def ln_vector(v, ch, X, out, w, root_ready, var_ready):
    for i in range(TT):
        v.bn_stats(w["stats"][:, i, :], X[:, i, :]).then_inc(ch.sem, 1)
    ch.n += TT
    v.wait_ge(ch.sem, ch.n)
    for i in range(TT):
        v.bn_aggr(w["mv"][:, i, :], w["stats"][:, i, :]).then_inc(ch.sem, 1)
    ch.n += TT
    v.wait_ge(ch.sem, ch.n)
    v.tensor_scalar(w["veps"][:, :], w["mv"][:, :, 1], EPS, None, ALU.add).then_inc(var_ready, 1)
    v.wait_ge(root_ready, 1)
    ch.link(v.reciprocal(w["div"][:, :], w["root"][:, :]))
    ch.link(v.tensor_tensor(w["div"][:, :], w["div"][:, :], w["veps"][:, :], ALU.mult))
    ch.link(v.tensor_tensor(w["div"][:, :], w["div"][:, :], w["root"][:, :], ALU.add))
    ch.link(v.tensor_scalar(w["div"][:, :], w["div"][:, :], 0.5, None, ALU.mult))
    ch.link(v.reciprocal(w["rstd"][:, :], w["div"][:, :]))
    for i in range(TT):
        v.tensor_scalar(out[:, i, :], X[:, i, :], w["mv"][:, i, 0:1], w["rstd"][:, i:i + 1],
                        ALU.subtract, ALU.mult).then_inc(ch.sem, 1)
    ch.n += TT
    v.wait_ge(ch.sem, ch.n)


def queries(nc, x, wq, q_dram, X, ident):
    SLOTS = 8
    QB = 4
    with ExitStack() as ctx:
        t = Tensors(nc, ctx, "qry")
        ln = ln_scratch(t)
        xn = t.sb("xn", [P, TT, D])
        xnT = t.sb("xnT", [P, KC, B * TQ])
        wq_sb = t.sb("wq", [P, SLOTS, KC, HD])
        q_sb = t.sb("q", [P, QB, B * TQ])
        ps = [t.ps(f"ps{i}") for i in range(QB)]
        x_ld, ident_ok, var_ready, root_ready, xn_ready = (t.sem(n) for n in ("x_ld", "ident_ok", "var_ready", "root_ready", "xn_ready"))
        xT_ps, xT_ok, q_ps, q_done, chain = (t.sem(n) for n in ("xT_ps", "xT_ok", "q_ps", "q_done", "chain"))
        wq_ld = [t.sem(f"wq_ld{i}") for i in range(SLOTS)]
        q_out = [t.sem(f"q_out{i}") for i in range(QB)]
        block = ctx.enter_context(nc.Block())

        @block.sync
        def _(sp):
            sp.dma_start(X[:, :, :], x.rearrange("b (r p) d -> p (b r) d", p=P)).then_inc(x_ld, 16)
            with sp.Fori(0, H // SLOTS) as r:
                for i in range(SLOTS):
                    sp.wait_ge(q_ps, r * SLOTS + (i + 1))
                    sp.dma_start(wq_sb[:, i, :, :], wq[:, bass.ds((r * SLOTS + i) * HD, HD)].rearrange("(c p) n -> p c n", p=P)).then_inc(wq_ld[i], 16)

        @block.gpsimd
        def _(pool):
            nc.gpsimd.memset(ident[:, :], 0.0).then_inc(ident_ok, 1)
            pool.wait_ge(ident_ok, 1)
            nc.gpsimd.affine_select(out=ident[:, :], in_=ident[:, :], compare_op=ALU.not_equal, fill=1.0,
                                    base=0, pattern=[[-1, P]], channel_multiplier=1).then_inc(ident_ok, 1)

        @block.vector
        def _(v):
            ch = Chain(v, chain)
            v.wait_ge(x_ld, 16)
            ln_vector(v, ch, X, xn, ln, root_ready, var_ready)
            v.engine_nop().then_inc(xn_ready, 1)
            for c in range(KC):
                v.wait_ge(xT_ps, c + 1)
                v.tensor_copy(xnT[:, c, :], ps[c][:, :]).then_inc(xT_ok, 1)

        @block.scalar
        def _(act):
            act.wait_ge(var_ready, 1)
            act.activation(ln["root"][:, :], ln["veps"][:, :], ACT.Sqrt).then_inc(root_ready, 1)
            for i in range(QB):
                act.sem_inc(q_out[i], 16)
            act.sem_inc(q_done, QB)
            with act.Fori(0, H // SLOTS) as r:
                for i in range(SLOTS):
                    act.wait_ge(q_ps, r * SLOTS + (SLOTS + i + 1))
                    act.wait_ge(q_out[i % QB], r * (SLOTS // QB * 16) + (i // QB + 1) * 16)
                    act.activation(q_sb[:, i % QB, :], ps[i % QB][:, :], ACT.Copy, scale=HD ** -0.5).then_inc(q_done, 1)
                    act.wait_ge(q_done, r * SLOTS + (QB + i + 1))
                    act.dma_start(q_dram[bass.ds(r * SLOTS + i, 1), :, :].rearrange("o p n -> p (o n)"), q_sb[:, i % QB, :]).then_inc(q_out[i % QB], 16)
            for i in range(QB):
                act.wait_ge(q_out[i], (H // QB + 1) * 16)

        @block.tensor
        def _(pe):
            pe.sem_inc(q_ps, SLOTS)
            pe.wait_ge(ident_ok, 2)
            pe.wait_ge(xn_ready, 1)
            for c in range(KC):
                for i in range(TT):
                    m = pe.transpose(ps[c][:, i * P:(i + 1) * P], xn[:, i, c * P:(c + 1) * P], ident[:, :])
                m.then_inc(xT_ps, 1)
            pe.wait_ge(xT_ok, KC)
            with pe.Fori(0, H // SLOTS) as r:
                for i in range(SLOTS):
                    pe.wait_ge(wq_ld[i], r * 16 + 16)
                    pe.wait_ge(q_done, r * SLOTS + (i + 1))
                    for c in range(KC):
                        m = pe.matmul(ps[i % QB][:, :], wq_sb[:, i, c, :], xnT[:, c, :], start=c == 0, stop=c == KC - 1)
                    m.then_inc(q_ps, 1)


def cross(nc, ctx_in, mask, wk, wv, wo, q_dram, X, ident):
    RING = 4
    HEAD_ITEMS = CC * SB
    GROUP_ITEMS = SB + RT * SB + SB + RT * SB
    BATCH_ITEMS = HEAD_ITEMS + HKV * GROUP_ITEMS
    STEPS = SCH // 2
    PIECES = 4
    PIECE = S // PIECES
    LAG = 2
    PT = LAG + 1
    with ExitStack() as ctx:
        t = Tensors(nc, ctx, "crs")
        prob = [t.sb(f"prob{h}", [P, RT, S]) for h in range(GRP)]
        ctxT = t.sb("ctxT", [P, CC, S])
        kh, kl = t.sb("kh", [P, S], F32R), t.sb("kl", [P, S], F32R)
        vh, vl = t.sb("vh", [P, SCH, HD], F32R), t.sb("vl", [P, SCH, HD], F32R)
        maskb = t.sb("maskb", [P, S], BF16)
        qf = t.sb("qf", [P, GRP, TQ])
        qh, ql = t.sb("qh", [P, GRP, TQ], F32R), t.sb("ql", [P, GRP, TQ], F32R)
        wk_sb, wv_sb = t.sb("wk", [P, CC, HD]), t.sb("wv", [P, CC, HD])
        wo_sb = t.sb("wo", [P, GRP, D])
        pth, ptl = t.sb("pth", [P, PT, BANK], F32R), t.sb("ptl", [P, PT, BANK], F32R)
        oT = t.sb("oT", [P, GRP, TQ])
        mx = t.sb("mx", [P, GRP, RT, SB])
        nmax = t.sb("nmax", [P, GRP, RT])
        rs = t.sb("rs", [P, GRP, RT, PIECES])
        rinv = t.sb("rinv", [P, RT])
        anyv = t.sb("anyv", [P, 1])
        cin = prob[0][:, :, :].rearrange("p r s -> p (r s)").rearrange("p (n c) -> p n c", c=DC)
        mask_u8 = prob[1][:, 0, 0:S // 4].bitcast(U8)

        ring = [t.ps(f"ring{i}") for i in range(RING)]
        tp = [t.ps(f"tp{i}") for i in range(2)]
        ov, op = t.ps("ov"), t.ps("op")

        names = ("ctx_ld", "mask_ld", "q_ld", "wk_ld", "wv_ld", "wo0_ld", "wo1_ld", "ring_full", "ring_free", "kv_hi", "q_hi", "q_lo",
                 "max_ready", "p_ready", "pt_full", "pt_hi", "pt_lo", "pv_done", "ot_ready", "op_full", "op_free", "mask_ok", "neg_ok", "inv_chain", "scores_seen")
        s = {n: t.sem(n) for n in names}
        wo_ld = (s["wo0_ld"], s["wo1_ld"])
        block = ctx.enter_context(nc.Block())

        def items(b, j):
            return b * BATCH_ITEMS + j * GROUP_ITEMS + HEAD_ITEMS

        def group(b, j):
            return b * HKV + j

        QK = (SB, SB + RT * SB + SB)
        VI = SB + RT * SB

        @block.sync
        def _(sp):
            with sp.Fori(0, B) as b:
                sp.wait_ge(s["op_free"], b * (HKV * GRP * RT) + 1)
                for n in range(4):
                    k = SCH // 4
                    sp.dma_start(cin[:, n * k:(n + 1) * k, :],
                                 ctx_in[bass.ds(b, 1), n * k * P:(n + 1) * k * P, :].rearrange("o (n p) c -> p (o n) c", p=P)).then_inc(s["ctx_ld"], 16)
                sp.dma_start(mask_u8, mask[bass.ds(b, 1), :].to_broadcast([P, S])).then_inc(s["mask_ld"], 16)

                def group_loads(j, first):
                    g = group(b, j)
                    if not first:
                        sp.wait_ge(s["ring_full"], items(b, j) + (SB - GROUP_ITEMS))
                    sp.dma_start(wk_sb[:, :, :], wk[:, bass.ds(j * HD, HD)].rearrange("(c p) n -> p c n", p=P)).then_inc(s["wk_ld"], 16)
                    if not first:
                        sp.wait_ge(s["q_lo"], g)
                    sp.dma_start(qf[:, :, :], q_dram[bass.ds(j * GRP, GRP), :, bass.ds(b * TQ, TQ)].rearrange("h p n -> p h n")).then_inc(s["q_ld"], 16)
                    if not first:
                        sp.wait_ge(s["ring_full"], items(b, j) + (QK[1] - GROUP_ITEMS))
                    sp.dma_start(wv_sb[:, :, :], wv[:, bass.ds(j * HD, HD)].rearrange("(c p) n -> p c n", p=P)).then_inc(s["wv_ld"], 16)
                    for h in range(GRP):
                        if not first:
                            sp.wait_ge(s["op_full"], g * (GRP * RT) - (GRP - 1 - h) * RT)
                        sp.dma_start(wo_sb[:, h, :], wo[bass.ds((j * GRP + h) * HD, HD), :]).then_inc(wo_ld[h], 16)

                group_loads(0, True)
                with sp.Fori(1, HKV) as j:
                    group_loads(j, False)

        @block.scalar
        def _(act):
            def exp_piece(u, h, r, p):
                act.wait_ge(s["max_ready"], u * RT + (r + 1))
                w = prob[h][:, r, p * PIECE:(p + 1) * PIECE]
                act.activation(w, w, ACT.Exp, bias=nmax[:, h, r:r + 1], accum_out=rs[:, h, r, p:p + 1]).then_inc(s["p_ready"], 1)

            def pt_high(u, k):
                act.wait_ge(s["pt_full"], u * STEPS + (k + 1))
                if k >= PT:
                    act.wait_ge(s["pv_done"], u * STEPS + (k - PT + 1))
                act.activation(pth[:, k % PT, :], tp[k % 2][:, :], ACT.Copy).then_inc(s["pt_hi"], 1)

            def o_out(u, h):
                act.wait_ge(s["pv_done"], u * STEPS + STEPS)
                act.activation(oT[:, h, :], ov[:, 0:TQ], ACT.Copy).then_inc(s["ot_ready"], 1)

            def stage_proj(R, out, at, u, h, exps):
                for n in range(SB):
                    act.wait_ge(s["ring_full"], R + (at + n + 1))
                    act.activation(out(n), ring[(at + n) % RING][:, :], ACT.Copy).then_inc(s["kv_hi"], 1)
                    if exps and n % 2 == 1:
                        exp_piece(u, h, RT - 1, n // 2)

            def group_work(b, j, first):
                g, R = group(b, j), items(b, j)
                act.wait_ge(s["q_ld"], g * 16 + 16)
                if not first:
                    act.wait_ge(s["ring_full"], R)
                act.activation(qh[:, :, :], qf[:, :, :], ACT.Copy).then_inc(s["q_hi"], 1)
                stage_proj(R, lambda n: kh[:, n * BANK:(n + 1) * BANK], 0, g * GRP - 1, 1, not first)
                for h in range(GRP):
                    if h == 1:
                        stage_proj(R, lambda n: vh[:, n * 4:(n + 1) * 4, :], VI, g * GRP, 0, True)
                    for k in range(STEPS):
                        if h == 1 or not first:
                            pt_high(g * GRP + (h - 1), k)
                        if k > STEPS // 2 and k % 2 == 1:
                            exp_piece(g * GRP + h, h, 0, (k - STEPS // 2) // 2)
                    if h == 1 or not first:
                        o_out(g * GRP + (h - 1), (h + 1) % 2)

            act.sem_inc(s["ot_ready"], 1)
            with act.Fori(0, B) as b:
                group_work(b, 0, True)
                with act.Fori(1, HKV) as j:
                    group_work(b, j, False)
                u = b * (HKV * GRP) + (HKV * GRP - 1)
                for p in range(PIECES):
                    exp_piece(u, 1, RT - 1, p)
                for k in range(STEPS):
                    pt_high(u, k)
                o_out(u, 1)

        @block.vector
        def _(v):
            def item_lo(R, idx, count, out, high):
                v.wait_ge(s["kv_hi"], count)
                v.tensor_tensor(out, ring[idx % RING][:, :], high.bitcast(F32), ALU.subtract).then_inc(s["ring_free"], 1)

            def scores_out(R, idx, h, k, u):
                r, c = k // SB, k % SB
                v.wait_ge(s["ring_full"], R + (idx + 1))
                v.sem_inc(s["scores_seen"], 1)
                v.tensor_tensor_reduce(prob[h][:, r, c * BANK:(c + 1) * BANK], ring[idx % RING][:, :], maskb[:, c * BANK:(c + 1) * BANK],
                                       op0=ALU.add, op1=ALU.max, scale=1.0, scalar=NEG, accum_out=mx[:, h, r, c:c + 1]).then_inc(s["ring_free"], 1)
                if c == SB - 1:
                    v.wait_ge(s["ring_free"], R + (idx + 1))
                    v.tensor_reduce(nmax[:, h, r:r + 1], mx[:, h, r, :], op=ALU.max, axis=AX.X, negate=True).then_inc(s["max_ready"], 1)

            def pt_low(u, k):
                v.wait_ge(s["pt_hi"], u * STEPS + (k + 1))
                v.tensor_tensor(ptl[:, k % PT, :], tp[k % 2][:, :], pth[:, k % PT, :].bitcast(F32), ALU.subtract).then_inc(s["pt_lo"], 1)

            def inverse(u, h):
                v.wait_ge(s["p_ready"], u * (RT * PIECES) + RT * PIECES)
                v.tensor_reduce(rinv[:, :], rs[:, h, :, :], op=ALU.add, axis=AX.X).then_inc(s["inv_chain"], 1)
                v.wait_ge(s["inv_chain"], u * 3 + 1)
                v.reciprocal(rinv[:, :], rinv[:, :]).then_inc(s["inv_chain"], 1)
                v.wait_ge(s["inv_chain"], u * 3 + 2)
                v.tensor_scalar(rinv[:, :], rinv[:, :], anyv[:, 0:1], None, ALU.mult).then_inc(s["inv_chain"], 1)
                v.wait_ge(s["inv_chain"], u * 3 + 3)

            def residual(b, u, r):
                v.wait_ge(s["op_full"], u * RT + (r + 1))
                w = X[:, bass.ds(b * RT + r, 1), :].rearrange("p o d -> p (o d)")
                v.scalar_tensor_tensor(w, op[:, :], rinv[:, r:r + 1], w, ALU.mult, ALU.add).then_inc(s["op_free"], 1)

            def group_work(b, j, first):
                g, R = group(b, j), items(b, j)
                v.wait_ge(s["q_hi"], g + 1)
                v.tensor_tensor(ql[:, :, :], qf[:, :, :], qh[:, :, :].bitcast(F32), ALU.subtract).then_inc(s["q_lo"], 1)
                for h in range(GRP):
                    prev = h == 1 or not first
                    u = g * GRP + (h - 1)
                    done = g * GRP + (h - 2)
                    for n in range(SB):
                        if h == 0:
                            item_lo(R, n, g * (2 * SB) + (n + 1), kl[:, n * BANK:(n + 1) * BANK], kh[:, n * BANK:(n + 1) * BANK])
                        else:
                            item_lo(R, VI + n, g * (2 * SB) + (SB + n + 1), vl[:, n * 4:(n + 1) * 4, :].rearrange("p a b -> p (a b)"),
                                    vh[:, n * 4:(n + 1) * 4, :].rearrange("p a b -> p (a b)"))
                        if not first:
                            if n == 3:
                                inverse(done, h)
                            if n in (4, 5):
                                residual(b, done, n - 4)
                    for k in range(STEPS):
                        scores_out(R, QK[h] + k, h, k, g * GRP + h)
                        if prev:
                            pt_low(u, k)

            v.sem_inc(s["op_free"], 1)
            with v.Fori(0, B) as b:
                v.wait_ge(s["mask_ld"], b * 16 + 16)
                v.tensor_scalar(maskb[:, :], mask_u8, 1.0, -NEG, ALU.subtract, ALU.mult).then_inc(s["mask_ok"], 1)
                v.tensor_reduce(anyv[:, :], mask_u8, op=ALU.max, axis=AX.X).then_inc(s["mask_ok"], 1)
                v.wait_ge(s["mask_ok"], b * 2 + 2)
                for i in range(HEAD_ITEMS):
                    v.wait_ge(s["ring_full"], b * BATCH_ITEMS + (i + 1))
                    v.tensor_copy(ctxT[:, i % CC, i // CC * BANK:(i // CC + 1) * BANK], ring[i % RING][:, :]).then_inc(s["ring_free"], 1)
                group_work(b, 0, True)
                with v.Fori(1, HKV) as j:
                    group_work(b, j, False)
                u = b * (HKV * GRP) + (HKV * GRP - 1)
                inverse(u - 1, 0)
                for r in range(RT):
                    residual(b, u - 1, r)
                for k in range(STEPS):
                    pt_low(u, k)
                inverse(u, 1)
                for r in range(RT):
                    residual(b, u, r)

        @block.tensor
        def _(pe):
            def project(g, u, h, r):
                if r == 0:
                    pe.wait_ge(s["ot_ready"], u + 2)
                    pe.wait_ge(wo_ld[h], g * 16 + 16)
                pe.wait_ge(s["op_free"], u * RT + (r + 1))
                pe.matmul(op[:, :], oT[:, h, r * P:(r + 1) * P], wo_sb[:, h, :], start=True, stop=True).then_inc(s["op_full"], 1)

            def score_item(R, h, k):
                r, c = k // SB, k % SB
                idx = QK[h] + k
                pe.wait_ge(s["ring_free"], R + (idx - RING + 1))
                out, q = ring[idx % RING][:, :], (qh, ql)
                ks = (kh[:, c * BANK:(c + 1) * BANK], kl[:, c * BANK:(c + 1) * BANK])
                for n, (a, w) in enumerate(((0, 1), (1, 0), (0, 0))):
                    m = pe.matmul(out, q[a][:, h, r * P:(r + 1) * P], ks[w], start=n == 0, stop=n == 2)
                m.then_inc(s["ring_full"], 1)

            def transposes(u, h, k):
                if k == 0:
                    pe.wait_ge(s["p_ready"], u * (RT * PIECES) + RT * PIECES)
                if k >= 2:
                    pe.wait_ge(s["pt_lo"], u * STEPS + (k - 1))
                for c in range(2):
                    for r in range(RT):
                        at = (c * RT + r) * P
                        m = pe.transpose(tp[k % 2][:, at:at + P], prob[h][:, r, (2 * k + c) * P:(2 * k + c + 1) * P], ident[:, :])
                m.then_inc(s["pt_full"], 1)

            def pv(u, k):
                pe.wait_ge(s["pt_lo"], u * STEPS + (k + 1))
                if k == 0:
                    pe.wait_ge(s["ot_ready"], u + 1)
                for c in range(2):
                    for n, (a, w) in enumerate(((vh, ptl), (vl, pth), (vh, pth))):
                        m = pe.matmul(ov[:, 0:TQ], a[:, 2 * k + c, :], w[:, k % PT, c * TQ:(c + 1) * TQ],
                                      start=k == 0 and c == 0 and n == 0, stop=k == STEPS - 1 and c == 1 and n == 2)
                m.then_inc(s["pv_done"], 1)

            def group_work(b, j, first):
                g, R = group(b, j), items(b, j)
                for h in range(GRP):
                    prev = h == 1 or not first
                    u, done = g * GRP + (h - 1), g * GRP + (h - 2)
                    pe.wait_ge(s["wv_ld" if h else "wk_ld"], g * 16 + 16)
                    for n in range(SB):
                        idx = (VI if h else 0) + n
                        pe.wait_ge(s["ring_free"], R + (idx - RING + 1))
                        if h == 0:
                            for c in range(CC):
                                m = pe.matmul(ring[idx % RING][:, :], wk_sb[:, c, :], ctxT[:, c, n * BANK:(n + 1) * BANK], start=c == 0, stop=c == CC - 1)
                        else:
                            for q in range(4):
                                for c in range(CC):
                                    m = pe.matmul(ring[idx % RING][:, q * P:(q + 1) * P], ctxT[:, c, (4 * n + q) * P:(4 * n + q + 1) * P], wv_sb[:, c, :],
                                                  start=c == 0, stop=c == CC - 1)
                        m.then_inc(s["ring_full"], 1)
                        if not first and n in (4, 5):
                            project(g - 1, done, h, n - 4)
                    if h == 0:
                        pe.wait_ge(s["q_lo"], g + 1)
                        pe.wait_ge(s["ring_free"], R + SB)
                    for k in range(STEPS):
                        score_item(R, h, k)
                        if prev:
                            transposes(u, (h + 1) % 2, k)
                            if k >= LAG:
                                pv(u, k - LAG)
                    if prev:
                        for k in range(STEPS - LAG, STEPS):
                            pv(u, k)

            with pe.Fori(0, B) as b:
                pe.wait_ge(s["ctx_ld"], b * 64 + 64)
                for i in range(HEAD_ITEMS):
                    if i >= RING:
                        pe.wait_ge(s["ring_free"], b * BATCH_ITEMS + (i - RING + 1))
                    for q in range(4):
                        m = pe.transpose(ring[i % RING][:, q * P:(q + 1) * P], cin[:, i // CC * 4 + q, i % CC * P:(i % CC + 1) * P], ident[:, :])
                    m.then_inc(s["ring_full"], 1)
                pe.wait_ge(s["ring_free"], b * BATCH_ITEMS + HEAD_ITEMS)
                group_work(b, 0, True)
                with pe.Fori(1, HKV) as j:
                    group_work(b, j, False)
                g = b * HKV + (HKV - 1)
                u = g * GRP + 1
                for r in range(RT):
                    project(g, u - 1, 0, r)
                for k in range(STEPS + LAG):
                    if k < STEPS:
                        transposes(u, 1, k)
                    if k >= LAG:
                        pv(u, k - LAG)
                for r in range(RT):
                    project(g, u, 1, r)


def selfattn(nc, a, X, ident):
    HN, HW = 16, 32
    HC = P // HW
    N = B * KC
    with ExitStack() as ctx:
        t = Tensors(nc, ctx, "att")
        ln = ln_scratch(t)
        xn = t.sb("xn", [P, TT, D])
        xnT = t.sb("xnT", [P, KC, B * TQ])
        w_raw = [t.sb(f"w{i}", [P, KC, D]) for i in range(4)]
        wT = [t.sb(f"wT{i}", [P, KC, D]) for i in range(4)]
        bias_rows = t.sb("bias_rows", [2 * KC, P])
        bias_cols = t.sb("bias_cols", [P, 2 * KC])
        vo_rows = t.sb("vo_rows", [1, 2, D])
        ones = t.sb("ones", [1, P])
        qT = t.sb("qT", [P, N, TQ])
        kT = t.sb("kT", [P, N, TQ])
        V = t.sb("V", [P, N, RT, P])
        headmask = t.sb("headmask", [P, HC])
        decay = t.sb("decay", [P, RT, TQ])
        kz = [t.sb(f"kz{i}", [P, HC, P]) for i in range(2)]
        sc = [t.sb(f"sc{i}", [P, HC, TQ]) for i in range(2)]
        nmax = [t.sb(f"nmax{i}", [P, HC]) for i in range(2)]
        rsum = [t.sb(f"rsum{i}", [P, HC]) for i in range(2)]
        cT = t.sb("cT", [P, HC * RT, P])
        O = t.sb("O", [P, RT, N, P])
        oT = t.sb("oT", [P, KC, B * TQ])
        bank = [t.ps(f"bank{i}") for i in range(8)]
        s_ps = [bank[0:2], bank[2:4]]
        t_ps, o_ps = bank[4:6], bank[6:8]
        names = ("var_ready", "root_ready", "xn_ready", "chain", "consts", "b_ld", "xT_ps", "xT_ok", "wT_ps", "wT_act", "wT_dve",
                 "bias_ps", "bias_ok", "q_ps", "q_ok", "k_ps", "k_ok", "v_ps", "v_ok", "kz_ok", "s_ps", "s_ok", "exp_ok",
                 "t_ps", "t_act", "t_dve", "o_ps", "o_ok", "inv", "oT_ps", "oT_ok", "out_ps", "out_ok")
        s = {n: t.sem(n) for n in names}
        w_ld = [t.sem(f"w_ld{i}") for i in range(4)]
        block = ctx.enter_context(nc.Block())
        wnames = ("q", "k", "v", "o")

        def bank_of(h, it):
            return (0, h * P, P) if it == 0 else (h // 2, h % 2 * TQ, TQ)

        @block.sync
        def _(sp):
            for i, n in enumerate(wnames):
                sp.dma_start(w_raw[i][:, :, :], a[f"L0_attn_{n}_w"].rearrange("(c p) n -> p c n", p=P)).then_inc(w_ld[i], 16)
            for i, n in enumerate(("q", "k")):
                sp.dma_start(bias_rows[i * KC:(i + 1) * KC, :], a[f"L0_attn_{n}_b"].rearrange("(c p) -> c p", p=P)).then_inc(s["b_ld"], 16)
            for i, n in enumerate(("v", "o")):
                sp.dma_start(vo_rows[:, i, :], a[f"L0_attn_{n}_b"].rearrange("(o d) -> o d", o=1)).then_inc(s["b_ld"], 16)

        @block.gpsimd
        def _(pool):
            c = s["consts"]
            nc.gpsimd.memset(ones[:, :], 1.0).then_inc(c, 1)
            nc.gpsimd.memset(headmask[:, :], 1.0).then_inc(c, 1)
            nc.gpsimd.iota(decay[:, :, :], pattern=[[-P, RT], [1, TQ]], base=0, channel_multiplier=-1, allow_small_or_imprecise_dtypes=True).then_inc(c, 1)
            pool.wait_ge(c, 3)
            nc.gpsimd.affine_select(out=headmask[:, :], in_=headmask[:, :], compare_op=ALU.is_ge, fill=0.0,
                                    base=0, pattern=[[-HW, HC]], channel_multiplier=1).then_inc(c, 1)
            pool.wait_ge(c, 4)
            nc.gpsimd.affine_select(out=headmask[:, :], in_=headmask[:, :], compare_op=ALU.is_ge, fill=0.0,
                                    base=HW - 1, pattern=[[HW, HC]], channel_multiplier=-1).then_inc(c, 1)
            nc.gpsimd.affine_select(out=decay[:, :, :], in_=decay[:, :, :], compare_op=ALU.is_ge, fill=NEG,
                                    base=0, pattern=[[P, RT], [-1, TQ]], channel_multiplier=1).then_inc(c, 1)

        @block.vector
        def _(v):
            ch = Chain(v, s["chain"])
            def weight(i):
                v.wait_ge(s["wT_ps"], i + 1)
                v.tensor_copy(wT[i // KC][:, i % KC, :], bank[i % 4][:, :]).then_inc(s["wT_dve"], 1)

            ln_vector(v, ch, X, xn, ln, s["root_ready"], s["var_ready"])
            v.engine_nop().then_inc(s["xn_ready"], 1)
            for i in range(1, 4 * KC, 2):
                weight(i)
            v.wait_ge(s["bias_ps"], 1)
            v.tensor_copy(bias_cols[:, :], bank[4][:, 0:2 * KC]).then_inc(s["bias_ok"], 1)
            for c in range(KC):
                v.wait_ge(s["xT_ps"], c + 1)
                v.tensor_copy(xnT[:, c, :], bank[4 + c][:, :]).then_inc(s["xT_ok"], 1)
            v.wait_ge(s["bias_ok"], 1)
            for c in range(KC):
                v.wait_ge(s["q_ps"], c + 1)
                v.tensor_scalar(qT.rearrange("p (b c) n -> p c b n", b=B)[:, c], bank[c][:, :].rearrange("p (b n) -> p b n", b=B),
                                bias_cols[:, c:c + 1], HW ** -0.5, ALU.add, ALU.mult).then_inc(s["q_ok"], 1)
            for i in range(TT):
                v.wait_ge(s["v_ps"], i + 1)
                v.tensor_copy(V.rearrange("p (b c) r n -> p b r c n", b=B)[:, i // RT, i % RT], bank[i][:, :].rearrange("p (c n) -> p c n", c=KC)).then_inc(s["v_ok"], 1)
            v.wait_ge(s["consts"], 6)
            v.wait_ge(s["k_ok"], KC)
            v.sem_inc(s["o_ok"], 2)

            def keys(it, n, par):
                v.tensor_tensor(kz[par][:, :, :], kT[:, bass.ds(n, 1), it * P:(it + 1) * P].to_broadcast([P, HC, P]),
                                headmask[:, :].unsqueeze(2).to_broadcast([P, HC, P]), ALU.mult).then_inc(s["kz_ok"], 1)

            def scores(it, n, par):
                u, J = n + it * N, (it + 1) * P
                v.wait_ge(s["s_ps"], u + 1)
                if it == 0:
                    v.tensor_tensor(sc[par][:, :, 0:J], s_ps[par][0][:, :].rearrange("p (h j) -> p h j", h=HC),
                                    decay[:, 0:1, 0:J].to_broadcast([P, HC, J]), ALU.add).then_inc(s["s_ok"], 2)
                else:
                    for q in range(2):
                        v.tensor_tensor(sc[par][:, 2 * q:2 * q + 2, :], s_ps[par][q][:, :].rearrange("p (h j) -> p h j", h=2),
                                        decay[:, 1:2, :].to_broadcast([P, 2, TQ]), ALU.add).then_inc(s["s_ok"], 1)
                v.wait_ge(s["s_ok"], u * 3 + 2)
                v.tensor_reduce(nmax[par][:, :], sc[par][:, :, 0:J], op=ALU.max, axis=AX.X, negate=True).then_inc(s["s_ok"], 1)

            def outputs(it, n, par):
                u = n + it * N
                if it == 1:
                    v.wait_ge(s["t_ps"], u * RT + 2)
                    v.tensor_copy(cT[:, HC:2 * HC, :].rearrange("p a b -> p (a b)"), t_ps[1][:, :]).then_inc(s["t_dve"], 1)
                v.wait_ge(s["exp_ok"], u * HC + HC)
                v.reciprocal(rsum[par][:, :], rsum[par][:, :]).then_inc(s["inv"], 1)
                v.wait_ge(s["inv"], u + 1)
                v.wait_ge(s["o_ps"], u + 1)
                v.tensor_tensor(O[:, it, bass.ds(n, 1), :].rearrange("p o (h w) -> p (o h) w", h=HC), o_ps[par][:, 0:P].rearrange("p (h w) -> p h w", h=HC),
                                rsum[par][:, :].unsqueeze(2).to_broadcast([P, HC, HW]), ALU.mult).then_inc(s["o_ok"], 1)

            for it in range(RT):
                keys(it, 0, 0)
                keys(it, 1, 1)
                scores(it, 0, 0)
                with v.Fori(0, (N - 2) // 2) as m:
                    for q in range(2):
                        n = m * 2 + q
                        scores(it, n + 1, (q + 1) % 2)
                        keys(it, n + 2, q)
                        outputs(it, n, q)
                scores(it, N - 1, 1)
                outputs(it, N - 2, 0)
                outputs(it, N - 1, 1)
            v.wait_ge(s["o_ok"], N * RT + 2)
            for c in range(KC):
                v.wait_ge(s["oT_ps"], c + 1)
                v.tensor_copy(oT[:, c, :], bank[c][:, :]).then_inc(s["oT_ok"], 1)
            for i in range(TT):
                v.wait_ge(s["out_ps"], i + 1)
                v.tensor_tensor(X[:, i, :], X[:, i, :], bank[4 + i][:, :], ALU.add).then_inc(s["out_ok"], 1)

        @block.scalar
        def _(act):
            act.wait_ge(s["var_ready"], 1)
            act.activation(ln["root"][:, :], ln["veps"][:, :], ACT.Sqrt).then_inc(s["root_ready"], 1)
            for i in range(0, 4 * KC, 2):
                act.wait_ge(s["wT_ps"], i + 1)
                act.activation(wT[i // KC][:, i % KC, :], bank[i % 4][:, :], ACT.Copy).then_inc(s["wT_act"], 1)
            act.wait_ge(s["bias_ok"], 1)
            for c in range(KC):
                act.wait_ge(s["k_ps"], c + 1)
                act.activation(kT.rearrange("p (b c) n -> p c b n", b=B)[:, c], bank[4 + c][:, :].rearrange("p (b n) -> p b n", b=B),
                               ACT.Identity, bias=bias_cols[:, KC + c:KC + c + 1]).then_inc(s["k_ok"], 1)

            def softmax(it, n, par):
                u, J = n + it * N, (it + 1) * P
                act.wait_ge(s["s_ok"], u * 3 + 3)
                for h in range(HC):
                    w = sc[par][:, h, 0:J]
                    act.activation(w, w, ACT.Exp, bias=nmax[par][:, h:h + 1], accum_out=rsum[par][:, h:h + 1]).then_inc(s["exp_ok"], 1)

            def turned(it, n):
                u = n + it * N
                act.wait_ge(s["t_ps"], u * RT + 1)
                act.activation(cT[:, 0:HC, :].rearrange("p a b -> p (a b)"), t_ps[0][:, :], ACT.Copy).then_inc(s["t_act"], 1)

            for it in range(RT):
                softmax(it, 0, 0)
                with act.Fori(0, (N - 2) // 2) as m:
                    for q in range(2):
                        n = m * 2 + q
                        turned(it, n)
                        softmax(it, n + 1, (q + 1) % 2)
                turned(it, N - 2)
                softmax(it, N - 1, 1)
                turned(it, N - 1)

        @block.tensor
        def _(pe):
            for i in range(4 * KC):
                w, c = i // KC, i % KC
                if c == 0:
                    pe.wait_ge(w_ld[w], 16)
                if i >= 4:
                    pe.wait_ge(s["wT_dve" if i % 2 else "wT_act"], (i - 4) // 2 + 1)
                for o in range(KC):
                    m = pe.transpose(bank[i % 4][:, o * P:(o + 1) * P], w_raw[w][:, o, c * P:(c + 1) * P], ident[:, :])
                m.then_inc(s["wT_ps"], 1)
            pe.wait_ge(s["b_ld"], 64)
            pe.matmul(bank[4][:, 0:2 * KC], bias_rows[:, :], ident[0:2 * KC, 0:2 * KC], start=True, stop=True).then_inc(s["bias_ps"], 1)
            pe.wait_ge(s["xn_ready"], 1)
            pe.wait_ge(s["bias_ok"], 1)
            for c in range(KC):
                for i in range(TT):
                    m = pe.transpose(bank[4 + c][:, i * P:(i + 1) * P], xn[:, i, c * P:(c + 1) * P], ident[:, :])
                m.then_inc(s["xT_ps"], 1)
            pe.wait_ge(s["xT_ok"], KC)
            pe.wait_ge(s["wT_act"], 2 * KC)
            pe.wait_ge(s["wT_dve"], 2 * KC)
            for base, w, done in ((0, 0, "q_ps"), (4, 1, "k_ps")):
                for o in range(KC):
                    for c in range(KC):
                        m = pe.matmul(bank[base + o][:, :], wT[w][:, c, o * P:(o + 1) * P], xnT[:, c, :], start=c == 0, stop=c == KC - 1)
                    m.then_inc(s[done], 1)
            pe.wait_ge(s["consts"], 6)
            for i in range(TT):
                pe.wait_ge(s["q_ok"], i + 1)
                for c in range(KC):
                    pe.matmul(bank[i][:, :], xnT[:, c, i * P:(i + 1) * P], wT[2][:, c, :], start=c == 0, stop=False)
                pe.matmul(bank[i][:, :], ones[:, :], vo_rows[:, 0, :], start=False, stop=True).then_inc(s["v_ps"], 1)
            pe.wait_ge(s["k_ok"], KC)
            pe.wait_ge(s["v_ok"], TT)

            def scores(it, n, par):
                u, J = n + it * N, (it + 1) * P
                pe.wait_ge(s["kz_ok"], u + 1)
                for h in range(HC):
                    k, at, w = bank_of(h, it)
                    m = pe.matmul(s_ps[par][k][:, at:at + w], kz[par][:, h, :], qT[:, bass.ds(n, 1), 0:J].rearrange("p o j -> p (o j)"), start=True, stop=True)
                m.then_inc(s["s_ps"], 1)

            def attend(it, n, par):
                u = n + it * N
                pe.wait_ge(s["exp_ok"], u * HC + HC)
                for j in range(it + 1):
                    for h in range(HC):
                        m = pe.transpose(t_ps[j][:, h * P:(h + 1) * P], sc[par][:, h, j * P:(j + 1) * P], ident[:, :])
                    m.then_inc(s["t_ps"], RT - it)
                pe.wait_ge(s["t_act"], u + 1)
                if it == 1:
                    pe.wait_ge(s["t_dve"], n + 1)
                pe.wait_ge(s["o_ok"], u + 1)
                for h in range(HC):
                    for j in range(it + 1):
                        m = pe.matmul(o_ps[par][:, h * HW:(h + 1) * HW], cT[:, j * HC + h, :],
                                      V[:, bass.ds(n, 1), j, h * HW:(h + 1) * HW].rearrange("p o w -> p (o w)"), start=j == 0, stop=j == it)
                m.then_inc(s["o_ps"], 1)

            for it in range(RT):
                scores(it, 0, 0)
                with pe.Fori(0, (N - 2) // 2) as m:
                    for q in range(2):
                        n = m * 2 + q
                        scores(it, n + 1, (q + 1) % 2)
                        attend(it, n, q)
                scores(it, N - 1, 1)
                attend(it, N - 2, 0)
                attend(it, N - 1, 1)
            pe.wait_ge(s["o_ok"], N * RT + 2)
            for c in range(KC):
                for i in range(TT):
                    m = pe.transpose(bank[c][:, i * P:(i + 1) * P], O[:, i % RT, i // RT * KC + c, :], ident[:, :])
                m.then_inc(s["oT_ps"], 1)
            pe.wait_ge(s["oT_ok"], KC)
            for i in range(TT):
                for c in range(KC):
                    pe.matmul(bank[4 + i][:, :], oT[:, c, i * P:(i + 1) * P], wT[3][:, c, :], start=c == 0, stop=False)
                pe.matmul(bank[4 + i][:, :], ones[:, :], vo_rows[:, 1, :], start=False, stop=True).then_inc(s["out_ps"], 1)


def experts(nc, a, out, X, ident):
    E, K = 8, 2
    CAP = int(B * TQ * 1.25 / E)
    SL = K * CAP
    F = 4 * D
    FC = F // P
    R = 32
    STRIDE = 1024
    LOWEST = -87.5
    with ExitStack() as ctx:
        t = Tensors(nc, ctx, "moe")
        w1 = [t.sb(f"w1_{i}", [P, KC, F]) for i in range(2)]
        w2 = [t.sb(f"w2_{i}", [P, FC, D]) for i in range(2)]
        wd = [t.sb(f"wd_{i}", [P, KC, R]) for i in range(2)]
        wu = [t.sb(f"wu_{i}", [R, D]) for i in range(2)]
        gate = t.sb("gate", [P, KC, E])
        xh, xl = t.sb("xh", [P, TT, D], F32R), t.sb("xl", [P, TT, D], F32R)
        sb2_row = t.sb("sb2_row", [1, D])
        b1_cols, b_cols = t.sb("b1_cols", [P, P]), t.sb("b_cols", [P, P])
        ones = t.sb("ones", [1, P])
        prob = t.sb("prob", [P, TT, E])
        lg = t.sb("lg", [P, TT, E])
        small = t.sb("small", [P, TT])
        top, topp = t.sb("top", [P, TT, 8]), t.sb("topp", [P, TT, 8])
        topi, topf = t.sb("topi", [P, TT, 8], U32), t.sb("topf", [P, TT, 8])
        onehot = t.sb("onehot", [P, TT, K, E])
        cnt = t.sb("cnt", [P, TT, K, E])
        ids = t.sb("ids", [P, TT, K])
        tri, all1 = t.sb("tri", [P, P]), t.sb("all1", [P, P])
        iota8, iotaS = t.sb("iota8", [P, E]), t.sb("iotaS", [P, CAP])
        ecol = t.sb("ecol", [P, E])
        rows = t.sb("rows", [CAP, K, B * TQ])
        sel = t.sb("sel", [P, TT, SL], F32R)
        bufT = t.sb("bufT", [P, KC, SL])
        rT = t.sb("rT", [R, SL])

        bank = [t.ps(f"bank{i}") for i in range(8)]
        h_ps, y_ps, t_ps, c_ps = bank[0:2], bank[2:4], bank[4:6], bank[6:8]

        names = ("consts", "chain", "var_ready", "root_ready", "xn_ready", "rows_ld", "gate_ld", "xT_ps", "xT_ok", "x_hi", "bT_ps", "bT_ok",
                 "lg_ps", "lm_ok", "exp_ok", "oh_ok", "cnt_ps", "ids_ok", "rows_ps", "rows_ok",
                 "sh_ps", "sh_ok", "sr_ps", "sr_ok", "so_ps", "so_ok",
                 "sel_ok", "g_ps", "g_ok", "h_ps", "h_ok", "r_ps", "r_ok", "y_ps", "y_ok", "yt_ps", "yt_hi", "yt_lo", "comb_ok", "c_ps", "c_ok", "stored")
        s = {n: t.sem(n) for n in names}
        w1_ld, w2_ld, ad_ld = ([t.sem(f"{n}{i}") for i in range(2)] for n in ("w1_ld", "w2_ld", "ad_ld"))

        with ExitStack() as first:
            f = Tensors(nc, first, "sh")
            ln = ln_scratch(f)
            xn = f.sb("xn", [P, TT, D])
            xnT = f.sb("xnT", [P, KC, B * TQ])
            b1_rows, b_rows = f.sb("b1_rows", [P, P]), f.sb("b_rows", [P, P])
            hS = f.sb("hS", [P, 8, B * TQ])
        rS = bufT[0:R, :, :].rearrange("p c n -> p (c n)")[:, 0:B * TQ]
        second = ctx.enter_context(ExitStack())
        f = Tensors(nc, second, "ex")
        hT = f.sb("hT", [P, FC, SL])
        yT = f.sb("yT", [P, KC, SL])
        yh, yl = f.sb("yh", [CAP, K, D], F32R), f.sb("yl", [CAP, K, D], F32R)
        comb = f.sb("comb", [CAP, K, B * TQ], F32R)
        block = ctx.enter_context(nc.Block())

        SB1 = E * KC

        @block.sync
        def _(sp):
            sp.dma_start(gate[:, :, :], a["L0_ffn_gate_w"].rearrange("(c p) e -> p c e", p=P)).then_inc(s["gate_ld"], 16)
            for c in range(KC):
                sp.dma_start(w1[1][:, c, :], a["L0_ffn_sw1"][c * P:(c + 1) * P, :]).then_inc(w1_ld[1], 16)
            sp.dma_start(wd[1][:, :, :], a["L0_ffn_swd"].rearrange("(c p) r -> p c r", p=P)).then_inc(ad_ld[1], 16)
            sp.dma_start(wu[1][:, :], a["L0_ffn_swu"]).then_inc(ad_ld[1], 16)
            for c in range(4):
                sp.dma_start(w2[1][:, c * 4:(c + 1) * 4, :], a["L0_ffn_sw2"][c * 4 * P:(c + 1) * 4 * P, :].rearrange("(c p) n -> p c n", p=P)).then_inc(w2_ld[1], 16)

            def expert_loads(e, i):
                for c in range(KC):
                    sp.dma_start(w1[i][:, c, :], a["L0_ffn_w1"][bass.ds(e, 1), c * P:(c + 1) * P, :].rearrange("o p n -> (o p) n")).then_inc(w1_ld[i], 16)
                sp.dma_start(wd[i][:, :, :], a["L0_ffn_wd"][bass.ds(e, 1), :, :].rearrange("o (c p) r -> p (o c) r", p=P)).then_inc(ad_ld[i], 16)
                sp.dma_start(wu[i][:, :], a["L0_ffn_wu"][bass.ds(e, 1), :, :].rearrange("o r n -> (o r) n")).then_inc(ad_ld[i], 16)

            def expert_loads2(e, i):
                for c in range(4):
                    sp.dma_start(w2[i][:, c * 4:(c + 1) * 4, :],
                                 a["L0_ffn_w2"][bass.ds(e, 1), c * 4 * P:(c + 1) * 4 * P, :].rearrange("o (c p) n -> p (o c) n", p=P)).then_inc(w2_ld[i], 16)

            expert_loads(0, 0)
            expert_loads2(0, 0)
            sp.wait_ge(s["sh_ps"], FC)
            sp.wait_ge(s["so_ps"], TT * 2)
            expert_loads(1, 1)
            expert_loads2(1, 1)
            with sp.Fori(0, (E - 2) // 2) as m:
                for q in range(2):
                    e = m * 2 + q
                    sp.wait_ge(s["r_ps"], e + 1)
                    sp.wait_ge(s["y_ps"], e * 2 + 2)
                    expert_loads(e + 2, q)
                    expert_loads2(e + 2, q)
            sp.wait_ge(s["c_ok"], E * K * TT)
            sp.dma_start(out.rearrange("b (r p) d -> p (b r) d", p=P), X[:, :, :]).then_inc(s["stored"], 16)
            sp.wait_ge(s["stored"], 16)

        @block.gpsimd
        def _(pool):
            c = s["consts"]
            nc.gpsimd.memset(ones[:, :], 1.0).then_inc(c, 1)
            nc.gpsimd.memset(all1[:, :], 1.0).then_inc(c, 1)
            nc.gpsimd.memset(tri[:, :], 1.0).then_inc(c, 1)
            nc.gpsimd.memset(b_rows[:, :], 0.0).then_inc(c, 1)
            nc.gpsimd.iota(iota8[:, :], pattern=[[1, E]], base=0, channel_multiplier=0, allow_small_or_imprecise_dtypes=True).then_inc(c, 1)
            nc.gpsimd.iota(iotaS[:, :], pattern=[[1, CAP]], base=1, channel_multiplier=0, allow_small_or_imprecise_dtypes=True).then_inc(c, 1)
            nc.gpsimd.iota(ecol[:, :], pattern=[[STRIDE, E]], base=1, channel_multiplier=1, allow_small_or_imprecise_dtypes=True).then_inc(c, 1)
            pool.wait_ge(c, 7)
            nc.gpsimd.affine_select(out=tri[:, :], in_=tri[:, :], compare_op=ALU.is_ge, fill=0.0,
                                    base=0, pattern=[[1, P]], channel_multiplier=-1).then_inc(c, 1)
            r = s["rows_ld"]
            pool.dma_start(b1_rows[:, :], a["L0_ffn_b1"].rearrange("e (c p) -> (e c) p", p=P)).then_inc(r, 16)
            pool.dma_start(b_rows[0:SB1, :], a["L0_ffn_b2"].rearrange("e (c p) -> (e c) p", p=P)).then_inc(r, 16)
            pool.dma_start(b_rows[SB1:SB1 + FC, :], a["L0_ffn_sb1"].rearrange("(c p) -> c p", p=P)).then_inc(r, 16)
            pool.dma_start(sb2_row[:, :], a["L0_ffn_sb2"].rearrange("(o d) -> o d", o=1)).then_inc(r, 16)
            pool.wait_ge(r, 64)

        @block.vector
        def _(v):
            ch = Chain(v, s["chain"])
            ln_vector(v, ch, X, xn, ln, s["root_ready"], s["var_ready"])
            v.engine_nop().then_inc(s["xn_ready"], 1)
            for c in range(KC):
                v.wait_ge(s["xT_ps"], c + 1)
                v.tensor_copy(xnT[:, c, :], bank[c][:, :]).then_inc(s["xT_ok"], 1)
            for i, cols in enumerate((b1_cols, b_cols)):
                v.wait_ge(s["bT_ps"], i + 1)
                v.tensor_copy(cols[:, :], bank[4 + i][:, 0:P]).then_inc(s["bT_ok"], 1)
            v.wait_ge(s["x_hi"], 1)
            v.tensor_tensor(xl[:, :, :], xn[:, :, :], xh[:, :, :].bitcast(F32), ALU.subtract).then_inc(s["x_hi"], 1)
            v.wait_ge(s["consts"], 8)
            v.wait_ge(s["lg_ps"], 1)
            ch.link(v.tensor_copy(lg[:, :, :], bank[6][:, 0:TT * E].rearrange("p (i e) -> p i e", e=E)))
            ch.link(v.tensor_reduce(small[:, :], lg[:, :, :], op=ALU.max, axis=AX.X))
            ch.link(v.tensor_tensor(lg[:, :, :], lg[:, :, :], small[:, :].unsqueeze(2).to_broadcast([P, TT, E]), ALU.subtract))
            ch.link(v.tensor_scalar(lg[:, :, :], lg[:, :, :], LOWEST, None, ALU.max))
            for i in range(TT):
                v.max(top[:, i, :], lg[:, i, :]).then_inc(s["chain"], 1)
            ch.n += TT
            v.wait_ge(s["chain"], ch.n)
            for i in range(TT):
                v.max_index(topi[:, i, :], top[:, i, :], lg[:, i, :]).then_inc(s["lm_ok"], 1)
            v.wait_ge(s["lm_ok"], TT)
            ch.link(v.tensor_copy(topf[:, :, :], topi[:, :, :]))
            for i in range(TT):
                for k in range(K):
                    v.tensor_scalar(onehot[:, i, k, :], iota8[:, :], topf[:, i, k:k + 1], None, ALU.is_equal).then_inc(s["oh_ok"], 1)
            v.wait_ge(s["exp_ok"], 2)
            ch.link(v.tensor_reduce(small[:, :], prob[:, :, :], op=ALU.add, axis=AX.X))
            ch.link(v.reciprocal(small[:, :], small[:, :]))
            ch.link(v.tensor_tensor(topp[:, :, :], topp[:, :, :], small[:, :].unsqueeze(2).to_broadcast([P, TT, 8]), ALU.mult))
            v.wait_ge(s["cnt_ps"], 1)
            ch.link(v.tensor_tensor(cnt[:, :, :, :].rearrange("p i k e -> p (i k e)"), bank[7][:, 0:TT * K * E],
                                    onehot[:, :, :, :].rearrange("p i k e -> p (i k e)"), ALU.mult))
            v.wait_ge(s["oh_ok"], TT * K)
            v.tensor_reduce(ids[:, :, :].rearrange("p i k -> p (i k)"), cnt[:, :, :, :].rearrange("p i k e -> p (i k) e"), op=ALU.add, axis=AX.X).then_inc(s["chain"], 1)
            ch.n += 1
            v.wait_ge(s["chain"], ch.n)
            v.scalar_tensor_tensor(ids[:, :, :], topf[:, :, 0:K], float(STRIDE), ids[:, :, :], ALU.mult, ALU.add).then_inc(s["ids_ok"], 1)

            def select(e):
                for k in range(K):
                    for i in range(TT):
                        m = v.tensor_scalar(sel[:, i, k * CAP:(k + 1) * CAP], iotaS[:, :], cnt[:, i, k, bass.ds(e, 1)], None, ALU.is_equal)
                        if i == TT - 1 and k == K - 1:
                            m.then_inc(s["sel_ok"], 1)

            def combine(e):
                for k in range(K):
                    m = v.tensor_scalar(comb[:, k, :], rows[:, k, :], ecol[0:CAP, bass.ds(e, 1)], None, ALU.is_equal)
                m.then_inc(s["comb_ok"], 1)

            for k in range(K):
                v.wait_ge(s["rows_ps"], k + 1)
                v.tensor_copy(rows[:, k, :], bank[4 + k][0:CAP, :]).then_inc(s["rows_ok"], 1)
            select(0)
            for i in range(2 * TT):
                v.wait_ge(s["so_ps"], i + 1)
                v.scalar_tensor_tensor(X[:, i % TT, :], bank[2 + i % 2][:, :], 0.2, X[:, i % TT, :], ALU.mult, ALU.add).then_inc(s["so_ok"], 1)
            v.wait_ge(s["rows_ok"], K)

            def turned(e):
                for k in range(K):
                    v.wait_ge(s["yt_hi"], e * K + (k + 1))
                    v.tensor_tensor(yl[:, k, :], t_ps[k][0:CAP, :], yh[:, k, :].bitcast(F32), ALU.subtract).then_inc(s["yt_lo"], 1)

            def residual(e):
                for k in range(K):
                    for i in range(TT):
                        n = k * TT + i
                        v.wait_ge(s["c_ps"], e * (K * TT) + (n + 1))
                        v.scalar_tensor_tensor(X[:, i, :], c_ps[n % 2][:, :], topp[:, i, k:k + 1], X[:, i, :], ALU.mult, ALU.add).then_inc(s["c_ok"], 1)

            def biased(e):
                for c in range(KC):
                    v.wait_ge(s["y_ps"], e * 2 + (c // 2 + 1))
                    m = v.tensor_scalar(yT[:, c, :], y_ps[c // 2][:, c % 2 * SL:(c % 2 + 1) * SL], b_cols[:, bass.ds(e * KC + c, 1)], None, ALU.add)
                    if c % 2:
                        m.then_inc(s["y_ok"], 1)

            def expert(e, first, last):
                if not last:
                    v.wait_ge(s["g_ps"], e * 2 + 2)
                    select(e + 1)
                if not first:
                    turned(e - 1)
                    residual(e - 1)
                combine(e)
                biased(e)

            expert(0, True, False)
            with v.Fori(0, (E - 2) // 2) as m:
                for q in range(2):
                    expert(m * 2 + (q + 1), False, False)
            expert(E - 1, False, True)
            turned(E - 1)
            residual(E - 1)

        @block.scalar
        def _(act):
            act.wait_ge(s["var_ready"], 1)
            act.activation(ln["root"][:, :], ln["veps"][:, :], ACT.Sqrt).then_inc(s["root_ready"], 1)
            act.wait_ge(s["xn_ready"], 1)
            act.activation(xh[:, :, :], xn[:, :, :], ACT.Copy).then_inc(s["x_hi"], 1)
            act.wait_ge(s["lm_ok"], TT)
            act.activation(prob[:, :, :], lg[:, :, :], ACT.Exp).then_inc(s["exp_ok"], 1)
            act.activation(topp[:, :, :], top[:, :, :], ACT.Exp).then_inc(s["exp_ok"], 1)
            act.wait_ge(s["bT_ok"], 2)
            for n in range(FC):
                act.wait_ge(s["sh_ps"], n + 1)
                if n == FC // 2:
                    act.wait_ge(s["so_ps"], TT)
                act.activation(hS[:, n % 8, :], h_ps[n % 2][:, :], ACT.Gelu, bias=b_cols[:, SB1 + n:SB1 + n + 1]).then_inc(s["sh_ok"], 1)
                if n == 0:
                    act.wait_ge(s["sr_ps"], 1)
                    act.activation(rS[:, :], bank[6][0:R, :], ACT.Gelu).then_inc(s["sr_ok"], 1)

            def gathered(e):
                for q in range(2):
                    act.wait_ge(s["g_ps"], e * 2 + (q + 1))
                    act.activation(bufT[:, 2 * q:2 * q + 2, :].rearrange("p c n -> p (c n)"), t_ps[q][:, 0:2 * SL], ACT.Copy).then_inc(s["g_ok"], 1)

            def hidden(e, n):
                act.wait_ge(s["h_ps"], e * (FC // 2) + (n + 1))
                for q in range(2):
                    m = act.activation(hT[:, 2 * n + q, :], h_ps[n % 2][:, q * SL:(q + 1) * SL], ACT.Gelu, bias=b1_cols[:, bass.ds(e * FC + (2 * n + q), 1)])
                m.then_inc(s["h_ok"], 1)

            def turned(e):
                for k in range(K):
                    act.wait_ge(s["yt_ps"], e * K + (k + 1))
                    act.activation(yh[:, k, :], t_ps[k][0:CAP, :], ACT.Copy).then_inc(s["yt_hi"], 1)

            def expert(e, first, last):
                for n in range(4):
                    hidden(e, n)
                if not first:
                    turned(e - 1)
                for n in range(4, FC // 2):
                    hidden(e, n)
                act.wait_ge(s["r_ps"], e + 1)
                act.activation(rT[:, :], bank[6][0:R, 0:SL], ACT.Gelu).then_inc(s["r_ok"], 1)
                if not last:
                    gathered(e + 1)

            gathered(0)
            expert(0, True, False)
            with act.Fori(0, (E - 2) // 2) as m:
                for q in range(2):
                    expert(m * 2 + (q + 1), False, False)
            expert(E - 1, False, True)
            turned(E - 1)

        @block.tensor
        def _(pe):
            pe.wait_ge(s["xn_ready"], 1)
            for c in range(KC):
                for i in range(TT):
                    m = pe.transpose(bank[c][:, i * P:(i + 1) * P], xn[:, i, c * P:(c + 1) * P], ident[:, :])
                m.then_inc(s["xT_ps"], 1)
            pe.wait_ge(s["rows_ld"], 64)
            pe.transpose(bank[4][:, 0:P], b1_rows[:, :], ident[:, :]).then_inc(s["bT_ps"], 1)
            pe.transpose(bank[5][:, 0:P], b_rows[:, :], ident[:, :]).then_inc(s["bT_ps"], 1)
            pe.wait_ge(s["xT_ok"], KC)
            pe.wait_ge(s["gate_ld"], 16)
            for i in range(TT):
                for c in range(KC):
                    m = pe.matmul(bank[6][:, i * E:(i + 1) * E], xnT[:, c, i * P:(i + 1) * P], gate[:, c, :], start=c == 0, stop=c == KC - 1)
            m.then_inc(s["lg_ps"], 1)

            def shared_hidden(n):
                if n >= 2:
                    pe.wait_ge(s["sh_ok"], n - 1)
                for c in range(KC):
                    m = pe.matmul(h_ps[n % 2][:, :], w1[1][:, c, n * P:(n + 1) * P], xnT[:, c, :], start=c == 0, stop=c == KC - 1)
                m.then_inc(s["sh_ps"], 1)

            def shared_out(half):
                pe.wait_ge(s["sh_ok"], (half + 1) * 8)
                for i in range(TT):
                    n = half * TT + i
                    if n >= 2:
                        pe.wait_ge(s["so_ok"], n - 1)
                    o = bank[2 + n % 2][:, :]
                    for c in range(8):
                        m = pe.matmul(o, hS[:, c, i * P:(i + 1) * P], w2[1][:, half * 8 + c, :], start=c == 0, stop=half == 0 and c == 7)
                    if half == 1:
                        pe.matmul(o, rS[:, i * P:(i + 1) * P], wu[1][:, :], start=False, stop=False)
                        m = pe.matmul(o, ones[:, :], sb2_row[:, :], start=False, stop=True)
                    m.then_inc(s["so_ps"], 1)

            pe.wait_ge(w1_ld[1], 64)
            pe.wait_ge(s["consts"], 8)
            shared_hidden(0)
            pe.wait_ge(s["lm_ok"], TT)
            pe.wait_ge(ad_ld[1], 32)
            for c in range(KC):
                m = pe.matmul(bank[6][0:R, :], wd[1][:, c, :], xnT[:, c, :], start=c == 0, stop=c == KC - 1)
            m.then_inc(s["sr_ps"], 1)
            for n in range(1, 4):
                shared_hidden(n)
            pe.wait_ge(s["oh_ok"], TT * K)
            for i in range(TT):
                for q in range(i + 1):
                    m = pe.matmul(bank[7][:, i * K * E:(i + 1) * K * E], (tri if q == i else all1)[:, :], onehot[:, q, :, :].rearrange("p k e -> p (k e)"),
                                  start=q == 0, stop=q == i)
            m.then_inc(s["cnt_ps"], 1)
            for n in range(4, 8):
                shared_hidden(n)
            pe.wait_ge(s["ids_ok"], 1)
            pe.wait_ge(s["bT_ok"], 2)
            for k in range(K):
                for i in range(TT):
                    m = pe.matmul(bank[4 + k][:, i * P:(i + 1) * P], ids[:, i, k:k + 1].to_broadcast([P, P]), ident[:, :], start=True, stop=True)
                m.then_inc(s["rows_ps"], 1)
            pe.wait_ge(w2_ld[1], 64)
            pe.wait_ge(s["sr_ok"], 1)
            shared_out(0)
            for n in range(8, FC):
                shared_hidden(n)
            shared_out(1)

            def gather(e):
                pe.wait_ge(s["sel_ok"], e + 1)
                for c in range(KC):
                    for i in range(TT):
                        for part in (xl, xh):
                            m = pe.matmul(t_ps[c // 2][:, c % 2 * SL:(c % 2 + 1) * SL], part[:, i, c * P:(c + 1) * P], sel[:, i, :],
                                          start=i == 0 and part is xl, stop=i == TT - 1 and part is xh)
                    if c % 2:
                        m.then_inc(s["g_ps"], 1)

            def turn(e):
                pe.wait_ge(s["y_ok"], e * 2 + 2)
                for k in range(K):
                    for c in range(KC):
                        m = pe.transpose(t_ps[k][0:CAP, c * P:(c + 1) * P], yT[:, c, k * CAP:(k + 1) * CAP], ident[:, :])
                    m.then_inc(s["yt_ps"], 1)

            def scatter(e, first):
                pe.wait_ge(s["comb_ok"], e + 1)
                pe.wait_ge(s["yt_lo"], e * K + K)
                for n in range(K * TT):
                    k, i = n // TT, n % TT
                    if not (first and n < 2):
                        pe.wait_ge(s["c_ok"], e * (K * TT) + (n - 1))
                    for part in (yl, yh):
                        m = pe.matmul(c_ps[n % 2][:, :], comb[:, k, i * P:(i + 1) * P], part[:, k, :], start=part is yl, stop=part is yh)
                    m.then_inc(s["c_ps"], 1)

            def expert(e, i, uses, before, last):
                first = before == 0
                pe.wait_ge(w1_ld[i], uses * 64)
                pe.wait_ge(s["g_ok"], e * 2 + 2)

                def layer1(n):
                    if not (first and n < 2):
                        pe.wait_ge(s["h_ok"], e * (FC // 2) + (n - 1))
                    for q in range(2):
                        fc = 2 * n + q
                        for c in range(KC):
                            m = pe.matmul(h_ps[n % 2][:, q * SL:(q + 1) * SL], w1[i][:, c, fc * P:(fc + 1) * P], bufT[:, c, :], start=c == 0, stop=c == KC - 1)
                    m.then_inc(s["h_ps"], 1)

                for n in range(4):
                    layer1(n)
                if not first:
                    turn(e - 1)
                for n in range(4, FC // 2):
                    layer1(n)
                pe.wait_ge(ad_ld[i], uses * 32)
                if before == 2:
                    pe.wait_ge(s["c_ok"], (e - 1) * (K * TT))
                for c in range(KC):
                    m = pe.matmul(bank[6][0:R, 0:SL], wd[i][:, c, :], bufT[:, c, :], start=c == 0, stop=c == KC - 1)
                m.then_inc(s["r_ps"], 1)
                pe.wait_ge(s["r_ok"], e + 1)
                if not first:
                    scatter(e - 1, before == 1)
                if not last:
                    gather(e + 1)
                pe.wait_ge(w2_ld[i], uses * 64)
                pe.wait_ge(s["h_ok"], e * (FC // 2) + FC // 2)
                for c in range(KC):
                    if c % 2 == 0 and not first:
                        pe.wait_ge(s["y_ok"], e * 2 + c // 2 - 1)
                    o = y_ps[c // 2][:, c % 2 * SL:(c % 2 + 1) * SL]
                    for n in range(FC):
                        pe.matmul(o, w2[i][:, n, c * P:(c + 1) * P], hT[:, n, :], start=n == 0, stop=False)
                    m = pe.matmul(o, wu[i][:, c * P:(c + 1) * P], rT[:, :], start=False, stop=True)
                    if c % 2:
                        m.then_inc(s["y_ps"], 1)

            pe.wait_ge(s["rows_ok"], K)
            gather(0)
            pe.wait_ge(s["so_ok"], 2 * TT)
            pe.wait_ge(s["sh_ok"], FC)
            expert(0, 0, 1, 0, False)
            expert(1, 1, 2, 1, False)
            with pe.Fori(0, (E - 4) // 2) as m:
                for q in range(2):
                    expert(m * 2 + (q + 2), q, m + (2 + q), 2, False)
            expert(E - 2, 0, E // 2, 2, False)
            expert(E - 1, 1, E // 2 + 1, 2, True)
            turn(E - 1)
            scatter(E - 1, False)


def perceiver(nc, a, out):
    q_dram = nc.dram_tensor("q_scratch", [H, HD, B * TQ], F32, kind="Internal").ap()
    with ExitStack() as ctx:
        t = Tensors(nc, ctx, "all")
        X = t.sb("X", [P, TT, D])
        ident = t.sb("ident", [P, P])
        queries(nc, a["x"], a["L0_xattn_Wq"], q_dram, X, ident)
        cross(nc, a["ctx_1024"], a["mask_BxS2_bf1"], a["L0_xattn_Wk"], a["L0_xattn_Wv"], a["L0_xattn_Wo"], q_dram, X, ident)
        selfattn(nc, a, X, ident)
        experts(nc, a, out, X, ident)


def kernel(**inputs):
    import numpy as _np
    import concourse.bacc as _bacc
    from concourse import mybir as _mybir
    from concourse.bass_utils import run_bass_kernel_spmd as _run

    nc = _bacc.Bacc("TRN2", target_bir_lowering=False, num_devices=1)
    arrays, args = {}, {}
    for name, value in inputs.items():
        a = _np.ascontiguousarray(value)
        if a.dtype == _np.bool_:
            a = a.view(_np.uint8)
        arrays[f"in_{name}"] = a
        args[name] = nc.dram_tensor(f"in_{name}", a.shape, _mybir.dt.from_np(a.dtype), kind="ExternalInput").ap()
    out = nc.dram_tensor("out_x", (B, TQ, D), _mybir.dt.float32, kind="ExternalOutput").ap()
    perceiver(nc, args, out)
    r = _run(nc, [arrays], core_ids=[0])
    return r.results[0]["out_x"]
```

```python
import concourse.bass as bass
from concourse import mybir
from contextlib import ExitStack

F32 = mybir.dt.float32
F32R = mybir.dt.float32r
BF16 = mybir.dt.bfloat16
U8 = mybir.dt.uint8
U32 = mybir.dt.uint32
ACT = mybir.ActivationFunctionType
ALU = mybir.AluOpType
AX = mybir.AxisListType

P = 128
BANK = 512
B, TQ, D = 2, 256, 512
TT = B * TQ // P
RT = TQ // P
KC = D // P
S, DC = 4096, 256
CC = DC // P
SCH = S // P
SB = S // BANK
H, HKV, HD = 16, 8, 128
GRP = H // HKV
EPS = 1e-5
NEG = -3.0e38


class Tensors:

    def __init__(self, nc, ctx, tag):
        self.nc, self.ctx, self.tag = nc, ctx, tag

    def sb(self, name, shape, dt=F32):
        return self.ctx.enter_context(self.nc.sbuf_tensor(f"{self.tag}_{name}", shape, dt))

    def ps(self, name, shape=(P, BANK), dt=F32):
        return self.ctx.enter_context(self.nc.psum_tensor(f"{self.tag}_{name}", list(shape), dt))

    def sem(self, name):
        return self.ctx.enter_context(self.nc.semaphore(f"{self.tag}_{name}"))


class Chain:

    def __init__(self, eng, sem):
        self.eng, self.sem, self.n = eng, sem, 0

    def link(self, ins):
        self.n += 1
        ins.then_inc(self.sem, 1)
        self.eng.wait_ge(self.sem, self.n)


def ln_scratch(t):
    return dict(stats=t.sb("ln_stats", [P, TT, 6]), mv=t.sb("ln_mv", [P, TT, 2]), root=t.sb("ln_root", [P, TT]),
                div=t.sb("ln_div", [P, TT]), rstd=t.sb("ln_rstd", [P, TT]), veps=t.sb("ln_veps", [P, TT]))


def ln_vector(v, ch, X, out, w, root_ready, var_ready):
    for i in range(TT):
        v.bn_stats(w["stats"][:, i, :], X[:, i, :]).then_inc(ch.sem, 1)
    ch.n += TT
    v.wait_ge(ch.sem, ch.n)
    for i in range(TT):
        v.bn_aggr(w["mv"][:, i, :], w["stats"][:, i, :]).then_inc(ch.sem, 1)
    ch.n += TT
    v.wait_ge(ch.sem, ch.n)
    v.tensor_scalar(w["veps"][:, :], w["mv"][:, :, 1], EPS, None, ALU.add).then_inc(var_ready, 1)
    v.wait_ge(root_ready, 1)
    ch.link(v.reciprocal(w["div"][:, :], w["root"][:, :]))
    ch.link(v.tensor_tensor(w["div"][:, :], w["div"][:, :], w["veps"][:, :], ALU.mult))
    ch.link(v.tensor_tensor(w["div"][:, :], w["div"][:, :], w["root"][:, :], ALU.add))
    ch.link(v.tensor_scalar(w["div"][:, :], w["div"][:, :], 0.5, None, ALU.mult))
    ch.link(v.reciprocal(w["rstd"][:, :], w["div"][:, :]))
    for i in range(TT):
        v.tensor_scalar(out[:, i, :], X[:, i, :], w["mv"][:, i, 0:1], w["rstd"][:, i:i + 1],
                        ALU.subtract, ALU.mult).then_inc(ch.sem, 1)
    ch.n += TT
    v.wait_ge(ch.sem, ch.n)


def context_piece(prob, ctx_in, b, n):
    k = BANK // P
    cin = prob[:, :, :].rearrange("p r s -> p (r s)").rearrange("p (n c) -> p n c", c=DC)
    return (cin[:, bass.ds(n * k, k), :],
            ctx_in[bass.ds(b, 1), bass.ds(n * BANK, BANK), :].rearrange("o (n p) c -> p (o n) c", p=P))


def queries(nc, x, wq, ctx_in, q_dram, X, ident, prob):
    SLOTS = 8
    QB = 4
    WB = 2
    with ExitStack() as ctx:
        t = Tensors(nc, ctx, "qry")
        ln = ln_scratch(t)
        xn = t.sb("xn", [P, TT, D])
        xh, xl = t.sb("xh", [P, KC, B * TQ], F32R), t.sb("xl", [P, KC, B * TQ], F32R)
        wq_sb = t.sb("wq", [P, SLOTS, KC, HD])
        wh, wl = ([t.sb(f"{n}{i}", [P, KC, HD], F32R) for i in range(WB)] for n in ("wh", "wl"))
        q_sb = t.sb("q", [P, QB, B * TQ])
        ps = [t.ps(f"ps{i}") for i in range(QB)]
        x_ld, ident_ok, var_ready, root_ready, xn_ready = (t.sem(n) for n in ("x_ld", "ident_ok", "var_ready", "root_ready", "xn_ready"))
        xT_ps, xT_hi, xT_lo, w_hi, w_lo, q_ps, q_done, chain, ctx_ld = (
            t.sem(n) for n in ("xT_ps", "xT_hi", "xT_lo", "w_hi", "w_lo", "q_ps", "q_done", "chain", "ctx_ld"))
        wq_ld = [t.sem(f"wq_ld{i}") for i in range(SLOTS)]
        q_out = [t.sem(f"q_out{i}") for i in range(QB)]
        block = ctx.enter_context(nc.Block())

        @block.sync
        def _(sp):
            for n in range(B):
                sp.dma_start(X[:, n * RT:(n + 1) * RT, :], x[n, :, :].rearrange("(r p) d -> p r d", p=P)).then_inc(x_ld, 16)
            with sp.Fori(0, H // SLOTS) as r:
                for i in range(SLOTS):
                    sp.wait_ge(w_lo, r * SLOTS + (i + 1))
                    sp.dma_start(wq_sb[:, i, :, :], wq[:, bass.ds((r * SLOTS + i) * HD, HD)].rearrange("(c p) n -> p c n", p=P)).then_inc(wq_ld[i], 16)
                for i in range(SB * SLOTS // H):
                    sp.dma_start(*context_piece(prob, ctx_in, 0, r * (SB * SLOTS // H) + i)).then_inc(ctx_ld, 16)
            sp.wait_ge(ctx_ld, SB * 16)

        @block.gpsimd
        def _(pool):
            nc.gpsimd.memset(ident[:, :], 0.0).then_inc(ident_ok, 1)
            pool.wait_ge(ident_ok, 1)
            nc.gpsimd.affine_select(out=ident[:, :], in_=ident[:, :], compare_op=ALU.not_equal, fill=1.0,
                                    base=0, pattern=[[-1, P]], channel_multiplier=1).then_inc(ident_ok, 1)

        @block.vector
        def _(v):
            ch = Chain(v, chain)
            v.sem_inc(w_lo, SLOTS)
            v.wait_ge(x_ld, B * 16)
            ln_vector(v, ch, X, xn, ln, root_ready, var_ready)
            v.engine_nop().then_inc(xn_ready, 1)
            for c in range(KC):
                v.wait_ge(xT_hi, c + 1)
                v.tensor_tensor(xl[:, c, :], ps[c][:, :], xh[:, c, :].bitcast(F32), ALU.subtract).then_inc(xT_lo, 1)
            with v.Fori(0, H // SLOTS) as r:
                for i in range(SLOTS):
                    v.wait_ge(w_hi, r * SLOTS + (i + 1))
                    v.tensor_tensor(wl[i % WB][:, :, :], wq_sb[:, i, :, :], wh[i % WB][:, :, :].bitcast(F32), ALU.subtract).then_inc(w_lo, 1)

        @block.scalar
        def _(act):
            act.wait_ge(var_ready, 1)
            act.activation(ln["root"][:, :], ln["veps"][:, :], ACT.Sqrt).then_inc(root_ready, 1)
            for c in range(KC):
                act.wait_ge(xT_ps, c + 1)
                act.activation(xh[:, c, :], ps[c][:, :], ACT.Copy).then_inc(xT_hi, 1)
            for i in range(QB):
                act.sem_inc(q_out[i], 16)
            act.sem_inc(q_done, QB)

            def weight_high(r, i):
                act.wait_ge(wq_ld[i], r * 16 + 16)
                act.wait_ge(q_ps, r * SLOTS + (i + 1))
                act.activation(wh[i % WB][:, :, :], wq_sb[:, i, :, :], ACT.Copy).then_inc(w_hi, 1)

            def query_out(head, r, i):
                act.wait_ge(q_ps, head + (WB + 1))
                act.wait_ge(q_out[i % QB], r * (SLOTS // QB * 16) + (i // QB + 1) * 16)
                act.activation(q_sb[:, i % QB, :], ps[i % QB][:, :], ACT.Copy, scale=HD ** -0.5).then_inc(q_done, 1)
                act.wait_ge(q_done, head + (QB + 1))
                act.dma_start(q_dram[bass.ds(head, 1), :, :].rearrange("o p n -> p (o n)"), q_sb[:, i % QB, :]).then_inc(q_out[i % QB], 16)

            weight_high(0, 0)
            with act.Fori(0, H // SLOTS - 1) as r:
                for i in range(SLOTS):
                    weight_high(r + (i + 1) // SLOTS, (i + 1) % SLOTS)
                    query_out(r * SLOTS + i, r, i)
            for i in range(SLOTS):
                r = H // SLOTS - 1
                if i + 1 < SLOTS:
                    weight_high(r, i + 1)
                query_out(r * SLOTS + i, r, i)
            for i in range(QB):
                act.wait_ge(q_out[i], (H // QB + 1) * 16)

        @block.tensor
        def _(pe):
            pe.sem_inc(q_ps, WB)
            pe.wait_ge(ident_ok, 2)
            pe.wait_ge(xn_ready, 1)
            for c in range(KC):
                for i in range(TT):
                    m = pe.transpose(ps[c][:, i * P:(i + 1) * P], xn[:, i, c * P:(c + 1) * P], ident[:, :])
                m.then_inc(xT_ps, 1)
            pe.wait_ge(xT_lo, KC)
            with pe.Fori(0, H // SLOTS) as r:
                for i in range(SLOTS):
                    pe.wait_ge(w_lo, r * SLOTS + (SLOTS + i + 1))
                    pe.wait_ge(q_done, r * SLOTS + (i + 1))
                    for n, (w, y, c) in enumerate((w, y, c) for w, y in ((wl, xh), (wh, xl), (wh, xh)) for c in range(KC)):
                        m = pe.matmul(ps[i % QB][:, :], w[i % WB][:, c, :], y[:, c, :], start=n == 0, stop=n == 3 * KC - 1)
                    m.then_inc(q_ps, 1)


def cross(nc, ctx_in, mask, wk, wv, wo, q_dram, X, ident, prob):
    RING = 4
    HEAD_ITEMS = CC * SB
    K_AT, V_AT = 0, SB + RT * SB
    QK_AT = (SB, V_AT + 2 * SB)
    GROUP_ITEMS = QK_AT[1] + RT * SB
    BATCH_ITEMS = HEAD_ITEMS + HKV * GROUP_ITEMS
    HIGHS = 2 * SB
    BATCH_HIGHS = HEAD_ITEMS + HKV * HIGHS
    STEPS = SCH // 2
    PARTS = 4
    PIECES = RT * PARTS
    PART = S // PARTS
    EARLY = 4
    SPLIT_AT = STEPS // 2
    BLOCKS = [r * PARTS + p for p in range(PARTS) for r in range(RT)]
    PROJECT_AT = (2, 4)
    MASKS = 4
    LAG = 2
    PT = LAG + 1
    with ExitStack() as ctx:
        t = Tensors(nc, ctx, "crs")
        ctxh, ctxl = t.sb("ctxh", [P, CC, S], F32R), t.sb("ctxl", [P, CC, S], F32R)
        kh, kl = t.sb("kh", [P, S], F32R), t.sb("kl", [P, S], F32R)
        vh, vl = t.sb("vh", [P, SCH, HD], F32R), t.sb("vl", [P, SCH, HD], F32R)
        maskb = t.sb("maskb", [P, S], BF16)
        qf = t.sb("qf", [P, GRP, TQ])
        qh, ql = t.sb("qh", [P, GRP, TQ], F32R), t.sb("ql", [P, GRP, TQ], F32R)
        wf = t.sb("wf", [P, 2, CC, HD])
        wh, wl = t.sb("wh", [P, 2, CC, HD], F32R), t.sb("wl", [P, 2, CC, HD], F32R)
        wo_sb = t.sb("wo", [P, GRP, D])
        pth, ptl = t.sb("pth", [P, PT, BANK], F32R), t.sb("ptl", [P, PT, BANK], F32R)
        oT = t.sb("oT", [P, GRP, TQ])
        mx = t.sb("mx", [P, RT, SB])
        nmax = t.sb("nmax", [P, RT])
        rs = t.sb("rs", [P, GRP, RT, PARTS])
        rinv = t.sb("rinv", [P, RT])
        anyp, anyv = t.sb("anyp", [P, SB]), t.sb("anyv", [P, 1])
        cin = prob[:, :, :].rearrange("p r s -> p (r s)").rearrange("p (n c) -> p n c", c=DC)
        mask_u8 = wo_sb[:, :, :].rearrange("p h d -> p (h d)").bitcast(U8)
        vT = (qf[:, :, :].rearrange("p h n -> p (h n)"), wf[:, :, :, :].rearrange("p w c n -> p (w c n)"))

        ring = [t.ps(f"ring{i}") for i in range(RING)]
        tp = [t.ps(f"tp{i}") for i in range(2)]
        ov, op = t.ps("ov"), t.ps("op")

        names = ("mask_ld", "q_ld", "w_ld", "wo0_ld", "wo1_ld", "ring_full", "ring_free", "hi_ok", "q_hi", "q_lo", "w_hi", "w_lo",
                 "max_ready", "p_ready", "pt_full", "pt_hi", "pt_lo", "pv_done", "ot_ready", "op_full", "op_free", "mask_ok", "inv_chain", "any_chain", "scores_seen")
        s = {n: t.sem(n) for n in names}
        ctx_ld = [t.sem(f"ctx_ld{i}") for i in range(PARTS)]
        wo_ld = (s["wo0_ld"], s["wo1_ld"])
        block = ctx.enter_context(nc.Block())

        def items(b, j):
            return b * BATCH_ITEMS + j * GROUP_ITEMS + HEAD_ITEMS

        def highs(b, j):
            return b * BATCH_HIGHS + j * HIGHS + HEAD_ITEMS

        def group(b, j):
            return b * HKV + j

        def vt_item(n):
            return V_AT + (2 * n - 1 if n else 0)

        def v_item(n):
            return V_AT + min(2 * n + 2, 2 * SB - 1)

        @block.sync
        def _(sp):
            def weight_loads(j):
                for w, src in enumerate((wk, wv)):
                    sp.dma_start(wf[:, w, :, :], src[:, bass.ds(j * HD, HD)].rearrange("(c p) n -> p c n", p=P)).then_inc(s["w_ld"], 16)

            def v_gone(b, j):
                sp.wait_ge(s["ring_full"], items(b, j) + QK_AT[1])

            def group_loads(b, j, first):
                g = group(b, j)
                sp.dma_start(qf[:, :, :], q_dram[bass.ds(j * GRP, GRP), :, bass.ds(b * TQ, TQ)].rearrange("h p n -> p h n")).then_inc(s["q_ld"], 16)
                for h in range(GRP):
                    if not first:
                        sp.wait_ge(s["op_full"], g * (GRP * RT) - (GRP - 1 - h) * RT)
                    elif h == 0:
                        sp.wait_ge(s["mask_ok"], (b + 1) * MASKS)
                    sp.dma_start(wo_sb[:, h, :], wo[bass.ds((j * GRP + h) * HD, HD), :]).then_inc(wo_ld[h], 16)

            weight_loads(0)
            for b in range(B):
                for p in range(PARTS):
                    if b == 0:
                        sp.sem_inc(ctx_ld[p], RT * 16)
                        continue
                    sp.wait_ge(s["pt_full"], (b * HKV * GRP - 1) * STEPS + (p + 1) * (STEPS // PARTS))
                    for r in range(RT):
                        sp.dma_start(*context_piece(prob, ctx_in, b, r * PARTS + p)).then_inc(ctx_ld[p], 16)
                if b:
                    sp.wait_ge(s["op_full"], b * (HKV * GRP * RT))
                sp.dma_start(mask_u8, mask[bass.ds(b, 1), :].to_broadcast([P, S])).then_inc(s["mask_ld"], 16)
                group_loads(b, 0, True)
                with sp.Fori(1, HKV) as j:
                    v_gone(b, j - 1)
                    weight_loads(j)
                    group_loads(b, j, False)
                if b < B - 1:
                    v_gone(b, HKV - 1)
                    weight_loads(0)

        @block.gpsimd
        def _(pool):
            for b in range(B):
                pool.wait_ge(s["mask_ld"], b * 16 + 16)
                for n in range(MASKS):
                    w = slice(n * S // MASKS, (n + 1) * S // MASKS)
                    nc.gpsimd.tensor_scalar(maskb[:, w], mask_u8[:, w], 1.0, -NEG, ALU.subtract, ALU.mult).then_inc(s["mask_ok"], 1)

        @block.scalar
        def _(act):
            def exp_piece(u, h, i):
                act.wait_ge(s["max_ready"], u + 1)
                p, r = i // RT, i % RT
                w = prob[:, r, p * PART:(p + 1) * PART]
                act.activation(w, w, ACT.Exp, bias=nmax[:, r:r + 1], accum_out=rs[:, h, r, p:p + 1]).then_inc(s["p_ready"], 1)

            def pt_high(u, k):
                act.wait_ge(s["pt_full"], u * STEPS + (k + 1))
                if k >= PT:
                    act.wait_ge(s["pv_done"], u * STEPS + (k - PT + 1))
                act.activation(pth[:, k % PT, :], tp[k % 2][:, :], ACT.Copy).then_inc(s["pt_hi"], 1)

            def o_out(u, h):
                act.wait_ge(s["pv_done"], u * STEPS + STEPS)
                act.activation(oT[:, h, :], ov[:, 0:TQ], ACT.Copy).then_inc(s["ot_ready"], 1)

            def high(R, at, out):
                act.wait_ge(s["ring_full"], R + (at + 1))
                act.activation(out, ring[at % RING][:, :], ACT.Copy).then_inc(s["hi_ok"], 1)

            def weights_high(g):
                act.wait_ge(s["w_ld"], g * 32 + 32)
                act.activation(wh[:, :, :, :], wf[:, :, :, :], ACT.Copy).then_inc(s["w_hi"], 1)

            def group_work(b, j, first, last=False):
                g, R = group(b, j), items(b, j)
                act.wait_ge(s["q_ld"], g * 16 + 16)
                act.wait_ge(s["ring_full"], R)
                act.activation(qh[:, :, :], qf[:, :, :], ACT.Copy).then_inc(s["q_hi"], 1)
                for h in range(GRP):
                    u = g * GRP + (h - 1)
                    prev = h == 1 or not first
                    for n in range(SB):
                        if prev and n < EARLY:
                            exp_piece(u, (h + 1) % 2, n)
                        high(R, K_AT + n if h == 0 else v_item(n),
                             kh[:, n * BANK:(n + 1) * BANK] if h == 0 else vh[:, n * 4:(n + 1) * 4, :])
                    for k in range(STEPS):
                        if prev:
                            pt_high(u, k)
                            if k < 2 * (PIECES - EARLY) and k % 2:
                                exp_piece(u, (h + 1) % 2, EARLY + k // 2)
                            if h == 1 and k == SPLIT_AT and not last:
                                weights_high(g + 1)
                    if prev:
                        o_out(u, (h + 1) % 2)

            act.sem_inc(s["ot_ready"], 1)
            weights_high(0)
            for b in range(B):
                for i in range(HEAD_ITEMS):
                    n = BLOCKS[i // CC]
                    high(b * BATCH_ITEMS, i, ctxh[:, i % CC, n * BANK:(n + 1) * BANK])
                group_work(b, 0, True)
                with act.Fori(1, HKV - (b == B - 1)) as j:
                    group_work(b, j, False)
                if b == B - 1:
                    group_work(b, HKV - 1, False, last=True)
                u = b * (HKV * GRP) + (HKV * GRP - 1)
                for i in range(RT):
                    exp_piece(u, 1, i)
                for k in range(STEPS):
                    pt_high(u, k)
                    if RT + k < PIECES:
                        exp_piece(u, 1, RT + k)
                o_out(u, 1)

        @block.vector
        def _(v):
            def low(at, count, out, high):
                v.wait_ge(s["hi_ok"], count)
                v.tensor_tensor(out, ring[at % RING][:, :], high.bitcast(F32), ALU.subtract).then_inc(s["ring_free"], 1)

            def scores_out(R, at, k, u):
                r, c = k % RT, k // RT
                v.wait_ge(s["ring_full"], R + (at + 1))
                v.sem_inc(s["scores_seen"], 1)
                v.tensor_tensor_reduce(prob[:, r, c * BANK:(c + 1) * BANK], ring[at % RING][:, :], maskb[:, c * BANK:(c + 1) * BANK],
                                       op0=ALU.add, op1=ALU.max, scale=1.0, scalar=NEG, accum_out=mx[:, r, c:c + 1]).then_inc(s["ring_free"], 1)
                if k == STEPS - 1:
                    v.wait_ge(s["ring_free"], R + (at + 1))
                    v.tensor_reduce(nmax[:, :], mx[:, :, :], op=ALU.max, axis=AX.X, negate=True).then_inc(s["max_ready"], 1)

            def pt_low(u, k):
                v.wait_ge(s["pt_hi"], u * STEPS + (k + 1))
                v.tensor_tensor(ptl[:, k % PT, :], tp[k % 2][:, :], pth[:, k % PT, :].bitcast(F32), ALU.subtract).then_inc(s["pt_lo"], 1)

            def inverse(u, h):
                v.wait_ge(s["p_ready"], u * PIECES + PIECES)
                v.tensor_reduce(rinv[:, :], rs[:, h, :, :], op=ALU.add, axis=AX.X).then_inc(s["inv_chain"], 1)
                v.wait_ge(s["inv_chain"], u * 3 + 1)
                v.reciprocal(rinv[:, :], rinv[:, :]).then_inc(s["inv_chain"], 1)
                v.wait_ge(s["inv_chain"], u * 3 + 2)
                v.tensor_scalar(rinv[:, :], rinv[:, :], anyv[:, 0:1], None, ALU.mult).then_inc(s["inv_chain"], 1)
                v.wait_ge(s["inv_chain"], u * 3 + 3)

            def residual(b, u, r):
                v.wait_ge(s["op_full"], u * RT + (r + 1))
                w = X[:, bass.ds(b * RT + r, 1), :].rearrange("p o d -> p (o d)")
                v.scalar_tensor_tensor(w, op[:, :], rinv[:, r:r + 1], w, ALU.mult, ALU.add).then_inc(s["op_free"], 1)

            def any_part(b, n):
                v.tensor_reduce(anyp[:, n:n + 1], maskb[:, n * BANK:(n + 1) * BANK], op=ALU.max, axis=AX.X).then_inc(s["any_chain"], 1)

            def any_valid(b):
                v.wait_ge(s["any_chain"], b * (SB + 2) + SB)
                v.tensor_reduce(anyv[:, :], anyp[:, :], op=ALU.max, axis=AX.X).then_inc(s["any_chain"], 1)
                v.wait_ge(s["any_chain"], b * (SB + 2) + SB + 1)
                v.tensor_scalar(anyv[:, :], anyv[:, :], 0.0, None, ALU.is_ge).then_inc(s["any_chain"], 1)
                v.wait_ge(s["any_chain"], b * (SB + 2) + SB + 2)

            def vt_out(R, n):
                v.wait_ge(s["ring_full"], R + (vt_item(n) + 1))
                v.tensor_copy(vT[n % 2], ring[vt_item(n) % RING][:, :]).then_inc(s["ring_free"], 1)

            def v_low(b, j, n):
                low(v_item(n), highs(b, j) + (SB + n + 1), vl[:, n * 4:(n + 1) * 4, :].rearrange("p a b -> p (a b)"),
                    vh[:, n * 4:(n + 1) * 4, :].rearrange("p a b -> p (a b)"))

            def weights_low(g):
                v.wait_ge(s["w_hi"], g + 1)
                v.tensor_tensor(wl[:, :, :, :], wf[:, :, :, :], wh[:, :, :, :].bitcast(F32), ALU.subtract).then_inc(s["w_lo"], 1)

            def group_work(b, j, first, last=False):
                g, R = group(b, j), items(b, j)
                v.wait_ge(s["q_hi"], g + 1)
                v.tensor_tensor(ql[:, :, :], qf[:, :, :], qh[:, :, :].bitcast(F32), ALU.subtract).then_inc(s["q_lo"], 1)
                for h in range(GRP):
                    prev = h == 1 or not first
                    u = g * GRP + (h - 1)
                    done = g * GRP + (h - 2)
                    for n in range(SB):
                        if h == 0:
                            low(K_AT + n, highs(b, j) + (n + 1), kl[:, n * BANK:(n + 1) * BANK], kh[:, n * BANK:(n + 1) * BANK])
                        else:
                            vt_out(R, n)
                            if n >= 1:
                                v_low(b, j, n - 1)
                            if first:
                                any_part(b, n)
                        if not first:
                            if n == 0:
                                inverse(done, h)
                            if n in PROJECT_AT:
                                residual(b, done, PROJECT_AT.index(n))
                    if h == 1:
                        v_low(b, j, SB - 1)
                    if first and h == 1:
                        any_valid(b)
                    for k in range(STEPS):
                        if prev:
                            pt_low(u, k)
                        if h == 1 and k == SPLIT_AT and not last:
                            weights_low(g + 1)
                        if first and h == 0 and k >= 1 and (k - 1) % (STEPS // MASKS) == 0:
                            v.wait_ge(s["mask_ok"], b * MASKS + (k - 1) // (STEPS // MASKS) + 1)
                        if k >= 1:
                            scores_out(R, QK_AT[h] + k - 1, k - 1, g * GRP + h)
                    scores_out(R, QK_AT[h] + STEPS - 1, STEPS - 1, g * GRP + h)

            v.sem_inc(s["op_free"], 1)
            weights_low(0)
            for b in range(B):
                for i in range(HEAD_ITEMS):
                    n = BLOCKS[i // CC]
                    w = (slice(None), i % CC, slice(n * BANK, (n + 1) * BANK))
                    low(i, b * BATCH_HIGHS + (i + 1), ctxl[w], ctxh[w])
                group_work(b, 0, True)
                with v.Fori(1, HKV - (b == B - 1)) as j:
                    group_work(b, j, False)
                if b == B - 1:
                    group_work(b, HKV - 1, False, last=True)
                u = b * (HKV * GRP) + (HKV * GRP - 1)
                inverse(u - 1, 0)
                for r in range(RT):
                    residual(b, u - 1, r)
                for k in range(STEPS):
                    pt_low(u, k)
                inverse(u, 1)
                for r in range(RT):
                    residual(b, u, r)

        @block.tensor
        def _(pe):
            def project(g, u, h, r):
                if r == 0:
                    pe.wait_ge(s["ot_ready"], u + 2)
                    pe.wait_ge(wo_ld[h], g * 16 + 16)
                pe.wait_ge(s["op_free"], u * RT + (r + 1))
                pe.matmul(op[:, :], oT[:, h, r * P:(r + 1) * P], wo_sb[:, h, :], start=True, stop=True).then_inc(s["op_full"], 1)

            def free(R, at):
                pe.wait_ge(s["ring_free"], R + (at - RING + 1))

            def proj_item(R, at, w, n):
                free(R, at)
                cols = slice(n * BANK, (n + 1) * BANK)
                for i, (a, x, c) in enumerate((a, x, c) for a, x in ((wl, ctxh), (wh, ctxl), (wh, ctxh)) for c in range(CC)):
                    m = pe.matmul(ring[at % RING][:, :], a[:, w, c, :], x[:, c, cols], start=i == 0, stop=i == 3 * CC - 1)
                m.then_inc(s["ring_full"], 1)

            def turn_item(R, n):
                pe.wait_ge(s["ring_free"], R + (vt_item(n) + 1))
                free(R, v_item(n))
                for q in range(4):
                    m = pe.transpose(ring[v_item(n) % RING][:, q * P:(q + 1) * P], vT[n % 2][:, q * P:(q + 1) * P], ident[:, :])
                m.then_inc(s["ring_full"], 1)

            def score_item(R, h, k):
                r, c = k % RT, k // RT
                at = QK_AT[h] + k
                free(R, at)
                rows, cols = slice(r * P, (r + 1) * P), slice(c * BANK, (c + 1) * BANK)
                for n, (a, w) in enumerate(((ql, kh), (qh, kl), (qh, kh))):
                    m = pe.matmul(ring[at % RING][:, :], a[:, h, rows], w[:, cols], start=n == 0, stop=n == 2)
                m.then_inc(s["ring_full"], 1)

            def transposes(u, k):
                if 2 * k % (SCH // PARTS) == 0:
                    pe.wait_ge(s["p_ready"], u * PIECES + (2 * k // (SCH // PARTS) + 1) * RT)
                if k >= 2:
                    pe.wait_ge(s["pt_lo"], u * STEPS + (k - 1))
                for c in range(2):
                    for r in range(RT):
                        at = (c * RT + r) * P
                        m = pe.transpose(tp[k % 2][:, at:at + P], prob[:, r, (2 * k + c) * P:(2 * k + c + 1) * P], ident[:, :])
                m.then_inc(s["pt_full"], 1)

            def pv(u, k):
                pe.wait_ge(s["pt_lo"], u * STEPS + (k + 1))
                if k == 0:
                    pe.wait_ge(s["ot_ready"], u + 1)
                for c in range(2):
                    for n, (a, w) in enumerate(((vh, ptl), (vl, pth), (vh, pth))):
                        m = pe.matmul(ov[:, 0:TQ], a[:, 2 * k + c, :], w[:, k % PT, c * TQ:(c + 1) * TQ],
                                      start=k == 0 and c == 0 and n == 0, stop=k == STEPS - 1 and c == 1 and n == 2)
                m.then_inc(s["pv_done"], 1)

            def group_work(b, j, first):
                g, R = group(b, j), items(b, j)
                pe.wait_ge(s["w_lo"], g + 1)
                for h in range(GRP):
                    prev = h == 1 or not first
                    u, done = g * GRP + (h - 1), g * GRP + (h - 2)
                    for n in range(SB):
                        proj_item(R, vt_item(n) if h else K_AT + n, h, n)
                        if h == 1 and n >= 1:
                            turn_item(R, n - 1)
                        if not first and n in PROJECT_AT:
                            project(g - 1, done, h, PROJECT_AT.index(n))
                    if h == 1:
                        turn_item(R, SB - 1)
                    else:
                        pe.wait_ge(s["q_lo"], g + 1)
                    for k in range(STEPS):
                        if prev:
                            transposes(u, k)
                        score_item(R, h, k)
                        if prev and k >= LAG:
                            pv(u, k - LAG)
                    if prev:
                        for k in range(STEPS - LAG, STEPS):
                            pv(u, k)

            with pe.Fori(0, B) as b:
                for i in range(HEAD_ITEMS):
                    n = BLOCKS[i // CC]
                    if i % (CC * RT) == 0:
                        pe.wait_ge(ctx_ld[i // (CC * RT)], (b + 1) * (RT * 16))
                    if i >= RING:
                        pe.wait_ge(s["ring_free"], b * BATCH_ITEMS + (i - RING + 1))
                    for q in range(4):
                        m = pe.transpose(ring[i % RING][:, q * P:(q + 1) * P], cin[:, n * 4 + q, i % CC * P:(i % CC + 1) * P], ident[:, :])
                    m.then_inc(s["ring_full"], 1)
                group_work(b, 0, True)
                with pe.Fori(1, HKV) as j:
                    group_work(b, j, False)
                g = b * HKV + (HKV - 1)
                u = g * GRP + 1
                for r in range(RT):
                    project(g, u - 1, 0, r)
                for k in range(STEPS + LAG):
                    if k < STEPS:
                        transposes(u, k)
                    if k >= LAG:
                        pv(u, k - LAG)
                for r in range(RT):
                    project(g, u, 1, r)


def selfattn(nc, a, X, ident):
    HN, HW = 16, 32
    HC = P // HW
    N = B * KC
    with ExitStack() as ctx:
        t = Tensors(nc, ctx, "att")
        ln = ln_scratch(t)
        xn = t.sb("xn", [P, TT, D])
        xnT = t.sb("xnT", [P, KC, B * TQ])
        w_raw = [t.sb(f"w{i}", [P, KC, D]) for i in range(4)]
        wT = [t.sb(f"wT{i}", [P, KC, D]) for i in range(4)]
        bias_rows = t.sb("bias_rows", [2 * KC, P])
        bias_cols = t.sb("bias_cols", [P, 2 * KC])
        vo_rows = t.sb("vo_rows", [1, 2, D])
        ones = t.sb("ones", [1, P])
        qT = t.sb("qT", [P, N, TQ])
        kT = t.sb("kT", [P, N, TQ])
        V = t.sb("V", [P, N, RT, P])
        headmask = t.sb("headmask", [P, HC])
        decay = t.sb("decay", [P, RT, TQ])
        kz = [t.sb(f"kz{i}", [P, HC, P]) for i in range(2)]
        sc = [t.sb(f"sc{i}", [P, HC, TQ]) for i in range(2)]
        nmax = [t.sb(f"nmax{i}", [P, HC]) for i in range(2)]
        rsum = [t.sb(f"rsum{i}", [P, HC]) for i in range(2)]
        cT = t.sb("cT", [P, HC * RT, P])
        O = t.sb("O", [P, RT, N, P])
        oT = t.sb("oT", [P, KC, B * TQ])
        bank = [t.ps(f"bank{i}") for i in range(8)]
        s_ps = [bank[0:2], bank[2:4]]
        t_ps, o_ps = bank[4:6], bank[6:8]
        names = ("var_ready", "root_ready", "xn_ready", "chain", "consts", "b_ld", "xT_ps", "xT_ok", "wT_ps", "wT_act", "wT_dve",
                 "bias_ps", "bias_ok", "q_ps", "q_ok", "k_ps", "k_ok", "v_ps", "v_ok", "kz_ok", "s_ps", "s_ok", "exp_ok",
                 "t_ps", "t_act", "t_dve", "o_ps", "o_ok", "inv", "oT_ps", "oT_ok", "out_ps", "out_ok")
        s = {n: t.sem(n) for n in names}
        w_ld = [t.sem(f"w_ld{i}") for i in range(4)]
        block = ctx.enter_context(nc.Block())
        wnames = ("q", "k", "v", "o")

        def bank_of(h, it):
            return (0, h * P, P) if it == 0 else (h // 2, h % 2 * TQ, TQ)

        @block.sync
        def _(sp):
            for i, n in enumerate(wnames):
                sp.dma_start(w_raw[i][:, :, :], a[f"L0_attn_{n}_w"].rearrange("(c p) n -> p c n", p=P)).then_inc(w_ld[i], 16)
            for i, n in enumerate(("q", "k")):
                sp.dma_start(bias_rows[i * KC:(i + 1) * KC, :], a[f"L0_attn_{n}_b"].rearrange("(c p) -> c p", p=P)).then_inc(s["b_ld"], 16)
            for i, n in enumerate(("v", "o")):
                sp.dma_start(vo_rows[:, i, :], a[f"L0_attn_{n}_b"].rearrange("(o d) -> o d", o=1)).then_inc(s["b_ld"], 16)

        @block.gpsimd
        def _(pool):
            c = s["consts"]
            nc.gpsimd.memset(ones[:, :], 1.0).then_inc(c, 1)
            nc.gpsimd.memset(headmask[:, :], 1.0).then_inc(c, 1)
            nc.gpsimd.iota(decay[:, :, :], pattern=[[-P, RT], [1, TQ]], base=0, channel_multiplier=-1, allow_small_or_imprecise_dtypes=True).then_inc(c, 1)
            pool.wait_ge(c, 3)
            nc.gpsimd.affine_select(out=headmask[:, :], in_=headmask[:, :], compare_op=ALU.is_ge, fill=0.0,
                                    base=0, pattern=[[-HW, HC]], channel_multiplier=1).then_inc(c, 1)
            pool.wait_ge(c, 4)
            nc.gpsimd.affine_select(out=headmask[:, :], in_=headmask[:, :], compare_op=ALU.is_ge, fill=0.0,
                                    base=HW - 1, pattern=[[HW, HC]], channel_multiplier=-1).then_inc(c, 1)
            nc.gpsimd.affine_select(out=decay[:, :, :], in_=decay[:, :, :], compare_op=ALU.is_ge, fill=NEG,
                                    base=0, pattern=[[P, RT], [-1, TQ]], channel_multiplier=1).then_inc(c, 1)

        @block.vector
        def _(v):
            ch = Chain(v, s["chain"])
            def weight(i):
                v.wait_ge(s["wT_ps"], i + 1)
                v.tensor_copy(wT[i // KC][:, i % KC, :], bank[i % 4][:, :]).then_inc(s["wT_dve"], 1)

            ln_vector(v, ch, X, xn, ln, s["root_ready"], s["var_ready"])
            v.engine_nop().then_inc(s["xn_ready"], 1)
            for i in range(1, 4 * KC, 2):
                weight(i)
            v.wait_ge(s["bias_ps"], 1)
            v.tensor_copy(bias_cols[:, :], bank[4][:, 0:2 * KC]).then_inc(s["bias_ok"], 1)
            for c in range(KC):
                v.wait_ge(s["xT_ps"], c + 1)
                v.tensor_copy(xnT[:, c, :], bank[4 + c][:, :]).then_inc(s["xT_ok"], 1)
            v.wait_ge(s["bias_ok"], 1)
            for c in range(KC):
                v.wait_ge(s["q_ps"], c + 1)
                v.tensor_scalar(qT.rearrange("p (b c) n -> p c b n", b=B)[:, c], bank[c][:, :].rearrange("p (b n) -> p b n", b=B),
                                bias_cols[:, c:c + 1], HW ** -0.5, ALU.add, ALU.mult).then_inc(s["q_ok"], 1)
            for i in range(TT):
                v.wait_ge(s["v_ps"], i + 1)
                v.tensor_copy(V.rearrange("p (b c) r n -> p b r c n", b=B)[:, i // RT, i % RT], bank[i][:, :].rearrange("p (c n) -> p c n", c=KC)).then_inc(s["v_ok"], 1)
            v.wait_ge(s["consts"], 6)
            v.wait_ge(s["k_ok"], KC)
            v.sem_inc(s["o_ok"], 2)

            def keys(it, n, par):
                v.tensor_tensor(kz[par][:, :, :], kT[:, bass.ds(n, 1), it * P:(it + 1) * P].to_broadcast([P, HC, P]),
                                headmask[:, :].unsqueeze(2).to_broadcast([P, HC, P]), ALU.mult).then_inc(s["kz_ok"], 1)

            def scores(it, n, par):
                u, J = n + it * N, (it + 1) * P
                v.wait_ge(s["s_ps"], u + 1)
                if it == 0:
                    v.tensor_tensor(sc[par][:, :, 0:J], s_ps[par][0][:, :].rearrange("p (h j) -> p h j", h=HC),
                                    decay[:, 0:1, 0:J].to_broadcast([P, HC, J]), ALU.add).then_inc(s["s_ok"], 2)
                else:
                    for q in range(2):
                        v.tensor_tensor(sc[par][:, 2 * q:2 * q + 2, :], s_ps[par][q][:, :].rearrange("p (h j) -> p h j", h=2),
                                        decay[:, 1:2, :].to_broadcast([P, 2, TQ]), ALU.add).then_inc(s["s_ok"], 1)
                v.wait_ge(s["s_ok"], u * 3 + 2)
                v.tensor_reduce(nmax[par][:, :], sc[par][:, :, 0:J], op=ALU.max, axis=AX.X, negate=True).then_inc(s["s_ok"], 1)

            def outputs(it, n, par):
                u = n + it * N
                if it == 1:
                    v.wait_ge(s["t_ps"], u * RT + 2)
                    v.tensor_copy(cT[:, HC:2 * HC, :].rearrange("p a b -> p (a b)"), t_ps[1][:, :]).then_inc(s["t_dve"], 1)
                v.wait_ge(s["exp_ok"], u * HC + HC)
                v.reciprocal(rsum[par][:, :], rsum[par][:, :]).then_inc(s["inv"], 1)
                v.wait_ge(s["inv"], u + 1)
                v.wait_ge(s["o_ps"], u + 1)
                v.tensor_tensor(O[:, it, bass.ds(n, 1), :].rearrange("p o (h w) -> p (o h) w", h=HC), o_ps[par][:, 0:P].rearrange("p (h w) -> p h w", h=HC),
                                rsum[par][:, :].unsqueeze(2).to_broadcast([P, HC, HW]), ALU.mult).then_inc(s["o_ok"], 1)

            for it in range(RT):
                keys(it, 0, 0)
                keys(it, 1, 1)
                scores(it, 0, 0)
                with v.Fori(0, (N - 2) // 2) as m:
                    for q in range(2):
                        n = m * 2 + q
                        scores(it, n + 1, (q + 1) % 2)
                        keys(it, n + 2, q)
                        outputs(it, n, q)
                scores(it, N - 1, 1)
                outputs(it, N - 2, 0)
                outputs(it, N - 1, 1)
            v.wait_ge(s["o_ok"], N * RT + 2)
            for c in range(KC):
                v.wait_ge(s["oT_ps"], c + 1)
                v.tensor_copy(oT[:, c, :], bank[c][:, :]).then_inc(s["oT_ok"], 1)
            for i in range(TT):
                v.wait_ge(s["out_ps"], i + 1)
                v.tensor_tensor(X[:, i, :], X[:, i, :], bank[4 + i][:, :], ALU.add).then_inc(s["out_ok"], 1)

        @block.scalar
        def _(act):
            act.wait_ge(s["var_ready"], 1)
            act.activation(ln["root"][:, :], ln["veps"][:, :], ACT.Sqrt).then_inc(s["root_ready"], 1)
            for i in range(0, 4 * KC, 2):
                act.wait_ge(s["wT_ps"], i + 1)
                act.activation(wT[i // KC][:, i % KC, :], bank[i % 4][:, :], ACT.Copy).then_inc(s["wT_act"], 1)
            act.wait_ge(s["bias_ok"], 1)
            for c in range(KC):
                act.wait_ge(s["k_ps"], c + 1)
                act.activation(kT.rearrange("p (b c) n -> p c b n", b=B)[:, c], bank[4 + c][:, :].rearrange("p (b n) -> p b n", b=B),
                               ACT.Identity, bias=bias_cols[:, KC + c:KC + c + 1]).then_inc(s["k_ok"], 1)

            def softmax(it, n, par):
                u, J = n + it * N, (it + 1) * P
                act.wait_ge(s["s_ok"], u * 3 + 3)
                for h in range(HC):
                    w = sc[par][:, h, 0:J]
                    act.activation(w, w, ACT.Exp, bias=nmax[par][:, h:h + 1], accum_out=rsum[par][:, h:h + 1]).then_inc(s["exp_ok"], 1)

            def turned(it, n):
                u = n + it * N
                act.wait_ge(s["t_ps"], u * RT + 1)
                act.activation(cT[:, 0:HC, :].rearrange("p a b -> p (a b)"), t_ps[0][:, :], ACT.Copy).then_inc(s["t_act"], 1)

            for it in range(RT):
                softmax(it, 0, 0)
                with act.Fori(0, (N - 2) // 2) as m:
                    for q in range(2):
                        n = m * 2 + q
                        turned(it, n)
                        softmax(it, n + 1, (q + 1) % 2)
                turned(it, N - 2)
                softmax(it, N - 1, 1)
                turned(it, N - 1)

        @block.tensor
        def _(pe):
            for i in range(4 * KC):
                w, c = i // KC, i % KC
                if c == 0:
                    pe.wait_ge(w_ld[w], 16)
                if i >= 4:
                    pe.wait_ge(s["wT_dve" if i % 2 else "wT_act"], (i - 4) // 2 + 1)
                for o in range(KC):
                    m = pe.transpose(bank[i % 4][:, o * P:(o + 1) * P], w_raw[w][:, o, c * P:(c + 1) * P], ident[:, :])
                m.then_inc(s["wT_ps"], 1)
            pe.wait_ge(s["b_ld"], 64)
            pe.matmul(bank[4][:, 0:2 * KC], bias_rows[:, :], ident[0:2 * KC, 0:2 * KC], start=True, stop=True).then_inc(s["bias_ps"], 1)
            pe.wait_ge(s["xn_ready"], 1)
            pe.wait_ge(s["bias_ok"], 1)
            for c in range(KC):
                for i in range(TT):
                    m = pe.transpose(bank[4 + c][:, i * P:(i + 1) * P], xn[:, i, c * P:(c + 1) * P], ident[:, :])
                m.then_inc(s["xT_ps"], 1)
            pe.wait_ge(s["xT_ok"], KC)
            pe.wait_ge(s["wT_act"], 2 * KC)
            pe.wait_ge(s["wT_dve"], 2 * KC)
            for base, w, done in ((0, 0, "q_ps"), (4, 1, "k_ps")):
                for o in range(KC):
                    for c in range(KC):
                        m = pe.matmul(bank[base + o][:, :], wT[w][:, c, o * P:(o + 1) * P], xnT[:, c, :], start=c == 0, stop=c == KC - 1)
                    m.then_inc(s[done], 1)
            pe.wait_ge(s["consts"], 6)
            for i in range(TT):
                pe.wait_ge(s["q_ok"], i + 1)
                for c in range(KC):
                    pe.matmul(bank[i][:, :], xnT[:, c, i * P:(i + 1) * P], wT[2][:, c, :], start=c == 0, stop=False)
                pe.matmul(bank[i][:, :], ones[:, :], vo_rows[:, 0, :], start=False, stop=True).then_inc(s["v_ps"], 1)
            pe.wait_ge(s["k_ok"], KC)
            pe.wait_ge(s["v_ok"], TT)

            def scores(it, n, par):
                u, J = n + it * N, (it + 1) * P
                pe.wait_ge(s["kz_ok"], u + 1)
                for h in range(HC):
                    k, at, w = bank_of(h, it)
                    m = pe.matmul(s_ps[par][k][:, at:at + w], kz[par][:, h, :], qT[:, bass.ds(n, 1), 0:J].rearrange("p o j -> p (o j)"), start=True, stop=True)
                m.then_inc(s["s_ps"], 1)

            def attend(it, n, par):
                u = n + it * N
                pe.wait_ge(s["exp_ok"], u * HC + HC)
                for j in range(it + 1):
                    for h in range(HC):
                        m = pe.transpose(t_ps[j][:, h * P:(h + 1) * P], sc[par][:, h, j * P:(j + 1) * P], ident[:, :])
                    m.then_inc(s["t_ps"], RT - it)
                pe.wait_ge(s["t_act"], u + 1)
                if it == 1:
                    pe.wait_ge(s["t_dve"], n + 1)
                pe.wait_ge(s["o_ok"], u + 1)
                for h in range(HC):
                    for j in range(it + 1):
                        m = pe.matmul(o_ps[par][:, h * HW:(h + 1) * HW], cT[:, j * HC + h, :],
                                      V[:, bass.ds(n, 1), j, h * HW:(h + 1) * HW].rearrange("p o w -> p (o w)"), start=j == 0, stop=j == it)
                m.then_inc(s["o_ps"], 1)

            for it in range(RT):
                scores(it, 0, 0)
                with pe.Fori(0, (N - 2) // 2) as m:
                    for q in range(2):
                        n = m * 2 + q
                        scores(it, n + 1, (q + 1) % 2)
                        attend(it, n, q)
                scores(it, N - 1, 1)
                attend(it, N - 2, 0)
                attend(it, N - 1, 1)
            pe.wait_ge(s["o_ok"], N * RT + 2)
            for c in range(KC):
                for i in range(TT):
                    m = pe.transpose(bank[c][:, i * P:(i + 1) * P], O[:, i % RT, i // RT * KC + c, :], ident[:, :])
                m.then_inc(s["oT_ps"], 1)
            pe.wait_ge(s["oT_ok"], KC)
            for i in range(TT):
                for c in range(KC):
                    pe.matmul(bank[4 + i][:, :], oT[:, c, i * P:(i + 1) * P], wT[3][:, c, :], start=c == 0, stop=False)
                pe.matmul(bank[4 + i][:, :], ones[:, :], vo_rows[:, 1, :], start=False, stop=True).then_inc(s["out_ps"], 1)


def experts(nc, a, out, X, ident):
    E, K = 8, 2
    CAP = int(B * TQ * 1.25 / E)
    SL = K * CAP
    F = 4 * D
    FC = F // P
    R = 32
    STRIDE = 1024
    LOWEST = -87.5
    with ExitStack() as ctx:
        t = Tensors(nc, ctx, "moe")
        w1 = [t.sb(f"w1_{i}", [P, KC, F]) for i in range(2)]
        w2 = [t.sb(f"w2_{i}", [P, FC, D]) for i in range(2)]
        wd = [t.sb(f"wd_{i}", [P, KC, R]) for i in range(2)]
        wu = [t.sb(f"wu_{i}", [R, D]) for i in range(2)]
        gate = t.sb("gate", [P, KC, E])
        xh, xl = t.sb("xh", [P, TT, D], F32R), t.sb("xl", [P, TT, D], F32R)
        sb2_row = t.sb("sb2_row", [1, D])
        b1_cols, b_cols = t.sb("b1_cols", [P, P]), t.sb("b_cols", [P, P])
        ones = t.sb("ones", [1, P])
        prob = t.sb("prob", [P, TT, E])
        lg = t.sb("lg", [P, TT, E])
        small = t.sb("small", [P, TT])
        top, topp = t.sb("top", [P, TT, 8]), t.sb("topp", [P, TT, 8])
        topi, topf = t.sb("topi", [P, TT, 8], U32), t.sb("topf", [P, TT, 8])
        onehot = t.sb("onehot", [P, TT, K, E])
        cnt = t.sb("cnt", [P, TT, K, E])
        ids = t.sb("ids", [P, TT, K])
        tri, all1 = t.sb("tri", [P, P]), t.sb("all1", [P, P])
        iota8, iotaS = t.sb("iota8", [P, E]), t.sb("iotaS", [P, CAP])
        ecol = t.sb("ecol", [P, E])
        rows = t.sb("rows", [CAP, K, B * TQ])
        sel = t.sb("sel", [P, TT, SL], F32R)
        bufT = t.sb("bufT", [P, KC, SL])
        rT = t.sb("rT", [R, SL])

        bank = [t.ps(f"bank{i}") for i in range(8)]
        h_ps, y_ps, t_ps, c_ps = bank[0:2], bank[2:4], bank[4:6], bank[6:8]

        names = ("consts", "chain", "var_ready", "root_ready", "xn_ready", "rows_ld", "gate_ld", "xT_ps", "xT_ok", "x_hi", "bT_ps", "bT_ok",
                 "lg_ps", "lm_ok", "exp_ok", "oh_ok", "cnt_ps", "ids_ok", "rows_ps", "rows_ok",
                 "sh_ps", "sh_ok", "sr_ps", "sr_ok", "so_ps", "so_ok",
                 "sel_ok", "g_ps", "g_ok", "h_ps", "h_ok", "r_ps", "r_ok", "y_ps", "y_ok", "yt_ps", "yt_hi", "yt_lo", "comb_ok", "c_ps", "c_ok", "stored")
        s = {n: t.sem(n) for n in names}
        w1_ld, w2_ld, ad_ld = ([t.sem(f"{n}{i}") for i in range(2)] for n in ("w1_ld", "w2_ld", "ad_ld"))

        with ExitStack() as first:
            f = Tensors(nc, first, "sh")
            ln = ln_scratch(f)
            xn = f.sb("xn", [P, TT, D])
            xnT = f.sb("xnT", [P, KC, B * TQ])
            b1_rows, b_rows = f.sb("b1_rows", [P, P]), f.sb("b_rows", [P, P])
            hS = f.sb("hS", [P, 8, B * TQ])
        rS = bufT[0:R, :, :].rearrange("p c n -> p (c n)")[:, 0:B * TQ]
        second = ctx.enter_context(ExitStack())
        f = Tensors(nc, second, "ex")
        hT = f.sb("hT", [P, FC, SL])
        yT = f.sb("yT", [P, KC, SL])
        yh, yl = f.sb("yh", [CAP, K, D], F32R), f.sb("yl", [CAP, K, D], F32R)
        comb = f.sb("comb", [CAP, K, B * TQ], F32R)
        block = ctx.enter_context(nc.Block())

        SB1 = E * KC

        @block.sync
        def _(sp):
            sp.dma_start(gate[:, :, :], a["L0_ffn_gate_w"].rearrange("(c p) e -> p c e", p=P)).then_inc(s["gate_ld"], 16)
            for c in range(KC):
                sp.dma_start(w1[1][:, c, :], a["L0_ffn_sw1"][c * P:(c + 1) * P, :]).then_inc(w1_ld[1], 16)
            sp.dma_start(wd[1][:, :, :], a["L0_ffn_swd"].rearrange("(c p) r -> p c r", p=P)).then_inc(ad_ld[1], 16)
            sp.dma_start(wu[1][:, :], a["L0_ffn_swu"]).then_inc(ad_ld[1], 16)
            for c in range(4):
                sp.dma_start(w2[1][:, c * 4:(c + 1) * 4, :], a["L0_ffn_sw2"][c * 4 * P:(c + 1) * 4 * P, :].rearrange("(c p) n -> p c n", p=P)).then_inc(w2_ld[1], 16)

            def expert_loads(e, i):
                for c in range(KC):
                    sp.dma_start(w1[i][:, c, :], a["L0_ffn_w1"][bass.ds(e, 1), c * P:(c + 1) * P, :].rearrange("o p n -> (o p) n")).then_inc(w1_ld[i], 16)
                sp.dma_start(wd[i][:, :, :], a["L0_ffn_wd"][bass.ds(e, 1), :, :].rearrange("o (c p) r -> p (o c) r", p=P)).then_inc(ad_ld[i], 16)
                sp.dma_start(wu[i][:, :], a["L0_ffn_wu"][bass.ds(e, 1), :, :].rearrange("o r n -> (o r) n")).then_inc(ad_ld[i], 16)

            def expert_loads2(e, i):
                for c in range(4):
                    sp.dma_start(w2[i][:, c * 4:(c + 1) * 4, :],
                                 a["L0_ffn_w2"][bass.ds(e, 1), c * 4 * P:(c + 1) * 4 * P, :].rearrange("o (c p) n -> p (o c) n", p=P)).then_inc(w2_ld[i], 16)

            expert_loads(0, 0)
            expert_loads2(0, 0)
            sp.wait_ge(s["sh_ps"], FC)
            sp.wait_ge(s["so_ps"], TT * 2)
            expert_loads(1, 1)
            expert_loads2(1, 1)
            with sp.Fori(0, (E - 2) // 2) as m:
                for q in range(2):
                    e = m * 2 + q
                    sp.wait_ge(s["r_ps"], e + 1)
                    sp.wait_ge(s["y_ps"], e * 2 + 2)
                    expert_loads(e + 2, q)
                    expert_loads2(e + 2, q)
            sp.wait_ge(s["c_ok"], E * K * TT)
            sp.dma_start(out.rearrange("b (r p) d -> p (b r) d", p=P), X[:, :, :]).then_inc(s["stored"], 16)
            sp.wait_ge(s["stored"], 16)

        @block.gpsimd
        def _(pool):
            c = s["consts"]
            nc.gpsimd.memset(ones[:, :], 1.0).then_inc(c, 1)
            nc.gpsimd.memset(all1[:, :], 1.0).then_inc(c, 1)
            nc.gpsimd.memset(tri[:, :], 1.0).then_inc(c, 1)
            nc.gpsimd.memset(b_rows[:, :], 0.0).then_inc(c, 1)
            nc.gpsimd.iota(iota8[:, :], pattern=[[1, E]], base=0, channel_multiplier=0, allow_small_or_imprecise_dtypes=True).then_inc(c, 1)
            nc.gpsimd.iota(iotaS[:, :], pattern=[[1, CAP]], base=1, channel_multiplier=0, allow_small_or_imprecise_dtypes=True).then_inc(c, 1)
            nc.gpsimd.iota(ecol[:, :], pattern=[[STRIDE, E]], base=1, channel_multiplier=1, allow_small_or_imprecise_dtypes=True).then_inc(c, 1)
            pool.wait_ge(c, 7)
            nc.gpsimd.affine_select(out=tri[:, :], in_=tri[:, :], compare_op=ALU.is_ge, fill=0.0,
                                    base=0, pattern=[[1, P]], channel_multiplier=-1).then_inc(c, 1)
            r = s["rows_ld"]
            pool.dma_start(b1_rows[:, :], a["L0_ffn_b1"].rearrange("e (c p) -> (e c) p", p=P)).then_inc(r, 16)
            pool.dma_start(b_rows[0:SB1, :], a["L0_ffn_b2"].rearrange("e (c p) -> (e c) p", p=P)).then_inc(r, 16)
            pool.dma_start(b_rows[SB1:SB1 + FC, :], a["L0_ffn_sb1"].rearrange("(c p) -> c p", p=P)).then_inc(r, 16)
            pool.dma_start(sb2_row[:, :], a["L0_ffn_sb2"].rearrange("(o d) -> o d", o=1)).then_inc(r, 16)
            pool.wait_ge(r, 64)

        @block.vector
        def _(v):
            ch = Chain(v, s["chain"])
            ln_vector(v, ch, X, xn, ln, s["root_ready"], s["var_ready"])
            v.engine_nop().then_inc(s["xn_ready"], 1)
            for c in range(KC):
                v.wait_ge(s["xT_ps"], c + 1)
                v.tensor_copy(xnT[:, c, :], bank[c][:, :]).then_inc(s["xT_ok"], 1)
            for i, cols in enumerate((b1_cols, b_cols)):
                v.wait_ge(s["bT_ps"], i + 1)
                v.tensor_copy(cols[:, :], bank[4 + i][:, 0:P]).then_inc(s["bT_ok"], 1)
            v.wait_ge(s["x_hi"], 1)
            v.tensor_tensor(xl[:, :, :], xn[:, :, :], xh[:, :, :].bitcast(F32), ALU.subtract).then_inc(s["x_hi"], 1)
            v.wait_ge(s["consts"], 8)
            v.wait_ge(s["lg_ps"], 1)
            ch.link(v.tensor_copy(lg[:, :, :], bank[6][:, 0:TT * E].rearrange("p (i e) -> p i e", e=E)))
            ch.link(v.tensor_reduce(small[:, :], lg[:, :, :], op=ALU.max, axis=AX.X))
            ch.link(v.tensor_tensor(lg[:, :, :], lg[:, :, :], small[:, :].unsqueeze(2).to_broadcast([P, TT, E]), ALU.subtract))
            ch.link(v.tensor_scalar(lg[:, :, :], lg[:, :, :], LOWEST, None, ALU.max))
            for i in range(TT):
                v.max(top[:, i, :], lg[:, i, :]).then_inc(s["chain"], 1)
            ch.n += TT
            v.wait_ge(s["chain"], ch.n)
            for i in range(TT):
                v.max_index(topi[:, i, :], top[:, i, :], lg[:, i, :]).then_inc(s["lm_ok"], 1)
            v.wait_ge(s["lm_ok"], TT)
            ch.link(v.tensor_copy(topf[:, :, :], topi[:, :, :]))
            for i in range(TT):
                for k in range(K):
                    v.tensor_scalar(onehot[:, i, k, :], iota8[:, :], topf[:, i, k:k + 1], None, ALU.is_equal).then_inc(s["oh_ok"], 1)
            v.wait_ge(s["exp_ok"], 2)
            ch.link(v.tensor_reduce(small[:, :], prob[:, :, :], op=ALU.add, axis=AX.X))
            ch.link(v.reciprocal(small[:, :], small[:, :]))
            ch.link(v.tensor_tensor(topp[:, :, :], topp[:, :, :], small[:, :].unsqueeze(2).to_broadcast([P, TT, 8]), ALU.mult))
            v.wait_ge(s["cnt_ps"], 1)
            ch.link(v.tensor_tensor(cnt[:, :, :, :].rearrange("p i k e -> p (i k e)"), bank[7][:, 0:TT * K * E],
                                    onehot[:, :, :, :].rearrange("p i k e -> p (i k e)"), ALU.mult))
            v.wait_ge(s["oh_ok"], TT * K)
            v.tensor_reduce(ids[:, :, :].rearrange("p i k -> p (i k)"), cnt[:, :, :, :].rearrange("p i k e -> p (i k) e"), op=ALU.add, axis=AX.X).then_inc(s["chain"], 1)
            ch.n += 1
            v.wait_ge(s["chain"], ch.n)
            v.scalar_tensor_tensor(ids[:, :, :], topf[:, :, 0:K], float(STRIDE), ids[:, :, :], ALU.mult, ALU.add).then_inc(s["ids_ok"], 1)

            def select(e):
                for k in range(K):
                    for i in range(TT):
                        m = v.tensor_scalar(sel[:, i, k * CAP:(k + 1) * CAP], iotaS[:, :], cnt[:, i, k, bass.ds(e, 1)], None, ALU.is_equal)
                        if i == TT - 1 and k == K - 1:
                            m.then_inc(s["sel_ok"], 1)

            def combine(e):
                for k in range(K):
                    m = v.tensor_scalar(comb[:, k, :], rows[:, k, :], ecol[0:CAP, bass.ds(e, 1)], None, ALU.is_equal)
                m.then_inc(s["comb_ok"], 1)

            for k in range(K):
                v.wait_ge(s["rows_ps"], k + 1)
                v.tensor_copy(rows[:, k, :], bank[4 + k][0:CAP, :]).then_inc(s["rows_ok"], 1)
            select(0)
            for i in range(2 * TT):
                v.wait_ge(s["so_ps"], i + 1)
                v.scalar_tensor_tensor(X[:, i % TT, :], bank[2 + i % 2][:, :], 0.2, X[:, i % TT, :], ALU.mult, ALU.add).then_inc(s["so_ok"], 1)
            v.wait_ge(s["rows_ok"], K)

            def turned(e):
                for k in range(K):
                    v.wait_ge(s["yt_hi"], e * K + (k + 1))
                    v.tensor_tensor(yl[:, k, :], t_ps[k][0:CAP, :], yh[:, k, :].bitcast(F32), ALU.subtract).then_inc(s["yt_lo"], 1)

            def residual(e):
                for k in range(K):
                    for i in range(TT):
                        n = k * TT + i
                        v.wait_ge(s["c_ps"], e * (K * TT) + (n + 1))
                        v.scalar_tensor_tensor(X[:, i, :], c_ps[n % 2][:, :], topp[:, i, k:k + 1], X[:, i, :], ALU.mult, ALU.add).then_inc(s["c_ok"], 1)

            def biased(e):
                for c in range(KC):
                    v.wait_ge(s["y_ps"], e * 2 + (c // 2 + 1))
                    m = v.tensor_scalar(yT[:, c, :], y_ps[c // 2][:, c % 2 * SL:(c % 2 + 1) * SL], b_cols[:, bass.ds(e * KC + c, 1)], None, ALU.add)
                    if c % 2:
                        m.then_inc(s["y_ok"], 1)

            def expert(e, first, last):
                if not last:
                    v.wait_ge(s["g_ps"], e * 2 + 2)
                    select(e + 1)
                if not first:
                    turned(e - 1)
                    residual(e - 1)
                combine(e)
                biased(e)

            expert(0, True, False)
            with v.Fori(0, (E - 2) // 2) as m:
                for q in range(2):
                    expert(m * 2 + (q + 1), False, False)
            expert(E - 1, False, True)
            turned(E - 1)
            residual(E - 1)

        @block.scalar
        def _(act):
            act.wait_ge(s["var_ready"], 1)
            act.activation(ln["root"][:, :], ln["veps"][:, :], ACT.Sqrt).then_inc(s["root_ready"], 1)
            act.wait_ge(s["xn_ready"], 1)
            act.activation(xh[:, :, :], xn[:, :, :], ACT.Copy).then_inc(s["x_hi"], 1)
            act.wait_ge(s["lm_ok"], TT)
            act.activation(prob[:, :, :], lg[:, :, :], ACT.Exp).then_inc(s["exp_ok"], 1)
            act.activation(topp[:, :, :], top[:, :, :], ACT.Exp).then_inc(s["exp_ok"], 1)
            act.wait_ge(s["bT_ok"], 2)
            for n in range(FC):
                act.wait_ge(s["sh_ps"], n + 1)
                if n == FC // 2:
                    act.wait_ge(s["so_ps"], TT)
                act.activation(hS[:, n % 8, :], h_ps[n % 2][:, :], ACT.Gelu, bias=b_cols[:, SB1 + n:SB1 + n + 1]).then_inc(s["sh_ok"], 1)
                if n == 0:
                    act.wait_ge(s["sr_ps"], 1)
                    act.activation(rS[:, :], bank[6][0:R, :], ACT.Gelu).then_inc(s["sr_ok"], 1)

            def gathered(e):
                for q in range(2):
                    act.wait_ge(s["g_ps"], e * 2 + (q + 1))
                    act.activation(bufT[:, 2 * q:2 * q + 2, :].rearrange("p c n -> p (c n)"), t_ps[q][:, 0:2 * SL], ACT.Copy).then_inc(s["g_ok"], 1)

            def hidden(e, n):
                act.wait_ge(s["h_ps"], e * (FC // 2) + (n + 1))
                for q in range(2):
                    m = act.activation(hT[:, 2 * n + q, :], h_ps[n % 2][:, q * SL:(q + 1) * SL], ACT.Gelu, bias=b1_cols[:, bass.ds(e * FC + (2 * n + q), 1)])
                m.then_inc(s["h_ok"], 1)

            def turned(e):
                for k in range(K):
                    act.wait_ge(s["yt_ps"], e * K + (k + 1))
                    act.activation(yh[:, k, :], t_ps[k][0:CAP, :], ACT.Copy).then_inc(s["yt_hi"], 1)

            def expert(e, first, last):
                for n in range(4):
                    hidden(e, n)
                if not first:
                    turned(e - 1)
                for n in range(4, FC // 2):
                    hidden(e, n)
                act.wait_ge(s["r_ps"], e + 1)
                act.activation(rT[:, :], bank[6][0:R, 0:SL], ACT.Gelu).then_inc(s["r_ok"], 1)
                if not last:
                    gathered(e + 1)

            gathered(0)
            expert(0, True, False)
            with act.Fori(0, (E - 2) // 2) as m:
                for q in range(2):
                    expert(m * 2 + (q + 1), False, False)
            expert(E - 1, False, True)
            turned(E - 1)

        @block.tensor
        def _(pe):
            pe.wait_ge(s["xn_ready"], 1)
            for c in range(KC):
                for i in range(TT):
                    m = pe.transpose(bank[c][:, i * P:(i + 1) * P], xn[:, i, c * P:(c + 1) * P], ident[:, :])
                m.then_inc(s["xT_ps"], 1)
            pe.wait_ge(s["rows_ld"], 64)
            pe.transpose(bank[4][:, 0:P], b1_rows[:, :], ident[:, :]).then_inc(s["bT_ps"], 1)
            pe.transpose(bank[5][:, 0:P], b_rows[:, :], ident[:, :]).then_inc(s["bT_ps"], 1)
            pe.wait_ge(s["xT_ok"], KC)
            pe.wait_ge(s["gate_ld"], 16)
            for i in range(TT):
                for c in range(KC):
                    m = pe.matmul(bank[6][:, i * E:(i + 1) * E], xnT[:, c, i * P:(i + 1) * P], gate[:, c, :], start=c == 0, stop=c == KC - 1)
            m.then_inc(s["lg_ps"], 1)

            def shared_hidden(n):
                if n >= 2:
                    pe.wait_ge(s["sh_ok"], n - 1)
                for c in range(KC):
                    m = pe.matmul(h_ps[n % 2][:, :], w1[1][:, c, n * P:(n + 1) * P], xnT[:, c, :], start=c == 0, stop=c == KC - 1)
                m.then_inc(s["sh_ps"], 1)

            def shared_out(half):
                pe.wait_ge(s["sh_ok"], (half + 1) * 8)
                for i in range(TT):
                    n = half * TT + i
                    if n >= 2:
                        pe.wait_ge(s["so_ok"], n - 1)
                    o = bank[2 + n % 2][:, :]
                    for c in range(8):
                        m = pe.matmul(o, hS[:, c, i * P:(i + 1) * P], w2[1][:, half * 8 + c, :], start=c == 0, stop=half == 0 and c == 7)
                    if half == 1:
                        pe.matmul(o, rS[:, i * P:(i + 1) * P], wu[1][:, :], start=False, stop=False)
                        m = pe.matmul(o, ones[:, :], sb2_row[:, :], start=False, stop=True)
                    m.then_inc(s["so_ps"], 1)

            pe.wait_ge(w1_ld[1], 64)
            pe.wait_ge(s["consts"], 8)
            shared_hidden(0)
            pe.wait_ge(s["lm_ok"], TT)
            pe.wait_ge(ad_ld[1], 32)
            for c in range(KC):
                m = pe.matmul(bank[6][0:R, :], wd[1][:, c, :], xnT[:, c, :], start=c == 0, stop=c == KC - 1)
            m.then_inc(s["sr_ps"], 1)
            for n in range(1, 4):
                shared_hidden(n)
            pe.wait_ge(s["oh_ok"], TT * K)
            for i in range(TT):
                for q in range(i + 1):
                    m = pe.matmul(bank[7][:, i * K * E:(i + 1) * K * E], (tri if q == i else all1)[:, :], onehot[:, q, :, :].rearrange("p k e -> p (k e)"),
                                  start=q == 0, stop=q == i)
            m.then_inc(s["cnt_ps"], 1)
            for n in range(4, 8):
                shared_hidden(n)
            pe.wait_ge(s["ids_ok"], 1)
            pe.wait_ge(s["bT_ok"], 2)
            for k in range(K):
                for i in range(TT):
                    m = pe.matmul(bank[4 + k][:, i * P:(i + 1) * P], ids[:, i, k:k + 1].to_broadcast([P, P]), ident[:, :], start=True, stop=True)
                m.then_inc(s["rows_ps"], 1)
            pe.wait_ge(w2_ld[1], 64)
            pe.wait_ge(s["sr_ok"], 1)
            shared_out(0)
            for n in range(8, FC):
                shared_hidden(n)
            shared_out(1)

            def gather(e):
                pe.wait_ge(s["sel_ok"], e + 1)
                for c in range(KC):
                    for i in range(TT):
                        for part in (xl, xh):
                            m = pe.matmul(t_ps[c // 2][:, c % 2 * SL:(c % 2 + 1) * SL], part[:, i, c * P:(c + 1) * P], sel[:, i, :],
                                          start=i == 0 and part is xl, stop=i == TT - 1 and part is xh)
                    if c % 2:
                        m.then_inc(s["g_ps"], 1)

            def turn(e):
                pe.wait_ge(s["y_ok"], e * 2 + 2)
                for k in range(K):
                    for c in range(KC):
                        m = pe.transpose(t_ps[k][0:CAP, c * P:(c + 1) * P], yT[:, c, k * CAP:(k + 1) * CAP], ident[:, :])
                    m.then_inc(s["yt_ps"], 1)

            def scatter(e, first):
                pe.wait_ge(s["comb_ok"], e + 1)
                pe.wait_ge(s["yt_lo"], e * K + K)
                for n in range(K * TT):
                    k, i = n // TT, n % TT
                    if not (first and n < 2):
                        pe.wait_ge(s["c_ok"], e * (K * TT) + (n - 1))
                    for part in (yl, yh):
                        m = pe.matmul(c_ps[n % 2][:, :], comb[:, k, i * P:(i + 1) * P], part[:, k, :], start=part is yl, stop=part is yh)
                    m.then_inc(s["c_ps"], 1)

            def expert(e, i, uses, before, last):
                first = before == 0
                pe.wait_ge(w1_ld[i], uses * 64)
                pe.wait_ge(s["g_ok"], e * 2 + 2)

                def layer1(n):
                    if not (first and n < 2):
                        pe.wait_ge(s["h_ok"], e * (FC // 2) + (n - 1))
                    for q in range(2):
                        fc = 2 * n + q
                        for c in range(KC):
                            m = pe.matmul(h_ps[n % 2][:, q * SL:(q + 1) * SL], w1[i][:, c, fc * P:(fc + 1) * P], bufT[:, c, :], start=c == 0, stop=c == KC - 1)
                    m.then_inc(s["h_ps"], 1)

                for n in range(4):
                    layer1(n)
                if not first:
                    turn(e - 1)
                for n in range(4, FC // 2):
                    layer1(n)
                pe.wait_ge(ad_ld[i], uses * 32)
                if before == 2:
                    pe.wait_ge(s["c_ok"], (e - 1) * (K * TT))
                for c in range(KC):
                    m = pe.matmul(bank[6][0:R, 0:SL], wd[i][:, c, :], bufT[:, c, :], start=c == 0, stop=c == KC - 1)
                m.then_inc(s["r_ps"], 1)
                pe.wait_ge(s["r_ok"], e + 1)
                if not first:
                    scatter(e - 1, before == 1)
                if not last:
                    gather(e + 1)
                pe.wait_ge(w2_ld[i], uses * 64)
                pe.wait_ge(s["h_ok"], e * (FC // 2) + FC // 2)
                for c in range(KC):
                    if c % 2 == 0 and not first:
                        pe.wait_ge(s["y_ok"], e * 2 + c // 2 - 1)
                    o = y_ps[c // 2][:, c % 2 * SL:(c % 2 + 1) * SL]
                    for n in range(FC):
                        pe.matmul(o, w2[i][:, n, c * P:(c + 1) * P], hT[:, n, :], start=n == 0, stop=False)
                    m = pe.matmul(o, wu[i][:, c * P:(c + 1) * P], rT[:, :], start=False, stop=True)
                    if c % 2:
                        m.then_inc(s["y_ps"], 1)

            pe.wait_ge(s["rows_ok"], K)
            gather(0)
            pe.wait_ge(s["so_ok"], 2 * TT)
            pe.wait_ge(s["sh_ok"], FC)
            expert(0, 0, 1, 0, False)
            expert(1, 1, 2, 1, False)
            with pe.Fori(0, (E - 4) // 2) as m:
                for q in range(2):
                    expert(m * 2 + (q + 2), q, m + (2 + q), 2, False)
            expert(E - 2, 0, E // 2, 2, False)
            expert(E - 1, 1, E // 2 + 1, 2, True)
            turn(E - 1)
            scatter(E - 1, False)


def perceiver(nc, a, out):
    q_dram = nc.dram_tensor("q_scratch", [H, HD, B * TQ], F32, kind="Internal").ap()
    with ExitStack() as ctx:
        t = Tensors(nc, ctx, "all")
        X = t.sb("X", [P, TT, D])
        ident = t.sb("ident", [P, P])
        with ExitStack() as both:
            prob = Tensors(nc, both, "crs").sb("prob", [P, RT, S])
            queries(nc, a["x"], a["L0_xattn_Wq"], a["ctx_1024"], q_dram, X, ident, prob)
            cross(nc, a["ctx_1024"], a["mask_BxS2_bf1"], a["L0_xattn_Wk"], a["L0_xattn_Wv"], a["L0_xattn_Wo"], q_dram, X, ident, prob)
        selfattn(nc, a, X, ident)
        experts(nc, a, out, X, ident)


def kernel(**inputs):
    import numpy as _np
    import concourse.bacc as _bacc
    from concourse import mybir as _mybir
    from concourse.bass_utils import run_bass_kernel_spmd as _run

    nc = _bacc.Bacc("TRN2", target_bir_lowering=False, num_devices=1)
    arrays, args = {}, {}
    for name, value in inputs.items():
        a = _np.ascontiguousarray(value)
        if a.dtype == _np.bool_:
            a = a.view(_np.uint8)
        arrays[f"in_{name}"] = a
        args[name] = nc.dram_tensor(f"in_{name}", a.shape, _mybir.dt.from_np(a.dtype), kind="ExternalInput").ap()
    out = nc.dram_tensor("out_x", (B, TQ, D), _mybir.dt.float32, kind="ExternalOutput").ap()
    perceiver(nc, args, out)
    r = _run(nc, [arrays], core_ids=[0])
    return r.results[0]["out_x"]
```

```python
import concourse.bass as bass
from concourse import mybir
from contextlib import ExitStack

F32 = mybir.dt.float32
F32R = mybir.dt.float32r
BF16 = mybir.dt.bfloat16
U8 = mybir.dt.uint8
U32 = mybir.dt.uint32
ACT = mybir.ActivationFunctionType
ALU = mybir.AluOpType
AX = mybir.AxisListType

P = 128
BANK = 512
B, TQ, D = 2, 256, 512
TT = B * TQ // P
RT = TQ // P
KC = D // P
S, DC = 4096, 256
CC = DC // P
SCH = S // P
SB = S // BANK
H, HKV, HD = 16, 8, 128
GRP = H // HKV
EPS = 1e-5
NEG = -3.0e38


class Tensors:

    def __init__(self, nc, ctx, tag):
        self.nc, self.ctx, self.tag = nc, ctx, tag

    def sb(self, name, shape, dt=F32):
        return self.ctx.enter_context(self.nc.sbuf_tensor(f"{self.tag}_{name}", shape, dt))

    def ps(self, name, shape=(P, BANK), dt=F32):
        return self.ctx.enter_context(self.nc.psum_tensor(f"{self.tag}_{name}", list(shape), dt))

    def sem(self, name):
        return self.ctx.enter_context(self.nc.semaphore(f"{self.tag}_{name}"))


class Chain:

    def __init__(self, eng, sem):
        self.eng, self.sem, self.n = eng, sem, 0

    def link(self, ins):
        self.n += 1
        ins.then_inc(self.sem, 1)
        self.eng.wait_ge(self.sem, self.n)


def ln_scratch(t):
    return dict(stats=t.sb("ln_stats", [P, TT, 6]), mv=t.sb("ln_mv", [P, TT, 2]), root=t.sb("ln_root", [P, TT]),
                div=t.sb("ln_div", [P, TT]), rstd=t.sb("ln_rstd", [P, TT]), veps=t.sb("ln_veps", [P, TT]),
                table=t.sb("ln_table", [P, 1]))


def ln_vector(v, ch, X, out, w, root_ready, var_ready):
    for i in range(TT):
        v.bn_stats(w["stats"][:, i, :], X[:, i, :]).then_inc(ch.sem, 1)
    ch.n += TT
    v.wait_ge(ch.sem, ch.n)
    for i in range(TT):
        v.bn_aggr(w["mv"][:, i, :], w["stats"][:, i, :]).then_inc(ch.sem, 1)
    ch.n += TT
    v.wait_ge(ch.sem, ch.n)
    v.tensor_scalar(w["veps"][:, :], w["mv"][:, :, 1], EPS, None, ALU.add).then_inc(var_ready, 1)
    v.wait_ge(root_ready, 1)
    ch.link(v.reciprocal(w["div"][:, :], w["root"][:, :]))
    ch.link(v.tensor_tensor(w["div"][:, :], w["div"][:, :], w["veps"][:, :], ALU.mult))
    ch.link(v.tensor_tensor(w["div"][:, :], w["div"][:, :], w["root"][:, :], ALU.add))
    ch.link(v.tensor_scalar(w["div"][:, :], w["div"][:, :], 0.5, None, ALU.mult))
    ch.link(v.reciprocal(w["rstd"][:, :], w["div"][:, :]))
    for i in range(TT):
        v.tensor_scalar(out[:, i, :], X[:, i, :], w["mv"][:, i, 0:1], w["rstd"][:, i:i + 1],
                        ALU.subtract, ALU.mult).then_inc(ch.sem, 1)
    ch.n += TT
    v.wait_ge(ch.sem, ch.n)


def context_piece(prob, ctx_in, b, n):
    k = BANK // P
    cin = prob[:, :, :].rearrange("p r s -> p (r s)").rearrange("p (n c) -> p n c", c=DC)
    return (cin[:, bass.ds(n * k, k), :],
            ctx_in[bass.ds(b, 1), bass.ds(n * BANK, BANK), :].rearrange("o (n p) c -> p (o n) c", p=P))


def raw_weight(prob, i, c):
    at = i * KC // RT * D + c % (KC // RT) * D
    return prob[:, c // (KC // RT), at:at + D]


def raw_weight_load(eng, prob, i, w, sem):
    k = KC // RT
    for r in range(RT):
        eng.dma_start(prob[:, r, i * k * D:(i + 1) * k * D].rearrange("p (c n) -> p c n", c=k),
                      w[r * k * P:(r + 1) * k * P, :].rearrange("(c p) n -> p c n", p=P)).then_inc(sem, 16)


def queries(nc, x, wq, ctx_in, q_dram, X, ident, prob):
    SLOTS = 4
    QB = 4
    WB = 2
    with ExitStack() as ctx:
        t = Tensors(nc, ctx, "qry")
        ln = ln_scratch(t)
        xn = t.sb("xn", [P, TT, D])
        xh, xl = t.sb("xh", [P, KC, B * TQ], F32R), t.sb("xl", [P, KC, B * TQ], F32R)
        wq_sb = t.sb("wq", [P, SLOTS, KC, HD])
        wh, wl = ([t.sb(f"{n}{i}", [P, KC, HD], F32R) for i in range(WB)] for n in ("wh", "wl"))
        q_sb = t.sb("q", [P, QB, B * TQ])
        ps = [t.ps(f"ps{i}") for i in range(QB)]
        x_ld, ident_ok, var_ready, root_ready, xn_ready = (t.sem(n) for n in ("x_ld", "ident_ok", "var_ready", "root_ready", "xn_ready"))
        xT_ps, xT_hi, xT_lo, w_hi, w_lo, q_ps, q_done, chain, ctx_ld = (
            t.sem(n) for n in ("xT_ps", "xT_hi", "xT_lo", "w_hi", "w_lo", "q_ps", "q_done", "chain", "ctx_ld"))
        wq_ld = [t.sem(f"wq_ld{i}") for i in range(SLOTS)]
        q_out = [t.sem(f"q_out{i}") for i in range(QB)]
        block = ctx.enter_context(nc.Block())

        @block.sync
        def _(sp):
            for n in range(B):
                sp.dma_start(X[:, n * RT:(n + 1) * RT, :], x[n, :, :].rearrange("(r p) d -> p r d", p=P)).then_inc(x_ld, 16)
            with sp.Fori(0, H // SLOTS) as r:
                for i in range(SLOTS):
                    sp.wait_ge(w_lo, r * SLOTS + (i + 1))
                    sp.dma_start(wq_sb[:, i, :, :], wq[:, bass.ds((r * SLOTS + i) * HD, HD)].rearrange("(c p) n -> p c n", p=P)).then_inc(wq_ld[i], 16)
                for i in range(SB * SLOTS // H):
                    sp.dma_start(*context_piece(prob, ctx_in, 0, r * (SB * SLOTS // H) + i)).then_inc(ctx_ld, 16)
            sp.wait_ge(ctx_ld, SB * 16)

        @block.gpsimd
        def _(pool):
            nc.gpsimd.memset(ident[:, :], 0.0).then_inc(ident_ok, 1)
            pool.wait_ge(ident_ok, 1)
            nc.gpsimd.affine_select(out=ident[:, :], in_=ident[:, :], compare_op=ALU.not_equal, fill=1.0,
                                    base=0, pattern=[[-1, P]], channel_multiplier=1).then_inc(ident_ok, 1)

        @block.vector
        def _(v):
            ch = Chain(v, chain)
            v.sem_inc(w_lo, SLOTS)
            v.wait_ge(x_ld, B * 16)
            ln_vector(v, ch, X, xn, ln, root_ready, var_ready)
            v.engine_nop().then_inc(xn_ready, 1)
            for c in range(KC):
                v.wait_ge(xT_hi, c + 1)
                v.tensor_tensor(xl[:, c, :], ps[c][:, :], xh[:, c, :].bitcast(F32), ALU.subtract).then_inc(xT_lo, 1)
            with v.Fori(0, H // SLOTS) as r:
                for i in range(SLOTS):
                    v.wait_ge(w_hi, r * SLOTS + (i + 1))
                    v.tensor_tensor(wl[i % WB][:, :, :], wq_sb[:, i, :, :], wh[i % WB][:, :, :].bitcast(F32), ALU.subtract).then_inc(w_lo, 1)

        @block.scalar
        def _(act):
            act.wait_ge(ident_ok, 2)
            act.activation(ln["table"][:, :], ident[:, 0:1], ACT.Sqrt)
            act.wait_ge(var_ready, 1)
            act.activation(ln["root"][:, :], ln["veps"][:, :], ACT.Sqrt).then_inc(root_ready, 1)
            for c in range(KC):
                act.wait_ge(xT_ps, c + 1)
                act.activation(xh[:, c, :], ps[c][:, :], ACT.Copy).then_inc(xT_hi, 1)
            for i in range(QB):
                act.sem_inc(q_out[i], 16)
            act.sem_inc(q_done, QB)

            def weight_high(r, i):
                act.wait_ge(wq_ld[i], r * 16 + 16)
                act.wait_ge(q_ps, r * SLOTS + (i + 1))
                act.activation(wh[i % WB][:, :, :], wq_sb[:, i, :, :], ACT.Copy).then_inc(w_hi, 1)

            def query_out(head, r, i):
                act.wait_ge(q_ps, head + (WB + 1))
                act.wait_ge(q_out[i % QB], r * (SLOTS // QB * 16) + (i // QB + 1) * 16)
                act.activation(q_sb[:, i % QB, :], ps[i % QB][:, :], ACT.Copy, scale=HD ** -0.5).then_inc(q_done, 1)
                act.wait_ge(q_done, head + (QB + 1))
                act.dma_start(q_dram[bass.ds(head, 1), :, :].rearrange("o p n -> p (o n)"), q_sb[:, i % QB, :]).then_inc(q_out[i % QB], 16)

            weight_high(0, 0)
            weight_high(0, 1)
            with act.Fori(0, H // SLOTS - 1) as r:
                for i in range(SLOTS):
                    weight_high(r + (i + WB) // SLOTS, (i + WB) % SLOTS)
                    query_out(r * SLOTS + i, r, i)
            for i in range(SLOTS):
                r = H // SLOTS - 1
                if i + WB < SLOTS:
                    weight_high(r, i + WB)
                query_out(r * SLOTS + i, r, i)
            for i in range(QB):
                act.wait_ge(q_out[i], (H // QB + 1) * 16)

        @block.tensor
        def _(pe):
            pe.sem_inc(q_ps, WB)
            pe.wait_ge(ident_ok, 2)
            pe.wait_ge(xn_ready, 1)
            for c in range(KC):
                for i in range(TT):
                    m = pe.transpose(ps[c][:, i * P:(i + 1) * P], xn[:, i, c * P:(c + 1) * P], ident[:, :])
                m.then_inc(xT_ps, 1)
            pe.wait_ge(xT_lo, KC)
            with pe.Fori(0, H // SLOTS) as r:
                for i in range(SLOTS):
                    pe.wait_ge(w_lo, r * SLOTS + (SLOTS + i + 1))
                    pe.wait_ge(q_done, r * SLOTS + (i + 1))
                    for n, (w, y, c) in enumerate((w, y, c) for w, y in ((wl, xh), (wh, xl), (wh, xh)) for c in range(KC)):
                        m = pe.matmul(ps[i % QB][:, :], w[i % WB][:, c, :], y[:, c, :], start=n == 0, stop=n == 3 * KC - 1)
                    m.then_inc(q_ps, 1)


def cross(nc, ctx_in, mask, wk, wv, wo, q_dram, attn_w, X, ident, prob):
    RING = 4
    HEAD_ITEMS = CC * SB
    K_AT, V_AT = 0, SB + RT * SB
    QK_AT = (SB, V_AT + 2 * SB)
    GROUP_ITEMS = QK_AT[1] + RT * SB
    BATCH_ITEMS = HEAD_ITEMS + HKV * GROUP_ITEMS
    HIGHS = 2 * SB
    BATCH_HIGHS = HEAD_ITEMS + HKV * HIGHS
    STEPS = SCH // 2
    PARTS = 4
    PIECES = RT * PARTS
    PART = S // PARTS
    EARLY = 4
    SPLIT_AT = STEPS // 2
    BLOCKS = [r * PARTS + p for p in range(PARTS) for r in range(RT)]
    PROJECT_AT = (2, 5)
    MASKS = 4
    LAG = 2
    PT = LAG + 1
    with ExitStack() as ctx:
        t = Tensors(nc, ctx, "crs")
        ctxh, ctxl = t.sb("ctxh", [P, CC, S], F32R), t.sb("ctxl", [P, CC, S], F32R)
        kh, kl = t.sb("kh", [P, S], F32R), t.sb("kl", [P, S], F32R)
        vh, vl = t.sb("vh", [P, SCH, HD], F32R), t.sb("vl", [P, SCH, HD], F32R)
        maskb = t.sb("maskb", [P, S], BF16)
        qf = t.sb("qf", [P, GRP, TQ])
        qh, ql = t.sb("qh", [P, GRP, TQ], F32R), t.sb("ql", [P, GRP, TQ], F32R)
        wf = t.sb("wf", [P, 2, CC, HD])
        wh, wl = t.sb("wh", [P, 2, CC, HD], F32R), t.sb("wl", [P, 2, CC, HD], F32R)
        wo_sb = t.sb("wo", [P, GRP, D])
        pth, ptl = t.sb("pth", [P, PT, BANK], F32R), t.sb("ptl", [P, PT, BANK], F32R)
        mx = t.sb("mx", [P, RT, SB])
        nmax = t.sb("nmax", [P, RT])
        rs = t.sb("rs", [P, GRP, RT, PARTS])
        rinv = t.sb("rinv", [P, RT])
        anyp, anyv = t.sb("anyp", [P, SB]), t.sb("anyv", [P, 1])
        cin = prob[:, :, :].rearrange("p r s -> p (r s)").rearrange("p (n c) -> p n c", c=DC)
        mask_u8 = wo_sb[:, :, :].rearrange("p h d -> p (h d)").bitcast(U8)
        wo_slot, o_slot = (STEPS - 3) % PT, (STEPS - 1) % PT
        oh, ol, woh, wol = pth[:, o_slot, 0:TQ], ptl[:, o_slot, 0:TQ], pth[:, wo_slot, :], ptl[:, wo_slot, :]
        vT = (qf[:, :, :].rearrange("p h n -> p (h n)"), wf[:, :, :, :].rearrange("p w c n -> p (w c n)"))

        ring = [t.ps(f"ring{i}") for i in range(RING)]
        tp = [t.ps(f"tp{i}") for i in range(2)]
        ov, op = t.ps("ov"), t.ps("op")

        names = ("mask_ld", "q_ld", "w_ld", "wo0_ld", "wo1_ld", "ring_full", "ring_free", "hi_ok", "q_hi", "q_lo", "w_hi", "w_lo",
                 "max_ready", "p_ready", "pt_full", "pt_hi", "pt_lo", "pv_done", "o_hi", "o_lo", "op_full", "op_free", "mask_ok", "inv_chain", "any_chain", "scores_seen")
        s = {n: t.sem(n) for n in names}
        ctx_ld = [t.sem(f"ctx_ld{i}") for i in range(PARTS)]
        wo_ld = (s["wo0_ld"], s["wo1_ld"])
        block = ctx.enter_context(nc.Block())

        def items(b, j):
            return b * BATCH_ITEMS + j * GROUP_ITEMS + HEAD_ITEMS

        def highs(b, j):
            return b * BATCH_HIGHS + j * HIGHS + HEAD_ITEMS

        def group(b, j):
            return b * HKV + j

        def vt_item(n):
            return V_AT + (2 * n - 1 if n else 0)

        def v_item(n):
            return V_AT + min(2 * n + 2, 2 * SB - 1)

        @block.sync
        def _(sp):
            def weight_loads(j):
                for w, src in enumerate((wk, wv)):
                    sp.dma_start(wf[:, w, :, :], src[:, bass.ds(j * HD, HD)].rearrange("(c p) n -> p c n", p=P)).then_inc(s["w_ld"], 16)

            def v_gone(b, j):
                sp.wait_ge(s["ring_full"], items(b, j) + QK_AT[1])

            def group_loads(b, j, first):
                g = group(b, j)
                sp.dma_start(qf[:, :, :], q_dram[bass.ds(j * GRP, GRP), :, bass.ds(b * TQ, TQ)].rearrange("h p n -> p h n")).then_inc(s["q_ld"], 16)
                for h in range(GRP):
                    if not first:
                        sp.wait_ge(s["op_full"], g * (GRP * RT) - (GRP - 1 - h) * RT)
                    elif h == 0:
                        sp.wait_ge(s["mask_ok"], (b + 1) * MASKS)
                    sp.dma_start(wo_sb[:, h, :], wo[bass.ds((j * GRP + h) * HD, HD), :]).then_inc(wo_ld[h], 16)

            weight_loads(0)
            for b in range(B):
                for p in range(PARTS):
                    if b == 0:
                        sp.sem_inc(ctx_ld[p], RT * 16)
                        continue
                    sp.wait_ge(s["pt_full"], (b * HKV * GRP - 1) * STEPS + (p + 1) * (STEPS // PARTS))
                    for r in range(RT):
                        sp.dma_start(*context_piece(prob, ctx_in, b, r * PARTS + p)).then_inc(ctx_ld[p], 16)
                if b:
                    sp.wait_ge(s["op_full"], b * (HKV * GRP * RT))
                sp.dma_start(mask_u8, mask[bass.ds(b, 1), :].to_broadcast([P, S])).then_inc(s["mask_ld"], 16)
                group_loads(b, 0, True)
                with sp.Fori(1, HKV) as j:
                    v_gone(b, j - 1)
                    weight_loads(j)
                    group_loads(b, j, False)
                if b < B - 1:
                    v_gone(b, HKV - 1)
                    weight_loads(0)
            for i, w in enumerate(attn_w):
                sp.wait_ge(s["pt_full"], (B * HKV * GRP - 1) * STEPS + (i + 1) * (STEPS // PARTS))
                raw_weight_load(sp, prob, i, w, s["w_ld"])
            sp.wait_ge(s["w_ld"], B * HKV * 32 + len(attn_w) * RT * 16)

        @block.gpsimd
        def _(pool):
            for b in range(B):
                pool.wait_ge(s["mask_ld"], b * 16 + 16)
                for n in range(MASKS):
                    w = slice(n * S // MASKS, (n + 1) * S // MASKS)
                    nc.gpsimd.tensor_scalar(maskb[:, w], mask_u8[:, w], 1.0, -NEG, ALU.subtract, ALU.mult).then_inc(s["mask_ok"], 1)

        @block.scalar
        def _(act):
            def exp_piece(u, h, i):
                act.wait_ge(s["max_ready"], u + 1)
                p, r = i // RT, i % RT
                w = prob[:, r, p * PART:(p + 1) * PART]
                act.activation(w, w, ACT.Exp, bias=nmax[:, r:r + 1], accum_out=rs[:, h, r, p:p + 1]).then_inc(s["p_ready"], 1)

            def pt_high(u, k):
                act.wait_ge(s["pt_full"], u * STEPS + (k + 1))
                if k >= PT:
                    act.wait_ge(s["pv_done"], u * STEPS + (k - PT + 1))
                act.activation(pth[:, k % PT, :], tp[k % 2][:, :], ACT.Copy).then_inc(s["pt_hi"], 1)

            def o_out(u, g, h):
                act.wait_ge(wo_ld[h], g * 16 + 16)
                act.wait_ge(s["pv_done"], u * STEPS + STEPS - 2)
                act.activation(woh, wo_sb[:, h, :], ACT.Copy).then_inc(s["o_hi"], 1)
                act.wait_ge(s["pv_done"], u * STEPS + STEPS)
                act.activation(oh, ov[:, 0:TQ], ACT.Copy).then_inc(s["o_hi"], 1)

            def high(R, at, out):
                act.wait_ge(s["ring_full"], R + (at + 1))
                act.activation(out, ring[at % RING][:, :], ACT.Copy).then_inc(s["hi_ok"], 1)

            def weights_high(g):
                act.wait_ge(s["w_ld"], g * 32 + 32)
                act.activation(wh[:, :, :, :], wf[:, :, :, :], ACT.Copy).then_inc(s["w_hi"], 1)

            def group_work(b, j, first, last=False):
                g, R = group(b, j), items(b, j)
                act.wait_ge(s["q_ld"], g * 16 + 16)
                act.wait_ge(s["ring_full"], R)
                act.activation(qh[:, :, :], qf[:, :, :], ACT.Copy).then_inc(s["q_hi"], 1)
                for h in range(GRP):
                    u = g * GRP + (h - 1)
                    prev = h == 1 or not first
                    for n in range(SB):
                        if prev and n < EARLY:
                            exp_piece(u, (h + 1) % 2, n)
                        high(R, K_AT + n if h == 0 else v_item(n),
                             kh[:, n * BANK:(n + 1) * BANK] if h == 0 else vh[:, n * 4:(n + 1) * 4, :])
                    for k in range(STEPS):
                        if prev:
                            pt_high(u, k)
                            if k < 2 * (PIECES - EARLY) and k % 2:
                                exp_piece(u, (h + 1) % 2, EARLY + k // 2)
                            if h == 1 and k == SPLIT_AT and not last:
                                weights_high(g + 1)
                    if prev:
                        o_out(u, g if h else g - 1, (h + 1) % 2)

            weights_high(0)
            for b in range(B):
                for i in range(HEAD_ITEMS):
                    n = BLOCKS[i // CC]
                    high(b * BATCH_ITEMS, i, ctxh[:, i % CC, n * BANK:(n + 1) * BANK])
                group_work(b, 0, True)
                with act.Fori(1, HKV - (b == B - 1)) as j:
                    group_work(b, j, False)
                if b == B - 1:
                    group_work(b, HKV - 1, False, last=True)
                u = b * (HKV * GRP) + (HKV * GRP - 1)
                for i in range(RT):
                    exp_piece(u, 1, i)
                for k in range(STEPS):
                    pt_high(u, k)
                    if RT + k < PIECES:
                        exp_piece(u, 1, RT + k)
                o_out(u, b * HKV + (HKV - 1), 1)

        @block.vector
        def _(v):
            def low(at, count, out, high):
                v.wait_ge(s["hi_ok"], count)
                v.tensor_tensor(out, ring[at % RING][:, :], high.bitcast(F32), ALU.subtract).then_inc(s["ring_free"], 1)

            def scores_out(R, at, k, u):
                r, c = k % RT, k // RT
                v.wait_ge(s["ring_full"], R + (at + 1))
                v.sem_inc(s["scores_seen"], 1)
                v.tensor_tensor_reduce(prob[:, r, c * BANK:(c + 1) * BANK], ring[at % RING][:, :], maskb[:, c * BANK:(c + 1) * BANK],
                                       op0=ALU.add, op1=ALU.max, scale=1.0, scalar=NEG, accum_out=mx[:, r, c:c + 1]).then_inc(s["ring_free"], 1)
                if k == STEPS - 1:
                    v.wait_ge(s["ring_free"], R + (at + 1))
                    v.tensor_reduce(nmax[:, :], mx[:, :, :], op=ALU.max, axis=AX.X, negate=True).then_inc(s["max_ready"], 1)

            def pt_low(u, k):
                v.wait_ge(s["pt_hi"], u * STEPS + (k + 1))
                v.tensor_tensor(ptl[:, k % PT, :], tp[k % 2][:, :], pth[:, k % PT, :].bitcast(F32), ALU.subtract).then_inc(s["pt_lo"], 1)

            def o_low(u, h):
                v.wait_ge(s["o_hi"], u * 2 + 1)
                v.tensor_tensor(wol, wo_sb[:, h, :], woh.bitcast(F32), ALU.subtract)
                v.wait_ge(s["o_hi"], u * 2 + 2)
                v.tensor_tensor(ol, ov[:, 0:TQ], oh.bitcast(F32), ALU.subtract).then_inc(s["o_lo"], 1)

            def inverse(u, h):
                v.wait_ge(s["p_ready"], u * PIECES + PIECES)
                v.tensor_reduce(rinv[:, :], rs[:, h, :, :], op=ALU.add, axis=AX.X).then_inc(s["inv_chain"], 1)
                v.wait_ge(s["inv_chain"], u * 3 + 1)
                v.reciprocal(rinv[:, :], rinv[:, :]).then_inc(s["inv_chain"], 1)
                v.wait_ge(s["inv_chain"], u * 3 + 2)
                v.tensor_scalar(rinv[:, :], rinv[:, :], anyv[:, 0:1], None, ALU.mult).then_inc(s["inv_chain"], 1)
                v.wait_ge(s["inv_chain"], u * 3 + 3)

            def residual(b, u, r):
                v.wait_ge(s["op_full"], u * RT + (r + 1))
                w = X[:, bass.ds(b * RT + r, 1), :].rearrange("p o d -> p (o d)")
                v.scalar_tensor_tensor(w, op[:, :], rinv[:, r:r + 1], w, ALU.mult, ALU.add).then_inc(s["op_free"], 1)

            def any_part(b, n):
                v.tensor_reduce(anyp[:, n:n + 1], maskb[:, n * BANK:(n + 1) * BANK], op=ALU.max, axis=AX.X).then_inc(s["any_chain"], 1)

            def any_valid(b):
                v.wait_ge(s["any_chain"], b * (SB + 2) + SB)
                v.tensor_reduce(anyv[:, :], anyp[:, :], op=ALU.max, axis=AX.X).then_inc(s["any_chain"], 1)
                v.wait_ge(s["any_chain"], b * (SB + 2) + SB + 1)
                v.tensor_scalar(anyv[:, :], anyv[:, :], 0.0, None, ALU.is_ge).then_inc(s["any_chain"], 1)
                v.wait_ge(s["any_chain"], b * (SB + 2) + SB + 2)

            def vt_out(R, n):
                v.wait_ge(s["ring_full"], R + (vt_item(n) + 1))
                v.tensor_copy(vT[n % 2], ring[vt_item(n) % RING][:, :]).then_inc(s["ring_free"], 1)

            def v_low(b, j, n):
                low(v_item(n), highs(b, j) + (SB + n + 1), vl[:, n * 4:(n + 1) * 4, :].rearrange("p a b -> p (a b)"),
                    vh[:, n * 4:(n + 1) * 4, :].rearrange("p a b -> p (a b)"))

            def weights_low(g):
                v.wait_ge(s["w_hi"], g + 1)
                v.tensor_tensor(wl[:, :, :, :], wf[:, :, :, :], wh[:, :, :, :].bitcast(F32), ALU.subtract).then_inc(s["w_lo"], 1)

            def group_work(b, j, first, last=False):
                g, R = group(b, j), items(b, j)
                v.wait_ge(s["q_hi"], g + 1)
                v.tensor_tensor(ql[:, :, :], qf[:, :, :], qh[:, :, :].bitcast(F32), ALU.subtract).then_inc(s["q_lo"], 1)
                for h in range(GRP):
                    prev = h == 1 or not first
                    u = g * GRP + (h - 1)
                    done = g * GRP + (h - 2)
                    for n in range(SB):
                        if h == 0:
                            low(K_AT + n, highs(b, j) + (n + 1), kl[:, n * BANK:(n + 1) * BANK], kh[:, n * BANK:(n + 1) * BANK])
                        else:
                            vt_out(R, n)
                            if n >= 1:
                                v_low(b, j, n - 1)
                            if first:
                                any_part(b, n)
                        if not first:
                            if n == 0:
                                inverse(done, h)
                            if n in PROJECT_AT:
                                residual(b, done, PROJECT_AT.index(n))
                    if h == 1:
                        v_low(b, j, SB - 1)
                    if first and h == 1:
                        any_valid(b)
                    for k in range(STEPS):
                        if prev:
                            pt_low(u, k)
                        if h == 1 and k == SPLIT_AT and not last:
                            weights_low(g + 1)
                        if first and h == 0 and k >= 1 and (k - 1) % (STEPS // MASKS) == 0:
                            v.wait_ge(s["mask_ok"], b * MASKS + (k - 1) // (STEPS // MASKS) + 1)
                        if k >= 1:
                            scores_out(R, QK_AT[h] + k - 1, k - 1, g * GRP + h)
                    scores_out(R, QK_AT[h] + STEPS - 1, STEPS - 1, g * GRP + h)
                    if prev:
                        o_low(u, (h + 1) % 2)

            v.sem_inc(s["o_lo"], 1)
            v.sem_inc(s["op_free"], 1)
            weights_low(0)
            for b in range(B):
                for i in range(HEAD_ITEMS):
                    n = BLOCKS[i // CC]
                    w = (slice(None), i % CC, slice(n * BANK, (n + 1) * BANK))
                    low(i, b * BATCH_HIGHS + (i + 1), ctxl[w], ctxh[w])
                group_work(b, 0, True)
                with v.Fori(1, HKV - (b == B - 1)) as j:
                    group_work(b, j, False)
                if b == B - 1:
                    group_work(b, HKV - 1, False, last=True)
                u = b * (HKV * GRP) + (HKV * GRP - 1)
                inverse(u - 1, 0)
                for r in range(RT):
                    residual(b, u - 1, r)
                for k in range(STEPS):
                    pt_low(u, k)
                o_low(u, 1)
                inverse(u, 1)
                for r in range(RT):
                    residual(b, u, r)

        @block.tensor
        def _(pe):
            def project(u, r):
                if r == 0:
                    pe.wait_ge(s["o_lo"], u + 2)
                pe.wait_ge(s["op_free"], u * RT + (r + 1))
                for n, (o, w) in enumerate(((ol, woh), (oh, wol), (oh, woh))):
                    m = pe.matmul(op[:, :], o[:, r * P:(r + 1) * P], w, start=n == 0, stop=n == 2)
                m.then_inc(s["op_full"], 1)

            def free(R, at):
                pe.wait_ge(s["ring_free"], R + (at - RING + 1))

            def proj_item(R, at, w, n):
                free(R, at)
                cols = slice(n * BANK, (n + 1) * BANK)
                for i, (a, x, c) in enumerate((a, x, c) for a, x in ((wl, ctxh), (wh, ctxl), (wh, ctxh)) for c in range(CC)):
                    m = pe.matmul(ring[at % RING][:, :], a[:, w, c, :], x[:, c, cols], start=i == 0, stop=i == 3 * CC - 1)
                m.then_inc(s["ring_full"], 1)

            def turn_item(R, n):
                pe.wait_ge(s["ring_free"], R + (vt_item(n) + 1))
                free(R, v_item(n))
                for q in range(4):
                    m = pe.transpose(ring[v_item(n) % RING][:, q * P:(q + 1) * P], vT[n % 2][:, q * P:(q + 1) * P], ident[:, :])
                m.then_inc(s["ring_full"], 1)

            def score_item(R, h, k):
                r, c = k % RT, k // RT
                at = QK_AT[h] + k
                free(R, at)
                rows, cols = slice(r * P, (r + 1) * P), slice(c * BANK, (c + 1) * BANK)
                for n, (a, w) in enumerate(((ql, kh), (qh, kl), (qh, kh))):
                    m = pe.matmul(ring[at % RING][:, :], a[:, h, rows], w[:, cols], start=n == 0, stop=n == 2)
                m.then_inc(s["ring_full"], 1)

            def transposes(u, k):
                if 2 * k % (SCH // PARTS) == 0:
                    pe.wait_ge(s["p_ready"], u * PIECES + (2 * k // (SCH // PARTS) + 1) * RT)
                if k >= 2:
                    pe.wait_ge(s["pt_lo"], u * STEPS + (k - 1))
                for c in range(2):
                    for r in range(RT):
                        at = (c * RT + r) * P
                        m = pe.transpose(tp[k % 2][:, at:at + P], prob[:, r, (2 * k + c) * P:(2 * k + c + 1) * P], ident[:, :])
                m.then_inc(s["pt_full"], 1)

            def pv(u, k):
                pe.wait_ge(s["pt_lo"], u * STEPS + (k + 1))
                if k == 0:
                    pe.wait_ge(s["o_lo"], u + 1)
                for c in range(2):
                    for n, (a, w) in enumerate(((vh, ptl), (vl, pth), (vh, pth))):
                        m = pe.matmul(ov[:, 0:TQ], a[:, 2 * k + c, :], w[:, k % PT, c * TQ:(c + 1) * TQ],
                                      start=k == 0 and c == 0 and n == 0, stop=k == STEPS - 1 and c == 1 and n == 2)
                m.then_inc(s["pv_done"], 1)

            def group_work(b, j, first):
                g, R = group(b, j), items(b, j)
                pe.wait_ge(s["w_lo"], g + 1)
                for h in range(GRP):
                    prev = h == 1 or not first
                    u, done = g * GRP + (h - 1), g * GRP + (h - 2)
                    for n in range(SB):
                        proj_item(R, vt_item(n) if h else K_AT + n, h, n)
                        if h == 1 and n >= 1:
                            turn_item(R, n - 1)
                        if not first and n in PROJECT_AT:
                            project(done, PROJECT_AT.index(n))
                    if h == 1:
                        turn_item(R, SB - 1)
                    else:
                        pe.wait_ge(s["q_lo"], g + 1)
                    for k in range(STEPS):
                        if prev:
                            transposes(u, k)
                        score_item(R, h, k)
                        if prev and k >= LAG:
                            pv(u, k - LAG)
                    if prev:
                        for k in range(STEPS - LAG, STEPS):
                            pv(u, k)

            with pe.Fori(0, B) as b:
                for i in range(HEAD_ITEMS):
                    n = BLOCKS[i // CC]
                    if i % (CC * RT) == 0:
                        pe.wait_ge(ctx_ld[i // (CC * RT)], (b + 1) * (RT * 16))
                    if i >= RING:
                        pe.wait_ge(s["ring_free"], b * BATCH_ITEMS + (i - RING + 1))
                    for q in range(4):
                        m = pe.transpose(ring[i % RING][:, q * P:(q + 1) * P], cin[:, n * 4 + q, i % CC * P:(i % CC + 1) * P], ident[:, :])
                    m.then_inc(s["ring_full"], 1)
                group_work(b, 0, True)
                with pe.Fori(1, HKV) as j:
                    group_work(b, j, False)
                g = b * HKV + (HKV - 1)
                u = g * GRP + 1
                for r in range(RT):
                    project(u - 1, r)
                for k in range(STEPS + LAG):
                    if k < STEPS:
                        transposes(u, k)
                    if k >= LAG:
                        pv(u, k - LAG)
                for r in range(RT):
                    project(u, r)


def selfattn(nc, a, X, ident, prob):
    HW = 32
    HC = P // HW
    N = B * KC
    U = N * RT
    BANKS = RT + 1
    with ExitStack() as ctx:
        t = Tensors(nc, ctx, "att")
        ln = ln_scratch(t)
        xn = t.sb("xn", [P, TT, D])
        xh, xl = t.sb("xh", [P, KC, B * TQ], F32R), t.sb("xl", [P, KC, B * TQ], F32R)
        wTh, wTl = ([t.sb(f"{n}{i}", [P, KC, D], F32R) for i in range(3)] for n in ("wTh", "wTl"))
        woT = t.sb("woT", [P, KC, D])
        bias_rows = t.sb("bias_rows", [2 * KC, P])
        bias_cols = t.sb("bias_cols", [P, 2 * KC])
        vo_bias = t.sb("vo_bias", [P, 2, D])
        qz = t.sb("qz", [P, N, HC, TQ])
        kT = t.sb("kT", [P, N, TQ])
        V = t.sb("V", [P, N, RT, P])
        decay = t.sb("decay", [P, RT, TQ])
        ks = [t.sb(f"ks{i}", [P, P]) for i in range(RT)]
        vs = [t.sb(f"vs{i}", [P, i + 1, P]) for i in range(RT)]
        sc = [t.sb(f"sc{i}", [P, HC, (i + 1) * P]) for i in range(RT)]
        mx = [t.sb(f"mx{i}", [P, HC]) for i in range(RT)]
        nmax = [t.sb(f"nmax{i}", [P, HC]) for i in range(RT)]
        rsum = [t.sb(f"rsum{i}", [P, HC]) for i in range(RT)]
        cT = [t.sb(f"cT{i}", [P, i + 1, HC * P]) for i in range(RT)]
        oT = t.sb("oT", [P, N, TQ])
        bank = [t.ps(f"bank{i}") for i in range(8)]
        s_ps = (bank[0:1], bank[1:3])
        t_ps = (bank[3:4], bank[4:6])
        o_ps = bank[6:8]
        names = ("var_ready", "root_ready", "xn_ready", "chain", "consts", "b_ld", "vo_ld", "xT_ps", "xT_hi", "xT_lo", "wT_ps", "wT_hi", "wT_ok",
                 "bias_ps", "bias_ok", "q_ps", "q_ok", "k_ps", "k_ok", "v_ps", "v_ok", "xb_ok", "ks_ok", "vs_ok", "s_ps", "s_seen", "s_ok", "max_ok",
                 "exp_ok", "inv_ok", "norm_ok", "norm2_ok", "t_ps", "cT_ok", "o_ps", "o_ok", "out_ps", "out_ok", "pool_seen")
        s = {n: t.sem(n) for n in names}
        wo_ld = t.sem("wo_ld")
        block = ctx.enter_context(nc.Block())

        def parts(n, it):
            heads = HC // (it + 1)
            return [(slice(j * heads, (j + 1) * heads), n * BANKS + (it + j + 1)) for j in range(it + 1)]

        @block.sync
        def _(sp):
            for j, m in enumerate(("q", "k")):
                sp.dma_start(bias_rows[j * KC:(j + 1) * KC, :], a[f"L0_attn_{m}_b"].rearrange("(c p) -> c p", p=P)).then_inc(s["b_ld"], 16)
            raw_weight_load(sp, prob, 3, a["L0_attn_o_w"], wo_ld)
            for i, n in enumerate(("v", "o")):
                sp.dma_start(vo_bias[:, i, :], a[f"L0_attn_{n}_b"].rearrange("(o d) -> o d", o=1).to_broadcast([P, D])).then_inc(s["vo_ld"], 16)

        @block.gpsimd
        def _(pool):
            c = s["consts"]
            nc.gpsimd.memset(qz[:, :, :, :], 0.0).then_inc(c, 1)
            nc.gpsimd.iota(decay[:, :, :], pattern=[[-P, RT], [1, TQ]], base=0, channel_multiplier=-1, allow_small_or_imprecise_dtypes=True).then_inc(c, 1)
            pool.wait_ge(c, 2)
            nc.gpsimd.affine_select(out=decay[:, :, :], in_=decay[:, :, :], compare_op=ALU.is_ge, fill=NEG,
                                    base=0, pattern=[[P, RT], [-1, TQ]], channel_multiplier=1).then_inc(c, 1)
            pool.wait_ge(s["vo_ld"], 32)
            pool.wait_ge(s["xn_ready"], 1)
            nc.gpsimd.tensor_tensor(X[:, :, :], X[:, :, :], vo_bias[:, 1:2, :].to_broadcast([P, TT, D]), ALU.add).then_inc(s["xb_ok"], 1)

            def keys(n, it):
                nc.gpsimd.tensor_copy(ks[it][:, :], kT[:, bass.ds(n, 1), it * P:(it + 1) * P].rearrange("p o j -> p (o j)")).then_inc(s["ks_ok"], 1)

            def values(n, it, first):
                if not first:
                    pool.wait_ge(s["o_ps"], n * RT + (it - 1))
                    pool.sem_inc(s["pool_seen"], 1)
                nc.gpsimd.tensor_copy(vs[it][:, :, :], V[:, bass.ds(n, 1), 0:it + 1, :].rearrange("p o r j -> p (o r) j")).then_inc(s["vs_ok"], 1)

            def normalise(n, it):
                for hs, done in parts(n, it)[:1]:
                    pool.wait_ge(s["inv_ok"], done)
                    pool.sem_inc(s["pool_seen"], 1)
                    w = sc[it][:, hs, :]
                    nc.gpsimd.tensor_tensor(w, w, rsum[it][:, hs].unsqueeze(2).to_broadcast([P, HC // (it + 1), (it + 1) * P]), ALU.mult).then_inc(s["norm_ok"], 1)

            def steps(n, first, last):
                for it in range(RT):
                    if not last:
                        keys(n + 1, it)
                    values(n, it, first)
                    if it == 0:
                        normalise(n, 1)
                    elif not last:
                        normalise(n + 1, 0)

            pool.wait_ge(s["k_ok"], KC)
            keys(0, 0)
            keys(0, 1)
            normalise(0, 0)
            pool.wait_ge(s["v_ok"], TT)
            steps(0, True, False)
            with pool.Fori(1, N - 1) as n:
                steps(n, False, False)
            steps(N - 1, False, True)

        @block.vector
        def _(v):
            ch = Chain(v, s["chain"])

            def weight(i):
                w, c = i // KC, i % KC
                if w < 3:
                    v.wait_ge(s["wT_hi"], i + 1)
                    v.tensor_tensor(wTl[w][:, c, :], bank[i % 4][:, :], wTh[w][:, c, :].bitcast(F32), ALU.subtract).then_inc(s["wT_ok"], 1)
                else:
                    v.wait_ge(s["wT_ps"], i + 1)
                    v.tensor_copy(woT[:, c, :], bank[i % 4][:, :]).then_inc(s["wT_ok"], 1)

            ln_vector(v, ch, X, xn, ln, s["root_ready"], s["var_ready"])
            v.engine_nop().then_inc(s["xn_ready"], 1)
            for i in range(2 * KC):
                weight(i)
            v.wait_ge(s["bias_ps"], 1)
            v.tensor_copy(bias_cols[:, :], bank[4][:, 0:2 * KC]).then_inc(s["bias_ok"], 1)
            for c in range(KC):
                v.wait_ge(s["xT_hi"], c + 1)
                v.tensor_tensor(xl[:, c, :], bank[4 + c][:, :], xh[:, c, :].bitcast(F32), ALU.subtract).then_inc(s["xT_lo"], 1)
            v.wait_ge(s["bias_ok"], 1)
            v.wait_ge(s["consts"], 3)
            for c in range(KC):
                v.wait_ge(s["q_ps"], c + 1)
                for h in range(HC):
                    w = slice(h * HW, (h + 1) * HW)
                    m = v.tensor_scalar(qz.rearrange("p (b c) h n -> p c h b n", b=B)[w, c, h], bank[c][w, :].rearrange("p (b n) -> p b n", b=B),
                                        bias_cols[w, c:c + 1], HW ** -0.5, ALU.add, ALU.mult)
                m.then_inc(s["q_ok"], 1)
            for i in range(2 * KC, 4 * KC):
                weight(i)
            def scores(n, it):
                J = (it + 1) * P
                for j, (hs, done) in enumerate(parts(n, it)):
                    v.wait_ge(s["s_ps"], done)
                    v.sem_inc(s["s_seen"], 1)
                    for h in range(hs.start, hs.stop):
                        at = (h - hs.start) * J
                        m = v.tensor_tensor_reduce(sc[it][:, h, :], s_ps[it][j][:, at:at + J], decay[:, it, 0:J],
                                                   op0=ALU.add, op1=ALU.max, scale=1.0, scalar=NEG, accum_out=mx[it][:, h:h + 1])
                    m.then_inc(s["s_ok"], 1)
                    v.wait_ge(s["s_ok"], done)
                    v.tensor_scalar(nmax[it][:, hs], mx[it][:, hs], -1.0, None, ALU.mult).then_inc(s["max_ok"], 1)

            def inverse(n, it):
                for hs, done in parts(n, it):
                    v.wait_ge(s["exp_ok"], done)
                    v.reciprocal(rsum[it][:, hs], rsum[it][:, hs]).then_inc(s["inv_ok"], 1)
                if it == 1:
                    v.wait_ge(s["inv_ok"], done)
                    w = sc[it][:, hs, :]
                    v.tensor_tensor(w, w, rsum[it][:, hs].unsqueeze(2).to_broadcast([P, HC // 2, 2 * P]), ALU.mult).then_inc(s["norm2_ok"], 1)

            def outputs(n, it):
                v.wait_ge(s["o_ps"], n * RT + (it + 1))
                for h in range(HC):
                    w = slice(h * HW, (h + 1) * HW)
                    m = v.tensor_copy(oT[w, bass.ds(n, 1), it * P:(it + 1) * P].rearrange("p o j -> p (o j)"), o_ps[it][w, h * P:(h + 1) * P])
                m.then_inc(s["o_ok"], 1)

            def steps(n, first, last):
                for it in range(RT):
                    if it == 0:
                        inverse(n, 1)
                    elif not last:
                        inverse(n + 1, 0)
                    if not last:
                        scores(n + 1, it)
                    if it == 1:
                        outputs(n, 0)
                    elif not first:
                        outputs(n - 1, 1)

            scores(0, 0)
            scores(0, 1)
            inverse(0, 0)
            v.wait_ge(s["vo_ld"], 32)
            for i in range(TT):
                v.wait_ge(s["v_ps"], i + 1)
                v.tensor_tensor(V.rearrange("p (b c) r n -> p b r c n", b=B)[:, i // RT, i % RT], bank[4 + i][:, :].rearrange("p (c n) -> p c n", c=KC),
                                vo_bias[:, 0, :].rearrange("p (c n) -> p c n", c=KC), ALU.add).then_inc(s["v_ok"], 1)
            steps(0, True, False)
            with v.Fori(1, N - 1) as n:
                steps(n, False, False)
            steps(N - 1, False, True)
            outputs(N - 1, 1)
            v.wait_ge(s["xb_ok"], 1)
            for i in range(TT):
                v.wait_ge(s["out_ps"], i + 1)
                v.tensor_tensor(X[:, i, :], X[:, i, :], bank[i][:, :], ALU.add).then_inc(s["out_ok"], 1)

        @block.scalar
        def _(act):
            act.activation(ln["table"][:, :], ident[:, 0:1], ACT.Sqrt)
            act.wait_ge(s["var_ready"], 1)
            act.activation(ln["root"][:, :], ln["veps"][:, :], ACT.Sqrt).then_inc(s["root_ready"], 1)

            def weight(i):
                act.wait_ge(s["wT_ps"], i + 1)
                act.activation(wTh[i // KC][:, i % KC, :], bank[i % 4][:, :], ACT.Copy).then_inc(s["wT_hi"], 1)

            for i in range(2 * KC):
                weight(i)
            for c in range(KC):
                act.wait_ge(s["xT_ps"], c + 1)
                act.activation(xh[:, c, :], bank[4 + c][:, :], ACT.Copy).then_inc(s["xT_hi"], 1)
            act.wait_ge(s["bias_ok"], 1)
            for c in range(KC):
                act.wait_ge(s["k_ps"], c + 1)
                act.activation(kT.rearrange("p (b c) n -> p c b n", b=B)[:, c], bank[4 + c][:, :].rearrange("p (b n) -> p b n", b=B),
                               ACT.Identity, bias=bias_cols[:, KC + c:KC + c + 1]).then_inc(s["k_ok"], 1)
            for i in range(2 * KC, 3 * KC):
                weight(i)

            def softmax(n, it):
                for hs, done in parts(n, it):
                    act.wait_ge(s["max_ok"], done)
                    for h in range(hs.start, hs.stop):
                        w = sc[it][:, h, :]
                        m = act.activation(w, w, ACT.Exp, bias=nmax[it][:, h:h + 1], accum_out=rsum[it][:, h:h + 1])
                    m.then_inc(s["exp_ok"], 1)

            def turned(n, it):
                for j in range(it + 1):
                    act.wait_ge(s["t_ps"], n * BANKS + (it + j + 1))
                    act.activation(cT[it][:, j, :], t_ps[it][j][:, :], ACT.Copy).then_inc(s["cT_ok"], 1)

            def steps(n, last):
                for it in range(RT):
                    turned(n, it)
                    if not last:
                        softmax(n + 1, it)

            softmax(0, 0)
            softmax(0, 1)
            with act.Fori(0, N - 1) as n:
                steps(n, False)
            steps(N - 1, True)

        @block.tensor
        def _(pe):
            def weight(i):
                w, c = i // KC, i % KC
                if i == 3 * KC:
                    pe.wait_ge(wo_ld, RT * 16)
                if i % (2 * KC) >= 4:
                    pe.wait_ge(s["wT_ok"], i - 3)
                for o in range(KC):
                    m = pe.transpose(bank[i % 4][:, o * P:(o + 1) * P], raw_weight(prob, w, o)[:, c * P:(c + 1) * P], ident[:, :])
                m.then_inc(s["wT_ps"], 1)

            for i in range(2 * KC):
                weight(i)
            pe.wait_ge(s["b_ld"], 32)
            pe.matmul(bank[4][:, 0:2 * KC], bias_rows[:, :], ident[0:2 * KC, 0:2 * KC], start=True, stop=True).then_inc(s["bias_ps"], 1)
            pe.wait_ge(s["xn_ready"], 1)
            pe.wait_ge(s["bias_ok"], 1)
            for c in range(KC):
                for i in range(TT):
                    m = pe.transpose(bank[4 + c][:, i * P:(i + 1) * P], xn[:, i, c * P:(c + 1) * P], ident[:, :])
                m.then_inc(s["xT_ps"], 1)
            pe.wait_ge(s["xT_lo"], KC)
            pe.wait_ge(s["wT_ok"], 2 * KC)
            for base, w, done in ((0, 0, "q_ps"), (4, 1, "k_ps")):
                for o in range(KC):
                    for n, (wt, y, c) in enumerate((wt, y, c) for wt, y in ((wTl, xh), (wTh, xl), (wTh, xh)) for c in range(KC)):
                        m = pe.matmul(bank[base + o][:, :], wt[w][:, c, o * P:(o + 1) * P], y[:, c, :], start=n == 0, stop=n == 3 * KC - 1)
                    m.then_inc(s[done], 1)
            for i in range(2 * KC, 4 * KC):
                if i < 3 * KC:
                    pe.wait_ge(s["q_ok"], i - 2 * KC + 1)
                weight(i)
            def scores(n, it, first):
                pe.wait_ge(s["ks_ok"], n * RT + (it + 1))
                for k, (hs, done) in enumerate(parts(n, it)):
                    if not first:
                        pe.wait_ge(s["s_ok"], done - BANKS)
                    pe.matmul(s_ps[it][k][:, :], ks[it][:, :], qz[:, bass.ds(n, 1), hs, 0:(it + 1) * P].rearrange("p o h j -> p (o h) j"),
                              start=True, stop=True).then_inc(s["s_ps"], 1)

            def transposes(n, it, first):
                pe.wait_ge(s["norm_ok"], n * RT + (it + 1))
                if it == 1:
                    pe.wait_ge(s["norm2_ok"], n + 1)
                for j in range(it + 1):
                    if not first:
                        pe.wait_ge(s["cT_ok"], n * BANKS - BANKS + (it + j + 1))
                    for h in range(HC):
                        m = pe.transpose(t_ps[it][j][:, h * P:(h + 1) * P], sc[it][:, h, j * P:(j + 1) * P], ident[:, :])
                    m.then_inc(s["t_ps"], 1)

            def values(n, it, first):
                pe.wait_ge(s["cT_ok"], n * BANKS + (2 * it + 1))
                pe.wait_ge(s["vs_ok"], n * RT + (it + 1))
                if not first:
                    pe.wait_ge(s["o_ok"], n * RT + (it - 1))
                for j in range(it + 1):
                    m = pe.matmul(o_ps[it][:, :], vs[it][:, j, :], cT[it][:, j, :], start=j == 0, stop=j == it)
                m.then_inc(s["o_ps"], 1)

            def steps(n, first, second, last):
                for it in range(RT):
                    transposes(n, it, first)
                    if not last:
                        scores(n + 1, it, False)
                    if it == 1:
                        values(n, 0, first)
                    elif not first:
                        values(n - 1, 1, second)

            pe.wait_ge(s["q_ok"], KC)
            pe.wait_ge(s["wT_ok"], 4 * KC)
            scores(0, 0, True)
            scores(0, 1, True)
            for i in range(TT):
                pe.wait_ge(s["k_ok"], i + 1)
                for n, (y, wt, c) in enumerate((y, wt, c) for y, wt in ((xl, wTh), (xh, wTl), (xh, wTh)) for c in range(KC)):
                    m = pe.matmul(bank[4 + i][:, :], y[:, c, i * P:(i + 1) * P], wt[2][:, c, :], start=n == 0, stop=n == 3 * KC - 1)
                m.then_inc(s["v_ps"], 1)
            pe.wait_ge(s["v_ok"], TT)
            steps(0, True, False, False)
            steps(1, False, True, False)
            with pe.Fori(2, N - 1) as n:
                steps(n, False, False, False)
            steps(N - 1, False, False, True)
            values(N - 1, 1, False)
            for i in range(TT):
                pe.wait_ge(s["o_ok"], (i // RT + 1) * (U // B))
                for c in range(KC):
                    m = pe.matmul(bank[i][:, :], oT[:, i // RT * KC + c, i % RT * P:(i % RT + 1) * P], woT[:, c, :], start=c == 0, stop=c == KC - 1)
                m.then_inc(s["out_ps"], 1)


def experts(nc, a, out, X, ident):
    E, K = 8, 2
    CAP = int(B * TQ * 1.25 / E)
    SL = K * CAP
    F = 4 * D
    FC = F // P
    R = 32
    STRIDE = 1024
    SB1 = E * KC
    PG = 4
    LG_AT = 256
    OUT_ORDER = (2, 3, 0, 1)
    LOWEST = -87.5
    with ExitStack() as ctx:
        t = Tensors(nc, ctx, "moe")
        w1 = [t.sb(f"w1_{i}", [P, KC, F]) for i in range(2)]
        w2_1 = t.sb("w2_1", [P, FC, D])
        wd = [t.sb(f"wd_{i}", [P, KC, R]) for i in range(2)]
        wu = [t.sb(f"wu_{i}", [R, D]) for i in range(2)]
        gate = t.sb("gate", [P, KC, E])
        xh, xl = t.sb("xh", [P, TT, D], F32R), t.sb("xl", [P, TT, D], F32R)
        sb2 = t.sb("sb2", [P, D])
        b1_cols, b_cols = t.sb("b1_cols", [P, P]), t.sb("b_cols", [P, SB1 + FC])
        prob = t.sb("prob", [P, TT, E])
        lg = t.sb("lg", [P, TT, E])
        small = t.sb("small", [P, TT])
        top, topp = t.sb("top", [P, TT, 8]), t.sb("topp", [P, TT, 8])
        topi, topf = t.sb("topi", [P, TT, 8], U32), t.sb("topf", [P, TT, 8])
        onehot = t.sb("onehot", [P, TT, K, E])
        cnt = t.sb("cnt", [P, TT, K, E])
        ids = t.sb("ids", [P, TT, K])
        tri, all1 = t.sb("tri", [P, P]), t.sb("all1", [P, P])
        iota8, iotaS = t.sb("iota8", [P, E]), t.sb("iotaS", [P, CAP])
        ecol = t.sb("ecol", [P, E])
        rows = t.sb("rows", [CAP, K, B * TQ])
        sel = t.sb("sel", [P, TT, 2 * SL], F32R)
        bufT = t.sb("bufT", [P, 2, KC, SL])
        rT = t.sb("rT", [R, SL])

        bank = [t.ps(f"bank{i}") for i in range(8)]
        h_ps, y_ps, t_ps, c_ps = bank[0:2], bank[2:4], bank[4:6], bank[6:8]

        names = ("consts", "chain", "var_ready", "root_ready", "xn_ready", "rows_ld", "gate_ld", "xT_ps", "xT_ok", "xT_lo", "x_hi", "bT_ps", "bT_ok",
                 "lgT_ps", "lgT_ok", "lg_ps", "lm_ok", "exp_ok", "oh_ok", "cnt_ps", "ids_ok", "rows_ps", "rows_ok",
                 "s1_hi", "s1_lo", "s2_hi", "s2_lo", "sh_ps", "sh_ok", "sh_hi", "sh_lo", "s2_ps", "sad_ld", "sr_ps", "sr_ok", "so_ps", "so_ok",
                 "sel_ok", "g_ps", "g_ok", "h_ps", "h_ok", "r_ps", "r_ok", "y_ps", "y_ok", "yt_ps", "yt_hi", "yt_lo", "comb_ok", "c_ps", "c_ok", "stored")
        s = {n: t.sem(n) for n in names}
        w1_ld, w2_ld, ad_ld = ([t.sem(f"{n}{i}") for i in range(2)] for n in ("w1_ld", "w2_ld", "ad_ld"))
        sw_ld = [t.sem(f"sw_ld{i}") for i in range(3)]

        with ExitStack() as first:
            f = Tensors(nc, first, "sh")
            xn = f.sb("xn", [P, TT, D])
            xnT = f.sb("xnT", [P, KC, B * TQ])
            xTh, xTl = f.sb("xTh", [P, KC, B * TQ], F32R), f.sb("xTl", [P, KC, B * TQ], F32R)
            s1h, s1l = ([f.sb(f"{n}{i}", [P, KC, P], F32R) for i in range(2)] for n in ("s1h", "s1l"))
            s2h, s2l = ([f.sb(f"{n}{i}", [P, D], F32R) for i in range(2)] for n in ("s2h", "s2l"))
            hf = [f.sb(f"hf{i}", [P, B * TQ]) for i in range(2)]
            hh, hl = ([f.sb(f"{n}{i}", [P, B * TQ], F32R) for i in range(2)] for n in ("hh", "hl"))
            ln = ln_scratch(f)
            b1_rows, b_rows = f.sb("b1_rows", [P, P]), f.sb("b_rows", [SB1 + FC, P])
        lgT = rows[0:E, 0, :]
        rS = bufT[0:R, 0, :, :].rearrange("p c n -> p (c n)")[:, 0:B * TQ]
        second = ctx.enter_context(ExitStack())
        f = Tensors(nc, second, "ex")
        w2 = [f.sb("w2_0", [P, FC, D]), w2_1]
        hT = f.sb("hT", [P, FC, SL])
        yT = f.sb("yT", [P, KC, SL])
        yh, yl = f.sb("yh", [CAP, K, D], F32R), f.sb("yl", [CAP, K, D], F32R)
        comb = f.sb("comb", [CAP, K, B * TQ], F32R)
        block = ctx.enter_context(nc.Block())

        @block.sync
        def _(sp):
            sp.dma_start(gate[:, :, :], a["L0_ffn_gate_w"].rearrange("(c p) e -> p c e", p=P)).then_inc(s["gate_ld"], 16)
            for g in range(FC // PG):
                w = slice(g * PG * P, (g + 1) * PG * P)
                sp.dma_start(w1[1][:, :, w], a["L0_ffn_sw1"][:, w].rearrange("(c p) n -> p c n", p=P)).then_inc(sw_ld[min(g, 2)], 16)
                sp.dma_start(w2[1][:, g * PG:(g + 1) * PG, :], a["L0_ffn_sw2"][w, :].rearrange("(c p) n -> p c n", p=P)).then_inc(sw_ld[min(g, 2)] if g else s["sad_ld"], 16)
                if g == 0:
                    sp.dma_start(wd[1][:, :, :], a["L0_ffn_swd"].rearrange("(c p) r -> p c r", p=P)).then_inc(s["sad_ld"], 16)
                    sp.dma_start(wu[1][:, :], a["L0_ffn_swu"]).then_inc(s["sad_ld"], 16)

            def expert_loads(e, i):
                for c in range(KC):
                    sp.dma_start(w1[i][:, c, :], a["L0_ffn_w1"][bass.ds(e, 1), c * P:(c + 1) * P, :].rearrange("o p n -> (o p) n")).then_inc(w1_ld[i], 16)
                sp.dma_start(wd[i][:, :, :], a["L0_ffn_wd"][bass.ds(e, 1), :, :].rearrange("o (c p) r -> p (o c) r", p=P)).then_inc(ad_ld[i], 16)
                sp.dma_start(wu[i][:, :], a["L0_ffn_wu"][bass.ds(e, 1), :, :].rearrange("o r n -> (o r) n")).then_inc(ad_ld[i], 16)

            def expert_loads2(e, i):
                for c in range(4):
                    sp.dma_start(w2[i][:, c * 4:(c + 1) * 4, :],
                                 a["L0_ffn_w2"][bass.ds(e, 1), c * 4 * P:(c + 1) * 4 * P, :].rearrange("o (c p) n -> p (o c) n", p=P)).then_inc(w2_ld[i], 16)

            expert_loads(0, 0)
            sp.wait_ge(s["x_hi"], 2)
            sp.wait_ge(s["sh_ps"], FC)
            expert_loads2(0, 0)
            sp.wait_ge(s["s1_lo"], FC)
            sp.wait_ge(s["s2_lo"], FC)
            sp.wait_ge(s["so_ps"], TT)
            expert_loads(1, 1)
            expert_loads2(1, 1)
            with sp.Fori(0, (E - 2) // 2) as m:
                for q in range(2):
                    e = m * 2 + q
                    sp.wait_ge(s["y_ps"], e * 2 + 2)
                    expert_loads(e + 2, q)
                    expert_loads2(e + 2, q)
            for i in range(TT):
                sp.wait_ge(s["c_ok"], E * K * TT - TT + i + 1)
                sp.dma_start(out[i // RT, i % RT * P:(i % RT + 1) * P, :], X[:, i, :]).then_inc(s["stored"], 16)
            sp.wait_ge(s["stored"], TT * 16)

        @block.gpsimd
        def _(pool):
            c = s["consts"]
            nc.gpsimd.memset(all1[:, :], 1.0).then_inc(c, 1)
            nc.gpsimd.memset(tri[:, :], 1.0).then_inc(c, 1)
            nc.gpsimd.iota(iota8[:, :], pattern=[[1, E]], base=0, channel_multiplier=0, allow_small_or_imprecise_dtypes=True).then_inc(c, 1)
            nc.gpsimd.iota(iotaS[:, :], pattern=[[1, CAP]], base=1, channel_multiplier=0, allow_small_or_imprecise_dtypes=True).then_inc(c, 1)
            nc.gpsimd.iota(ecol[:, :], pattern=[[STRIDE, E]], base=1, channel_multiplier=1, allow_small_or_imprecise_dtypes=True).then_inc(c, 1)
            pool.wait_ge(c, 5)
            nc.gpsimd.affine_select(out=tri[:, :], in_=tri[:, :], compare_op=ALU.is_ge, fill=0.0,
                                    base=0, pattern=[[1, P]], channel_multiplier=-1).then_inc(c, 1)
            pool.wait_ge(s["rows_ld"], 64)
            nc.gpsimd.tensor_scalar(sb2[:, :], sb2[:, :], 0.2, None, ALU.mult).then_inc(c, 1)
            pool.wait_ge(c, 7)
            pool.wait_ge(s["xn_ready"], 1)
            nc.gpsimd.tensor_tensor(X[:, :, :], X[:, :, :], sb2[:, :].unsqueeze(1).to_broadcast([P, TT, D]), ALU.add).then_inc(c, 1)

        @block.vector
        def _(v):
            ch = Chain(v, s["chain"])
            ln_vector(v, ch, X, xn, ln, s["root_ready"], s["var_ready"])
            v.engine_nop().then_inc(s["xn_ready"], 1)
            for c in range(KC):
                v.wait_ge(s["xT_ok"], c + 1)
                v.tensor_tensor(xTl[:, c, :], bank[c][:, :], xTh[:, c, :].bitcast(F32), ALU.subtract).then_inc(s["xT_lo"], 1)
            v.wait_ge(s["bT_ps"], 2)
            v.tensor_copy(b1_cols[:, :], bank[7][:, 0:P]).then_inc(s["bT_ok"], 1)
            v.tensor_copy(b_cols[:, :], bank[7][:, P:P + SB1 + FC]).then_inc(s["bT_ok"], 1)

            def first_low(n, q):
                v.wait_ge(s["s1_hi"], n + 1)
                v.tensor_tensor(s1l[q][:, :, :], w1[1][:, :, bass.ds(n * P, P)], s1h[q][:, :, :].bitcast(F32), ALU.subtract).then_inc(s["s1_lo"], 1)

            def second_low(n, q):
                v.wait_ge(s["s2_hi"], n + 1)
                v.tensor_tensor(s2l[q][:, :], w2[1][:, bass.ds(n, 1), :].rearrange("p o n -> p (o n)"), s2h[q][:, :].bitcast(F32), ALU.subtract).then_inc(s["s2_lo"], 1)

            def shared(n, q, left):
                v.wait_ge(s["sh_hi"], n + 1)
                v.tensor_tensor(hl[q][:, :], hf[q][:, :], hh[q][:, :].bitcast(F32), ALU.subtract).then_inc(s["sh_lo"], 1)
                if left > 2:
                    first_low(n + 2, q)
                if left > 1:
                    second_low(n + 1, 1 - q)

            first_low(0, 0)
            v.wait_ge(s["lgT_ps"], 1)
            v.tensor_copy(lgT, bank[6][0:E, :]).then_inc(s["lgT_ok"], 1)
            first_low(1, 1)
            second_low(0, 0)
            v.wait_ge(s["consts"], 6)
            v.wait_ge(s["lg_ps"], 1)
            ch.link(v.tensor_copy(lg[:, :, :], bank[7][:, LG_AT:LG_AT + TT * E].rearrange("p (i e) -> p i e", e=E)))
            ch.link(v.tensor_reduce(small[:, :], lg[:, :, :], op=ALU.max, axis=AX.X))
            ch.link(v.tensor_tensor(lg[:, :, :], lg[:, :, :], small[:, :].unsqueeze(2).to_broadcast([P, TT, E]), ALU.subtract))
            ch.link(v.tensor_scalar(lg[:, :, :], lg[:, :, :], LOWEST, None, ALU.max))
            for i in range(TT):
                v.max(top[:, i, :], lg[:, i, :]).then_inc(s["chain"], 1)
            ch.n += TT
            v.wait_ge(s["chain"], ch.n)
            for i in range(TT):
                v.max_index(topi[:, i, :], top[:, i, :], lg[:, i, :]).then_inc(s["lm_ok"], 1)
            v.wait_ge(s["lm_ok"], TT)
            ch.link(v.tensor_copy(topf[:, :, :], topi[:, :, :]))
            for i in range(TT):
                for k in range(K):
                    v.tensor_scalar(onehot[:, i, k, :], iota8[:, :], topf[:, i, k:k + 1], None, ALU.is_equal).then_inc(s["oh_ok"], 1)
            shared(0, 0, FC)
            shared(1, 1, FC - 1)
            v.wait_ge(s["exp_ok"], 2)
            ch.link(v.tensor_reduce(small[:, :], prob[:, :, :], op=ALU.add, axis=AX.X))
            ch.link(v.reciprocal(small[:, :], small[:, :]))
            ch.link(v.tensor_tensor(topp[:, :, :], topp[:, :, :], small[:, :].unsqueeze(2).to_broadcast([P, TT, 8]), ALU.mult))
            v.wait_ge(s["cnt_ps"], 1)
            ch.link(v.tensor_tensor(cnt[:, :, :, :].rearrange("p i k e -> p (i k e)"), bank[7][:, 0:TT * K * E],
                                    onehot[:, :, :, :].rearrange("p i k e -> p (i k e)"), ALU.mult))
            v.wait_ge(s["oh_ok"], TT * K)
            v.tensor_reduce(ids[:, :, :].rearrange("p i k -> p (i k)"), cnt[:, :, :, :].rearrange("p i k e -> p (i k) e"), op=ALU.add, axis=AX.X).then_inc(s["chain"], 1)
            ch.n += 1
            v.wait_ge(s["chain"], ch.n)
            v.scalar_tensor_tensor(ids[:, :, :], topf[:, :, 0:K], float(STRIDE), ids[:, :, :], ALU.mult, ALU.add).then_inc(s["ids_ok"], 1)

            def select(p):
                for j, k, i in ((j, k, i) for j in range(2) for k in range(K) for i in range(TT)):
                    at = j * SL + k * CAP
                    m = v.tensor_scalar(sel[:, i, at:at + CAP], iotaS[:, :], cnt[:, i, k, bass.ds(p * 2 + j, 1)], None, ALU.is_equal)
                m.then_inc(s["sel_ok"], 1)

            def combine(e):
                for k in range(K):
                    m = v.tensor_scalar(comb[:, k, :], rows[:, k, :], ecol[0:CAP, bass.ds(e, 1)], None, ALU.is_equal)
                m.then_inc(s["comb_ok"], 1)

            for n in range(2, 6):
                shared(n, n % 2, FC - n)
                if n >= 4:
                    v.wait_ge(s["rows_ps"], n - 3)
                    v.tensor_copy(rows[:, n - 4, :], bank[7][0:CAP, :]).then_inc(s["rows_ok"], 1)
            v.wait_ge(s["x_hi"], 1)
            v.tensor_tensor(xl[:, :, :], xn[:, :, :], xh[:, :, :].bitcast(F32), ALU.subtract).then_inc(s["x_hi"], 1)
            with v.Fori(3, FC // 2 - 1) as m:
                for q in range(2):
                    shared(m * 2 + q, q, FC)
            shared(FC - 2, 0, 2)
            shared(FC - 1, 1, 1)
            select(0)
            v.wait_ge(s["consts"], 8)
            for n, i in enumerate(OUT_ORDER):
                v.wait_ge(s["so_ps"], n + 1)
                v.scalar_tensor_tensor(X[:, i, :], bank[2 + i][:, :], 0.2, X[:, i, :], ALU.mult, ALU.add).then_inc(s["so_ok"], 1)
            v.wait_ge(s["rows_ok"], K)

            def turned(e):
                for k in range(K):
                    v.wait_ge(s["yt_hi"], e * K + (k + 1))
                    v.tensor_tensor(yl[:, k, :], t_ps[k][0:CAP, :], yh[:, k, :].bitcast(F32), ALU.subtract).then_inc(s["yt_lo"], 1)

            def residual(e):
                for k in range(K):
                    for i in range(TT):
                        n = k * TT + i
                        v.wait_ge(s["c_ps"], e * (K * TT) + (n + 1))
                        v.scalar_tensor_tensor(X[:, i, :], c_ps[n % 2][:, :], topp[:, i, k:k + 1], X[:, i, :], ALU.mult, ALU.add).then_inc(s["c_ok"], 1)

            def biased(e):
                for c in range(KC):
                    v.wait_ge(s["y_ps"], e * 2 + (c // 2 + 1))
                    m = v.tensor_scalar(yT[:, c, :], y_ps[c // 2][:, c % 2 * SL:(c % 2 + 1) * SL], b_cols[:, bass.ds(e * KC + c, 1)], None, ALU.add)
                    if c % 2:
                        m.then_inc(s["y_ok"], 1)

            def expert(e, first, pair=None):
                if pair is not None:
                    v.wait_ge(s["g_ps"], pair * KC + KC)
                    select(pair + 1)
                if not first:
                    turned(e - 1)
                    residual(e - 1)
                combine(e)
                biased(e)

            expert(0, True, 0)
            with v.Fori(0, (E - 4) // 2) as m:
                expert(m * 2 + 1, False)
                expert(m * 2 + 2, False, m + 1)
            for e in range(E - 3, E):
                expert(e, False)
            turned(E - 1)
            residual(E - 1)

        @block.scalar
        def _(act):
            act.activation(ln["table"][:, :], ident[:, 0:1], ACT.Sqrt)
            r = s["rows_ld"]
            act.dma_start(b1_rows[:, :], a["L0_ffn_b1"].rearrange("e (c p) -> (e c) p", p=P)).then_inc(r, 16)
            act.dma_start(b_rows[0:SB1, :], a["L0_ffn_b2"].rearrange("e (c p) -> (e c) p", p=P)).then_inc(r, 16)
            act.dma_start(b_rows[SB1:SB1 + FC, :], a["L0_ffn_sb1"].rearrange("(c p) -> c p", p=P)).then_inc(r, 16)
            act.dma_start(sb2[:, :], a["L0_ffn_sb2"].rearrange("(o d) -> o d", o=1).to_broadcast([P, D])).then_inc(r, 16)
            act.wait_ge(s["var_ready"], 1)
            act.activation(ln["root"][:, :], ln["veps"][:, :], ACT.Sqrt).then_inc(s["root_ready"], 1)
            for c in range(KC):
                act.wait_ge(s["xT_ps"], c + 1)
                act.activation(xTh[:, c, :], bank[c][:, :], ACT.Copy)
                act.activation(xnT[:, c, :], bank[c][:, :], ACT.Copy).then_inc(s["xT_ok"], 1)

            def first_high(n, q, early):
                if not early:
                    act.wait_ge(s["sh_ps"], n - 1)
                act.activation(s1h[q][:, :, :], w1[1][:, :, bass.ds(n * P, P)], ACT.Copy).then_inc(s["s1_hi"], 1)

            def second_high(n, q, early):
                if not early:
                    act.wait_ge(s["s2_ps"], n - 1)
                act.activation(s2h[q][:, :], w2[1][:, bass.ds(n, 1), :].rearrange("p o n -> p (o n)"), ACT.Copy).then_inc(s["s2_hi"], 1)

            def shared(n, q, early, left):
                act.wait_ge(s["sh_ps"], n + 1)
                if not early:
                    act.wait_ge(s["sh_lo"], n - 1)
                act.activation(hf[q][:, :], h_ps[q][:, :], ACT.Gelu, bias=b_cols[:, bass.ds(SB1 + n, 1)]).then_inc(s["sh_ok"], 1)
                act.wait_ge(s["sh_ok"], n + 1)
                if not early:
                    act.wait_ge(s["s2_ps"], n - 1)
                act.activation(hh[q][:, :], hf[q][:, :], ACT.Copy).then_inc(s["sh_hi"], 1)
                if left > 2:
                    first_high(n + 2, q, False)
                if left > 1:
                    second_high(n + 1, 1 - q, n == 0 if early else False)

            act.wait_ge(sw_ld[0], 16)
            first_high(0, 0, True)
            first_high(1, 1, True)
            act.wait_ge(s["sad_ld"], 48)
            second_high(0, 0, True)
            act.wait_ge(s["lm_ok"], TT)
            act.activation(prob[:, :, :], lg[:, :, :], ACT.Exp).then_inc(s["exp_ok"], 1)
            act.activation(topp[:, :, :], top[:, :, :], ACT.Exp).then_inc(s["exp_ok"], 1)
            act.wait_ge(s["bT_ok"], 2)
            for n in range(6):
                if n == 2:
                    act.wait_ge(sw_ld[1], 32)
                shared(n, n % 2, n < 2, FC - n)
                if n == 0:
                    act.wait_ge(s["sr_ps"], 1)
                    act.activation(rS, bank[6][0:R, :], ACT.Gelu).then_inc(s["sr_ok"], 1)
                if n == 4:
                    act.activation(xh[:, :, :], xn[:, :, :], ACT.Copy).then_inc(s["x_hi"], 1)
            act.wait_ge(sw_ld[2], (FC // PG - 2) * 32)
            with act.Fori(3, FC // 2 - 1) as m:
                for q in range(2):
                    shared(m * 2 + q, q, False, FC)
            shared(FC - 2, 0, False, 2)
            shared(FC - 1, 1, False, 1)

            def gathered(p):
                for c in range(KC):
                    act.wait_ge(s["g_ps"], p * KC + (c + 1))
                    act.activation(bufT[:, :, c, :], t_ps[c % 2][:, 0:2 * SL].rearrange("p (j n) -> p j n", j=2), ACT.Copy).then_inc(s["g_ok"], 1)

            def hidden(e, n):
                act.wait_ge(s["h_ps"], e * (FC // 2) + (n + 1))
                for q in range(2):
                    m = act.activation(hT[:, 2 * n + q, :], h_ps[n % 2][:, q * SL:(q + 1) * SL], ACT.Gelu, bias=b1_cols[:, bass.ds(e * FC + (2 * n + q), 1)])
                m.then_inc(s["h_ok"], 1)

            def turned(e):
                for k in range(K):
                    act.wait_ge(s["yt_ps"], e * K + (k + 1))
                    act.activation(yh[:, k, :], t_ps[k][0:CAP, :], ACT.Copy).then_inc(s["yt_hi"], 1)

            def expert(e, first, pair=None):
                for n in range(4):
                    hidden(e, n)
                if not first:
                    turned(e - 1)
                hidden(e, 4)
                act.wait_ge(s["r_ps"], e + 1)
                act.activation(rT[:, :], bank[6][0:R, 0:SL], ACT.Gelu).then_inc(s["r_ok"], 1)
                for n in range(5, FC // 2):
                    hidden(e, n)
                if pair is not None:
                    gathered(pair + 1)

            gathered(0)
            expert(0, True)
            with act.Fori(0, (E - 2) // 2) as m:
                expert(m * 2 + 1, False, m)
                expert(m * 2 + 2, False)
            expert(E - 1, False)
            turned(E - 1)

        @block.tensor
        def _(pe):
            pe.wait_ge(s["xn_ready"], 1)
            for c in range(KC):
                for i in range(TT):
                    m = pe.transpose(bank[c][:, i * P:(i + 1) * P], xn[:, i, c * P:(c + 1) * P], ident[:, :])
                m.then_inc(s["xT_ps"], 1)
            pe.wait_ge(s["rows_ld"], 64)
            pe.transpose(bank[7][:, 0:P], b1_rows[:, :], ident[:, :]).then_inc(s["bT_ps"], 1)
            pe.transpose(bank[7][:, P:P + SB1 + FC], b_rows[:, :], ident[0:SB1 + FC, 0:SB1 + FC]).then_inc(s["bT_ps"], 1)
            pe.wait_ge(s["xT_ok"], KC)
            pe.wait_ge(s["gate_ld"], 16)
            for c in range(KC):
                m = pe.matmul(bank[6][0:E, :], gate[:, c, :], xnT[:, c, :], start=c == 0, stop=c == KC - 1)
            m.then_inc(s["lgT_ps"], 1)

            def shared_hidden(n, q, early=False):
                pe.wait_ge(s["s1_lo"], n + 1)
                if not early:
                    pe.wait_ge(s["sh_ok"], n - 1)
                for i, (w, y, c) in enumerate((w, y, c) for w, y in ((s1l, xTh), (s1h, xTl), (s1h, xTh)) for c in range(KC)):
                    m = pe.matmul(h_ps[q][:, :], w[q][:, c, :], y[:, c, :], start=i == 0, stop=i == 3 * KC - 1)
                m.then_inc(s["sh_ps"], 1)

            def shared_out(n, q, first=False):
                pe.wait_ge(s["s2_lo"], n + 1)
                pe.wait_ge(s["sh_lo"], n + 1)
                for i in range(TT):
                    for k, (y, w) in enumerate(((hl, s2h), (hh, s2l), (hh, s2h))):
                        m = pe.matmul(bank[2 + i][:, :], y[q][:, i * P:(i + 1) * P], w[q][:, :], start=first and k == 0, stop=False)
                m.then_inc(s["s2_ps"], 1)

            def id_rows(k):
                for i in range(TT):
                    m = pe.matmul(bank[7][:, i * P:(i + 1) * P], ids[:, i, k:k + 1].to_broadcast([P, P]), ident[:, :], start=True, stop=True)
                m.then_inc(s["rows_ps"], 1)

            pe.wait_ge(s["xT_lo"], KC)
            shared_hidden(0, 0, True)
            pe.wait_ge(s["bT_ok"], 2)
            pe.wait_ge(s["lgT_ok"], 1)
            for i in range(TT):
                m = pe.transpose(bank[7][:, LG_AT + i * E:LG_AT + (i + 1) * E], rows[0:E, 0, i * P:(i + 1) * P], ident[0:E, 0:E])
            m.then_inc(s["lg_ps"], 1)
            shared_hidden(1, 1, True)
            pe.wait_ge(s["sad_ld"], 48)
            for c in range(KC):
                m = pe.matmul(bank[6][0:R, :], wd[1][:, c, :], xnT[:, c, :], start=c == 0, stop=c == KC - 1)
            m.then_inc(s["sr_ps"], 1)
            shared_out(0, 0, True)
            shared_hidden(2, 0)
            shared_out(1, 1)
            pe.wait_ge(s["consts"], 6)
            pe.wait_ge(s["oh_ok"], TT * K)
            for i in range(TT):
                for q in range(i + 1):
                    m = pe.matmul(bank[7][:, i * K * E:(i + 1) * K * E], (tri if q == i else all1)[:, :], onehot[:, q, :, :].rearrange("p k e -> p (k e)"),
                                  start=q == 0, stop=q == i)
            m.then_inc(s["cnt_ps"], 1)
            for n in range(2, 6):
                shared_hidden(n + 1, (n + 1) % 2)
                shared_out(n, n % 2)
                if n == 3:
                    pe.wait_ge(s["ids_ok"], 1)
                    id_rows(0)
                if n == 4:
                    pe.wait_ge(s["rows_ok"], 1)
                    id_rows(1)
            with pe.Fori(3, FC // 2 - 1) as m:
                for q in range(2):
                    shared_hidden(m * 2 + (q + 1), 1 - q)
                    shared_out(m * 2 + q, q)
            shared_hidden(FC - 1, 1)
            shared_out(FC - 2, 0)
            shared_out(FC - 1, 1)
            pe.wait_ge(s["sr_ok"], 1)
            for i in OUT_ORDER:
                pe.matmul(bank[2 + i][:, :], rS[:, i * P:(i + 1) * P], wu[1][:, :], start=False, stop=True).then_inc(s["so_ps"], 1)

            def gather(p):
                pe.wait_ge(s["sel_ok"], p + 1)
                for c in range(KC):
                    if c >= 2:
                        pe.wait_ge(s["g_ok"], p * KC + (c - 1))
                    for i in range(TT):
                        for part in (xl, xh):
                            m = pe.matmul(t_ps[c % 2][:, 0:2 * SL], part[:, i, c * P:(c + 1) * P], sel[:, i, :],
                                          start=i == 0 and part is xl, stop=i == TT - 1 and part is xh)
                    m.then_inc(s["g_ps"], 1)

            def turn(e):
                pe.wait_ge(s["y_ok"], e * 2 + 2)
                for k in range(K):
                    for c in range(KC):
                        m = pe.transpose(t_ps[k][0:CAP, c * P:(c + 1) * P], yT[:, c, k * CAP:(k + 1) * CAP], ident[:, :])
                    m.then_inc(s["yt_ps"], 1)

            def scatter(e, first, start, stop):
                if start == 0:
                    pe.wait_ge(s["comb_ok"], e + 1)
                    pe.wait_ge(s["yt_lo"], e * K + K)
                for n in range(start, stop):
                    k, i = n // TT, n % TT
                    if not (first and n < 2):
                        pe.wait_ge(s["c_ok"], e * (K * TT) + (n - 1))
                    for part in (yl, yh):
                        m = pe.matmul(c_ps[n % 2][:, :], comb[:, k, i * P:(i + 1) * P], part[:, k, :], start=part is yl, stop=part is yh)
                    m.then_inc(s["c_ps"], 1)

            def expert(e, i, uses, before, pair=None):
                first = before == 0
                pe.wait_ge(w1_ld[i], uses * 64)
                pe.wait_ge(s["g_ok"], uses * KC)

                def layer1(n):
                    if not (first and n < 2):
                        pe.wait_ge(s["h_ok"], e * (FC // 2) + (n - 1))
                    for q in range(2):
                        fc = 2 * n + q
                        for c in range(KC):
                            m = pe.matmul(h_ps[n % 2][:, q * SL:(q + 1) * SL], w1[i][:, c, fc * P:(fc + 1) * P], bufT[:, i, c, :], start=c == 0, stop=c == KC - 1)
                    m.then_inc(s["h_ps"], 1)

                for n in range(4):
                    layer1(n)
                if not first:
                    turn(e - 1)
                layer1(4)
                pe.wait_ge(ad_ld[i], uses * 32)
                if before == 2:
                    pe.wait_ge(s["c_ok"], (e - 1) * (K * TT))
                for c in range(KC):
                    m = pe.matmul(bank[6][0:R, 0:SL], wd[i][:, c, :], bufT[:, i, c, :], start=c == 0, stop=c == KC - 1)
                m.then_inc(s["r_ps"], 1)
                for n in range(3):
                    layer1(5 + n)
                    if not first:
                        pe.wait_ge(s["r_ok"], e + 1)
                        scatter(e - 1, before == 1, 2 * n, 2 * n + 2)
                if pair is not None:
                    gather(pair + 1)
                pe.wait_ge(w2_ld[i], uses * 64)
                pe.wait_ge(s["h_ok"], e * (FC // 2) + FC // 2)
                for c in range(KC):
                    if c % 2 == 0 and not first:
                        pe.wait_ge(s["y_ok"], e * 2 + c // 2 - 1)
                    o = y_ps[c // 2][:, c % 2 * SL:(c % 2 + 1) * SL]
                    for n in range(FC):
                        pe.matmul(o, w2[i][:, n, c * P:(c + 1) * P], hT[:, n, :], start=n == 0, stop=False)
                    m = pe.matmul(o, wu[i][:, c * P:(c + 1) * P], rT[:, :], start=False, stop=True)
                    if c % 2:
                        m.then_inc(s["y_ps"], 1)
                    if c == 0 and not first:
                        scatter(e - 1, before == 1, 6, K * TT)

            pe.wait_ge(s["x_hi"], 2)
            pe.wait_ge(s["rows_ok"], K)
            pe.wait_ge(s["so_ok"], 2)
            gather(0)
            pe.wait_ge(s["so_ok"], TT)
            pe.wait_ge(s["sh_ok"], FC)
            expert(0, 0, 1, 0)
            expert(1, 1, 1, 1, 0)
            with pe.Fori(0, (E - 4) // 2) as m:
                expert(m * 2 + 2, 0, m + 2, 2)
                expert(m * 2 + 3, 1, m + 2, 2, m + 1)
            expert(E - 2, 0, E // 2, 2)
            expert(E - 1, 1, E // 2, 2)
            turn(E - 1)
            scatter(E - 1, False, 0, K * TT)


def perceiver(nc, a, out):
    q_dram = nc.dram_tensor("q_scratch", [H, HD, B * TQ], F32, kind="Internal").ap()
    with ExitStack() as ctx:
        t = Tensors(nc, ctx, "all")
        X = t.sb("X", [P, TT, D])
        ident = t.sb("ident", [P, P])
        with ExitStack() as three:
            prob = Tensors(nc, three, "crs").sb("prob", [P, RT, S])
            queries(nc, a["x"], a["L0_xattn_Wq"], a["ctx_1024"], q_dram, X, ident, prob)
            cross(nc, a["ctx_1024"], a["mask_BxS2_bf1"], a["L0_xattn_Wk"], a["L0_xattn_Wv"], a["L0_xattn_Wo"], q_dram,
                  [a[f"L0_attn_{n}_w"] for n in ("q", "k", "v")], X, ident, prob)
            selfattn(nc, a, X, ident, prob)
        experts(nc, a, out, X, ident)


def kernel(**inputs):
    import numpy as _np
    import concourse.bacc as _bacc
    from concourse import mybir as _mybir
    from concourse.bass_utils import run_bass_kernel_spmd as _run

    nc = _bacc.Bacc("TRN2", target_bir_lowering=False, num_devices=1)
    arrays, args = {}, {}
    for name, value in inputs.items():
        a = _np.ascontiguousarray(value)
        if a.dtype == _np.bool_:
            a = a.view(_np.uint8)
        arrays[f"in_{name}"] = a
        args[name] = nc.dram_tensor(f"in_{name}", a.shape, _mybir.dt.from_np(a.dtype), kind="ExternalInput").ap()
    out = nc.dram_tensor("out_x", (B, TQ, D), _mybir.dt.float32, kind="ExternalOutput").ap()
    perceiver(nc, args, out)
    r = _run(nc, [arrays], core_ids=[0])
    return r.results[0]["out_x"]
```
